# Optimizing a Trainium2 kernel written in Bass

```python
import numpy as np
import jax
import jax.numpy as jnp

def _softmax(x, axis=-1):
    return jax.nn.softmax(x, axis=axis)

def _gelu(x):
    return jax.nn.gelu(x, approximate=True)

def _silu(x):
    return jax.nn.silu(x)

def _sigmoid(x):
    return jax.nn.sigmoid(x)

def _layernorm(x, axis=-1, eps=1e-05):
    m = jnp.mean(x, axis=axis, keepdims=True)
    v = jnp.var(x, axis=axis, keepdims=True)
    return (x - m) / jnp.sqrt(v + eps)

def _scatter_add(tgt, idx, src, axis=0):
    return tgt.at[idx].add(src)

def _segment_sum(src, seg, n):
    return jax.ops.segment_sum(src, seg, n)
kernel_name = 'mk_gnn_resnorm_d2_gnn_r8_a86afb'

def setup_inputs(seed: int=0):
    np.random.seed(seed)
    _w = jnp.asarray

    def _rec_inputs():
        import jax
        import jax.numpy as jnp
        _gk = jax.random.key(seed)
        x = -0.000202 + 1 * jax.random.normal(jax.random.fold_in(_gk, 1), (6250, 128), jnp.float32)
        _s = jax.random.randint(jax.random.fold_in(_gk, 2), (100000,), 0, 6250, jnp.int32)
        _d = jax.random.randint(jax.random.fold_in(_gk, 3), (100000,), 0, 6250, jnp.int32)
        _loop = jnp.arange(6250, dtype=jnp.int32)
        src = jnp.concatenate([_s, _d, _loop])
        dst = jnp.concatenate([_d, _s, _loop])
        _o = jnp.argsort(dst, stable=True)
        src = src[_o]
        dst = dst[_o]
        edge_attr_20 = -8.62073e-06 + 0.999901 * jax.random.normal(jax.random.fold_in(_gk, 12), (206250, 20), jnp.float32)
        edge_weight = jax.random.uniform(jax.random.fold_in(_gk, 14), (206250,), jnp.float32, 0.0, 0.999999)
        return (x, src, dst, edge_attr_20, edge_weight)
    x, src, dst, edge_attr_20, edge_weight = _rec_inputs()

    def _L0_gnn_setup():
        import jax, jax.numpy as jnp
        import numpy as np
        N_ATOMS = 6250
        N_EDGES = 200000
        N_ATOM_BASIS = 128
        N_RBF = 20
        N_FILTERS = 128
        LOG2 = 0.6931471805599453

        def ssp(x):
            return jax.nn.softplus(x) - LOG2
        key = jax.random.key(seed)
        ks = jax.random.split(key, 16)
        x = jax.random.normal(ks[0], (N_ATOMS, N_ATOM_BASIS), dtype=jnp.float32)
        f_ij = jax.random.normal(ks[1], (N_EDGES, N_RBF), dtype=jnp.float32)
        rcut_ij = jax.random.uniform(ks[2], (N_EDGES,), dtype=jnp.float32)
        idx_i = jnp.sort(jax.random.randint(ks[3], (N_EDGES,), 0, N_ATOMS))
        idx_j = jax.random.randint(ks[4], (N_EDGES,), 0, N_ATOMS)
        s = lambda fi: 1.0 / np.sqrt(fi)
        W_in2f = jax.random.normal(ks[5], (N_ATOM_BASIS, N_FILTERS), dtype=jnp.float32) * s(N_ATOM_BASIS)
        W_f1 = jax.random.normal(ks[6], (N_RBF, N_FILTERS), dtype=jnp.float32) * s(N_RBF)
        b_f1 = jnp.zeros((N_FILTERS,), dtype=jnp.float32)
        W_f2 = jax.random.normal(ks[7], (N_FILTERS, N_FILTERS), dtype=jnp.float32) * s(N_FILTERS)
        b_f2 = jnp.zeros((N_FILTERS,), dtype=jnp.float32)
        W_o1 = jax.random.normal(ks[8], (N_FILTERS, N_ATOM_BASIS), dtype=jnp.float32) * s(N_FILTERS)
        b_o1 = jnp.zeros((N_ATOM_BASIS,), dtype=jnp.float32)
        W_o2 = jax.random.normal(ks[9], (N_ATOM_BASIS, N_ATOM_BASIS), dtype=jnp.float32) * s(N_ATOM_BASIS)
        b_o2 = jnp.zeros((N_ATOM_BASIS,), dtype=jnp.float32)
        return {'x': x, 'f_ij': f_ij, 'rcut_ij': rcut_ij, 'idx_i': idx_i, 'idx_j': idx_j, 'W_in2f': W_in2f, 'W_f1': W_f1, 'b_f1': b_f1, 'W_f2': W_f2, 'b_f2': b_f2, 'W_o1': W_o1, 'b_o1': b_o1, 'W_o2': W_o2, 'b_o2': b_o2}
    _L0_gnn_all = _L0_gnn_setup()
    _L0_gnn_in = {k: v for k, v in _L0_gnn_all.items() if k in ('W_in2f', 'W_f1', 'b_f1', 'W_f2', 'b_f2', 'W_o1', 'b_o1', 'W_o2', 'b_o2')}
    del _L0_gnn_all

    def _L1_gnn_setup():
        import jax, jax.numpy as jnp
        import numpy as np
        EPS = 1e-09
        LN_EPS = 1e-05

        def _proj_normalize(v):
            return v / (jnp.linalg.norm(v, axis=-1, keepdims=True) + EPS)
        N, E, Fin, Fout = (6250, 75000, 128, 128)
        key = jax.random.key(seed)
        ks = jax.random.split(key, 8)
        x = jax.random.normal(ks[0], (N, Fin), jnp.float32)
        edge_index = jax.random.randint(ks[1], (2, E), 0, N, dtype=jnp.int64)
        edge_weight = jax.random.normal(ks[2], (E,), jnp.float32)
        W_self = jax.random.normal(ks[3], (Fin, Fout), jnp.float32) / np.sqrt(Fin)
        b_self = jnp.zeros((Fout,), jnp.float32)
        W_nb = jax.random.normal(ks[4], (Fin, Fout), jnp.float32) / np.sqrt(Fin)
        b_nb = jnp.zeros((Fout,), jnp.float32)
        gamma = jnp.ones((Fout,), jnp.float32)
        beta = jnp.zeros((Fout,), jnp.float32)
        return dict(x=x, edge_index=edge_index, edge_weight=edge_weight, W_self=W_self, b_self=b_self, W_nb=W_nb, b_nb=b_nb, gamma=gamma, beta=beta)
    _L1_gnn_all = _L1_gnn_setup()
    _L1_gnn_in = {k: v for k, v in _L1_gnn_all.items() if k in ('W_self', 'b_self', 'W_nb', 'b_nb', 'gamma', 'beta')}
    del _L1_gnn_all
    return {'x': x, 'src': src, 'dst': dst, 'edge_attr_20': edge_attr_20, 'edge_weight': edge_weight, 'L0_gnn_W_in2f': _L0_gnn_in['W_in2f'], 'L0_gnn_W_f1': _L0_gnn_in['W_f1'], 'L0_gnn_b_f1': _L0_gnn_in['b_f1'], 'L0_gnn_W_f2': _L0_gnn_in['W_f2'], 'L0_gnn_b_f2': _L0_gnn_in['b_f2'], 'L0_gnn_W_o1': _L0_gnn_in['W_o1'], 'L0_gnn_b_o1': _L0_gnn_in['b_o1'], 'L0_gnn_W_o2': _L0_gnn_in['W_o2'], 'L0_gnn_b_o2': _L0_gnn_in['b_o2'], 'L1_gnn_W_self': _L1_gnn_in['W_self'], 'L1_gnn_b_self': _L1_gnn_in['b_self'], 'L1_gnn_W_nb': _L1_gnn_in['W_nb'], 'L1_gnn_b_nb': _L1_gnn_in['b_nb'], 'L1_gnn_gamma': _L1_gnn_in['gamma'], 'L1_gnn_beta': _L1_gnn_in['beta']}

def reference(x, src, dst, edge_attr_20, edge_weight, L0_gnn_W_in2f, L0_gnn_W_f1, L0_gnn_b_f1, L0_gnn_W_f2, L0_gnn_b_f2, L0_gnn_W_o1, L0_gnn_b_o1, L0_gnn_W_o2, L0_gnn_b_o2, L1_gnn_W_self, L1_gnn_b_self, L1_gnn_W_nb, L1_gnn_b_nb, L1_gnn_gamma, L1_gnn_beta):
    import jax
    import jax.numpy as jnp

    def _L0_gnn_ref(x, f_ij, rcut_ij, idx_i, idx_j, W_in2f, W_f1, b_f1, W_f2, b_f2, W_o1, b_o1, W_o2, b_o2):
        import jax, jax.numpy as jnp
        import numpy as np
        N_ATOMS = 6250
        N_EDGES = 200000
        N_ATOM_BASIS = 128
        N_RBF = 20
        N_FILTERS = 128
        LOG2 = 0.6931471805599453

        def ssp(x):
            return jax.nn.softplus(x) - LOG2
        h = x @ W_in2f
        Wij = ssp(f_ij @ W_f1 + b_f1) @ W_f2 + b_f2
        Wij = Wij * rcut_ij[:, None]
        x_ij = h[idx_j] * Wij
        agg = jax.ops.segment_sum(x_ij, idx_i, num_segments=h.shape[0])
        out = ssp(agg @ W_o1 + b_o1) @ W_o2 + b_o2
        return out

    def _L1_gnn_ref(x, edge_index, edge_weight, W_self, b_self, W_nb, b_nb, gamma, beta):
        import jax, jax.numpy as jnp
        import numpy as np
        EPS = 1e-09
        LN_EPS = 1e-05

        def _proj_normalize(v):
            return v / (jnp.linalg.norm(v, axis=-1, keepdims=True) + EPS)
        N = x.shape[0]
        src, tgt = (edge_index[0], edge_index[1])
        seg_max = jax.ops.segment_max(edge_weight, tgt, num_segments=N)
        ew = jnp.exp(edge_weight - seg_max[tgt])
        denom = jax.ops.segment_sum(ew, tgt, num_segments=N)
        alpha = ew / denom[tgt]
        agg = jax.ops.segment_sum(alpha[:, None] * x[src], tgt, num_segments=N)
        agg = _proj_normalize(agg)
        self_feat = x @ W_self + b_self
        nb_feat = agg @ W_nb + b_nb
        comb = _proj_normalize(0.5 * (self_feat + nb_feat))
        mu = jnp.mean(comb, axis=-1, keepdims=True)
        var = jnp.var(comb, axis=-1, keepdims=True)
        out = (comb - mu) / jnp.sqrt(var + LN_EPS) * gamma + beta
        return out
    edge_index = jnp.stack([src, dst])
    x = _layernorm(x + _L0_gnn_ref(x, edge_attr_20, edge_weight, src, dst, L0_gnn_W_in2f, L0_gnn_W_f1, L0_gnn_b_f1, L0_gnn_W_f2, L0_gnn_b_f2, L0_gnn_W_o1, L0_gnn_b_o1, L0_gnn_W_o2, L0_gnn_b_o2), axis=-1)
    x = _layernorm(x + _L1_gnn_ref(x, edge_index, edge_weight, L1_gnn_W_self, L1_gnn_b_self, L1_gnn_W_nb, L1_gnn_b_nb, L1_gnn_gamma, L1_gnn_beta), axis=-1)
    return x

_drawn_inputs = setup_inputs


def setup_inputs(seed=0):
    import zlib

    import numpy as np

    out = dict(_drawn_inputs(seed))
    spreads = {'L0_gnn_b_f1': (0.0, 0.1),
     'L0_gnn_b_f2': (0.0, 0.1),
     'L0_gnn_b_o1': (0.0, 0.1),
     'L0_gnn_b_o2': (0.0, 0.1),
     'L1_gnn_b_self': (0.0, 0.1),
     'L1_gnn_b_nb': (0.0, 0.1),
     'L1_gnn_gamma': (1.0, 0.2),
     'L1_gnn_beta': (0.0, 0.1)}
    factors = {}
    for name, (base, spread) in spreads.items():
        noise = np.random.default_rng([zlib.crc32(name.encode()), seed]).standard_normal(out[name].shape)
        drawn = base * np.exp(spread * noise) if base else spread * noise
        out[name] = jnp.asarray(drawn.astype(out[name].dtype))
    for name, factor in factors.items():
        out[name] = (out[name] * factor).astype(out[name].dtype)
    return out
```

```python
import concourse.bass as bass
from concourse import mybir
from contextlib import ExitStack

F32, BF16, I32, U16 = mybir.dt.float32, mybir.dt.bfloat16, mybir.dt.int32, mybir.dt.uint16
ALU = mybir.AluOpType
ACT = mybir.ActivationFunctionType
AX = mybir.AxisListType

P = 128
NODES, EDGES, D, RBF = 6250, 206250, 128, 20
NBLK = -(-NODES // P)
NBP = 52
COLS = 1616
ET = P * COLS
NBU = NBLK + 1
PAD_NODE = NBLK * P
G2, G4 = 2 * P, 4 * P
BODY = 8
STEP = 4


def windows(rows, unit):
    most = (EDGES - NBLK) // rows + NBLK
    return -(-most // unit) * unit


NW2 = windows(G2, 2 * BODY)
NW4 = windows(G4, BODY)
Q2, Q4 = -(-NW2 // P), -(-NW4 // P)
SKIP = float(1 << 22)
FAR = 1.0e6
LOG2 = 0.6931471805599453
CAP = 20.0
EXP_LN = "natural_log_exp_and_others"
BIG = 2.0 ** 127
LN_EPS, EPS = 1e-5, 1e-9
MSG = D + 1
ROWS_OK = "the tables hold rows clamped to the arrays' length"


class Program:
    pass


class Chain:

    def __init__(self, eng, sem):
        self.eng, self.sem, self.n = eng, sem, 0

    def then(self, instruction):
        instruction.then_inc(self.sem, 1)
        self.n += 1
        self.eng.wait_ge(self.sem, self.n)


def rank_buckets(nc, eng, t, hi, base, pos, mask, run, sem):
    nc.vector.memset(pos, 0.0).then_inc(sem, 1)
    eng.wait_ge(sem, 1)
    with eng.Fori(0, NBU) as b:
        nc.vector.tensor_scalar(mask, hi, t.bucket_ids[:, bass.ds(b, 1)], None, ALU.is_equal).then_inc(sem, 1)
        eng.wait_ge(sem, 3 * b + 2)
        nc.vector.tensor_tensor_scan(run, t.ones_row[:, :], mask, base[:, bass.ds(b, 1)],
                                     ALU.mult, ALU.add).then_inc(sem, 1)
        eng.wait_ge(sem, 3 * b + 3)
        eng.sem_inc(t.ticks, 1)
        nc.vector.copy_predicated(pos, mask, run).then_inc(sem, 1)
        eng.wait_ge(sem, 3 * b + 4)
        eng.sem_inc(t.ticks, 1)


def window_tables(nc, chain, sb, t, start, rows, q, tag, scratch):
    shift = rows.bit_length() - 1
    n, ni, ng, gend = (sb(f"{x}_{tag}", [P, NBLK], dt) for x, dt in (("n", F32), ("ni", I32), ("ng", F32), ("gend", F32)))
    a, a2 = sb(f"a_{tag}", [P, NBLK], F32), sb(f"a2_{tag}", [P, NBLK], F32)
    gi, g = sb(f"gi_{tag}", [P, q], I32), t.window_ids[tag]
    cmp_, pick = (scratch[:, k * q * NBLK:(k + 1) * q * NBLK].rearrange("p (q b) -> p q b", q=q) for k in range(2))
    wb, bc, pad, s, s2, b2 = (sb(f"{x}_{tag}", [P, q], F32) for x in ("wb", "bc", "pad", "s", "s2", "b2"))
    ints, first_node = t.window_ints[tag], t.window_nodes[tag]
    v = nc.vector
    chain.then(v.tensor_tensor(n[:, :], start[:, 1:NBLK + 1], start[:, 0:NBLK], ALU.subtract))
    chain.then(v.tensor_scalar(ni[:, :], n[:, :], float(rows - 1), None, ALU.add))
    chain.then(v.tensor_scalar(ni[:, :], ni[:, :], shift, None, ALU.logical_shift_right))
    chain.then(v.tensor_copy(ng[:, :], ni[:, :]))
    chain.then(v.tensor_tensor_scan(gend[:, :], t.ones_row[:, 0:NBLK], ng[:, :], 0.0, ALU.mult, ALU.add))
    chain.then(v.tensor_tensor(a[:, :], ng[:, :], gend[:, :], ALU.subtract))
    chain.then(v.scalar_tensor_tensor(a2[:, :], a[:, :], float(rows), start[:, 0:NBLK], ALU.mult, ALU.add))
    wide = [P, q, NBLK]
    chain.then(v.tensor_tensor(cmp_[:, :, :], gend[:, None, :].to_broadcast(wide), g[:, :, None].to_broadcast(wide), ALU.is_le))
    chain.then(v.tensor_reduce(wb[:, :], cmp_[:, :, :], AX.X, ALU.add))
    chain.then(v.tensor_tensor(cmp_[:, :, :], t.bucket_ids[:, None, 0:NBLK].to_broadcast(wide),
                               wb[:, :, None].to_broadcast(wide), ALU.is_equal))
    chain.then(v.tensor_tensor(pick[:, :, :], cmp_[:, :, :], a2[:, None, :].to_broadcast(wide), ALU.mult))
    chain.then(v.tensor_reduce(s[:, :], pick[:, :, :], AX.X, ALU.add))
    chain.then(v.scalar_tensor_tensor(s2[:, :], g[:, :], float(rows), s[:, :], ALU.mult, ALU.add))
    chain.then(v.tensor_scalar(s[:, :], s2[:, :], float(ET - rows), None, ALU.min))
    chain.then(v.tensor_scalar(pad[:, :], wb[:, :], NBLK - 0.5, -FAR, ALU.is_gt, ALU.mult))
    chain.then(v.tensor_scalar(bc[:, :], wb[:, :], NBLK - 1.0, None, ALU.min))
    chain.then(v.scalar_tensor_tensor(first_node[:, :], bc[:, :], float(P), pad[:, :], ALU.mult, ALU.add))
    for k, scale in enumerate((None, MSG, 3 * D)[:ints.shape[1]]):
        if scale is None:
            chain.then(v.tensor_copy(ints[:, k, :], s[:, :]))
        else:
            chain.then(v.tensor_scalar(ints[:, k, :], bc[:, :], float(scale), None, ALU.mult))


def prologue(nc, t, a):
    with ExitStack() as ctx:
        def sb(name, shape, dt=F32):
            return ctx.enter_context(nc.sbuf_tensor(name, shape, dt))

        def ps(name, shape, dt=F32):
            return ctx.enter_context(nc.psum_tensor(name, shape, dt))

        def sem(name):
            return ctx.enter_context(nc.semaphore(name))

        src_i, dst_i, next_i = sb("src_i", [P, COLS], I32), sb("dst_i", [P, COLS], I32), sb("next_i", [P, COLS], I32)
        weight = sb("weight", [P, COLS])
        hi_i = sb("hi_i", [P, COLS], I32)
        hi_src, hi_dst, hi_next = sb("hi_src", [P, COLS], BF16), t.hi_dst, sb("hi_next", [P, COLS], BF16)
        pos = sb("pos", [P, COLS])
        fell = sb("fell", [P, COLS], BF16)
        fell_n, flag = sb("fell_n", [P, 1]), t.flag
        thresholds, sign_junk = sb("thresholds", [P, NBU + 1]), sb("sign_junk", [P, COLS], BF16)
        sgn = {k: sb(f"sgn_{k}", [P, NBU + 1]) for k in ("src", "dst")}
        below = {k: sb(f"below_{k}", [P, NBU + 1]) for k in ("src", "dst")}
        count = {k: sb(f"count_{k}", [P, NBU]) for k in ("src", "dst")}
        start = {k: sb(f"start_{k}", [P, NBU + 1]) for k in ("src", "dst")}
        base = {"src": sb("base_src", [P, NBU]), "dst": t.base_dst}
        xT = [sb(f"xT{i}", [P, 4 * P]) for i in range(2)]
        h = [sb(f"h{i}", [P, 4, D]) for i in range(2)]
        rest = sb("rest", [P, 4, D])
        colsum = sb("colsum", [1, 2, D])
        b2row, b2rest, b2rest2, b2part = sb("b2row", [1, D]), sb("b2rest", [1, D]), sb("b2rest2", [1, D]), sb("b2part", [1, 3, D], BF16)
        zero_rows = sb("zero_rows", [P, 5 * MSG])
        psT, psH = [ps(f"psT{i}", [P, 4 * P]) for i in range(2)], [ps(f"psH{i}", [P, 4, D]) for i in range(2)]
        ps_tot = {k: ps(f"ps_tot_{k}", [P, 2, 64]) for k in ("src", "dst")}
        ps_small, ps_fell = ps("ps_small", [P, 4, D]), ps("ps_fell", [P, 4 * D])

        loaded = {k: sem(f"loaded_{k}") for k in ("x", "src", "dst", "w", "weights", "b2", "tables")}
        stored, tail_stored = sem("stored"), sem("tail_stored")
        consts_made, pool_step = sem("consts_made"), sem("pool_step")
        hi_ready, signs_ready, totals_in, below_ready, bases_ready = (sem(x) for x in ("hi_ready", "signs_ready", "totals_in", "below_ready", "bases_ready"))
        dve_step, rank_step, meta_ready, tables_ready = (sem(x) for x in ("dve_step", "rank_step", "meta_ready", "tables_ready"))
        xT_made, xT_copied, h_made, h_copied, h_split, pool_h = (sem(x) for x in ("xT_made", "xT_copied", "h_made", "h_copied", "h_split", "pool_h"))
        small_made, b2_ready, b2_stored, sign_step = sem("small_made"), sem("b2_ready"), sem("b2_stored"), sem("sign_step")
        block = ctx.enter_context(nc.Block())

        @block.sync
        def _(sp):
            flat = lambda x: x[0:ET].rearrange("(p c) -> p c", p=P)
            sp.dma_start(src_i[:, :], flat(a["src"])).then_inc(loaded["src"], 16)
            sp.dma_start(dst_i[:, :], flat(a["dst"])).then_inc(loaded["dst"], 16)
            sp.dma_start(next_i[:, :], a["dst"][1:ET + 1].rearrange("(p c) -> p c", p=P)).then_inc(loaded["dst"], 16)
            sp.dma_start(weight[:, :], flat(a["edge_weight"])).then_inc(loaded["w"], 16)
            for b in range(0, NBP, NBP // 4):
                sp.dma_start(t.x_nodes[:, b:b + NBP // 4, :], a["x"][b * P:(b + NBP // 4) * P, :].rearrange("(b p) d -> p b d", p=P)).then_inc(loaded["x"], 16)
            sp.dma_start(t.filters_by_dst.rearrange("(p c) f -> p (c f)", p=P), a["edge_attr"].rearrange("(p c) f -> p (c f)", p=P)).then_inc(stored, 16)
            for n, (tag, nw) in enumerate((("src", NW4), ("dst", NW2))):
                sp.wait_ge(tables_ready, n + 1)
                q = t.window_ids[tag].shape[1]
                for k in range(n + 2):
                    sp.dma_start(t.ints_dram[tag][k, :].rearrange("(p q) -> p q", p=P), t.window_ints[tag][:, k, :]).then_inc(loaded["tables"], 16)
                sp.dma_start(t.nodes_dram[tag].rearrange("(p q) -> p q", p=P), t.window_nodes[tag][:, :]).then_inc(loaded["tables"], 16)
                sp.wait_ge(loaded["tables"], n * 96 + 16 * (n + 3))
                for k in range(n + 2):
                    sp.dma_start(t.regs[tag][0:1, k, :], t.ints_dram[tag][k:k + 1, :]).then_inc(loaded["tables"], 16)
                sp.dma_start(t.first[tag][:, :], t.nodes_dram[tag][None, :].to_broadcast([P, q * P])).then_inc(loaded["tables"], 16)
                sp.wait_ge(loaded["tables"], n * 96 + 32 * (n + 3))
            sp.wait_ge(b2_ready, 1)
            sp.dma_start(t.b2_dram.rearrange("(a k) d -> a k d", a=1), b2part[:, :, :]).then_inc(b2_stored, 16)
            sp.wait_ge(b2_stored, 16)
            for k in range(STEP):
                sp.dma_start(t.b2_rows[:, k, :], t.b2_dram).then_inc(b2_stored, 16)
            sp.wait_ge(b2_stored, 80)
            sp.wait_ge(stored, 16)

        @block.gpsimd
        def _(pool):
            g = nc.gpsimd
            g.memset(t.ones[:, :], 1.0).then_inc(pool_step, 1)
            g.memset(t.ones_row[:, :], 1.0).then_inc(pool_step, 1)
            g.memset(t.ones3[:, :], 1.0).then_inc(pool_step, 1)
            g.memset(zero_rows[:, :], 0.0).then_inc(pool_step, 1)
            pool.wait_ge(pool_step, 4)
            g.affine_select(out=t.ident[:, :], in_=t.ones[:, :], compare_op=ALU.is_equal, fill=0.0, base=0,
                            pattern=[[-1, P]], channel_multiplier=1).then_inc(pool_step, 1)
            g.affine_select(out=t.before[:, :], in_=t.ones[:, :], compare_op=ALU.is_gt, fill=0.0, base=0,
                            pattern=[[1, P]], channel_multiplier=-1).then_inc(pool_step, 1)
            g.iota(t.ids[:, :], pattern=[[1, P]], base=0, channel_multiplier=0,
                   allow_small_or_imprecise_dtypes=True).then_inc(pool_step, 1)
            g.iota(t.bucket_ids[:, :], pattern=[[1, NBU + 1]], base=0, channel_multiplier=0,
                   allow_small_or_imprecise_dtypes=True).then_inc(pool_step, 1)
            for tag, q in (("src", Q4), ("dst", Q2)):
                g.iota(t.window_ids[tag][:, :], pattern=[[1, q]], base=0, channel_multiplier=q,
                       allow_small_or_imprecise_dtypes=True).then_inc(pool_step, 1)
            pool.wait_ge(pool_step, 10)
            g.tensor_scalar(thresholds[:, :], t.bucket_ids[:, :], -1.0, 0.5, ALU.mult, ALU.add).then_inc(pool_step, 1)
            g.tensor_copy(t.ident16[:, :], t.ident[:, :]).then_inc(pool_step, 1)
            g.tensor_copy(t.ids16[:, :], t.ids[:, :]).then_inc(pool_step, 1)
            g.tensor_scalar(t.minus_big[:, :], t.ident[:, :], -BIG, 0.0, ALU.mult, ALU.add).then_inc(pool_step, 1)
            pool.wait_ge(pool_step, 14)
            g.memset(t.f_ones[:, :, :, :], 1.0).then_inc(consts_made, 1)
            g.memset(t.w1[:, :, :], 0.0).then_inc(consts_made, 1)
            pool.wait_ge(consts_made, 2)
            for k in range(STEP):
                row = k * (P // STEP)
                pool.dma_start(t.w1[row:row + RBF, k, :], a["W_f1"]).then_inc(loaded["weights"], 16)
                pool.dma_start(t.w1[row + RBF:row + RBF + 1, k, :], a["b_f1"][None, :]).then_inc(loaded["weights"], 16)
            for k, w in enumerate((a["W_in2f"], a["W_f2"], a["W_o1"], a["W_o2"], a["W_self"], a["W_nb"])):
                pool.dma_start(t.weights[:, k, :], w).then_inc(loaded["weights"], 16)
            for k, v in enumerate((a["b_f2"], a["b_o2"], a["b_self"], a["b_nb"])):
                pool.dma_start(t.rows[:, k, :], v[None, :]).then_inc(loaded["weights"], 16)
            for k, v in enumerate((a["gamma"], a["beta"])):
                pool.dma_start(t.gb[:, k, :], v[None, :].to_broadcast([P, D])).then_inc(loaded["weights"], 16)
            pool.dma_start(t.b_o1[:, :], a["b_o1"][:, None]).then_inc(loaded["weights"], 16)
            n_tail = ET - EDGES
            head = n_tail // P * P
            pool.dma_start(t.messages[EDGES:EDGES + head, :].rearrange("(p k) d -> p (k d)", p=P), zero_rows[:, 0:head // P * MSG]).then_inc(tail_stored, 16)
            pool.dma_start(t.messages[EDGES + head:ET, :], zero_rows[0:n_tail - head, 0:MSG]).then_inc(tail_stored, 16)
            for q in range(NBP // 4):
                pool.wait_ge(h_copied, q + 1)
                hq, part = h[q % 2][:, :, :], lambda k: t.h3[:, 4 * q:4 * q + 4, k, :]
                g.tensor_copy(part(0), hq).then_inc(pool_h, 1)
                pool.wait_ge(pool_h, 5 * q + 1)
                g.tensor_tensor(rest[:, :, :], hq, part(0), ALU.subtract).then_inc(pool_h, 1)
                pool.wait_ge(pool_h, 5 * q + 2)
                g.tensor_copy(part(1), rest[:, :, :]).then_inc(pool_h, 1)
                pool.wait_ge(pool_h, 5 * q + 3)
                g.tensor_tensor(part(2), rest[:, :, :], part(1), ALU.subtract).then_inc(pool_h, 1)
                pool.wait_ge(pool_h, 5 * q + 4)
                g.memset(t.pool_junk[:, :], 0.0).then_inc(pool_h, 1)
                pool.wait_ge(pool_h, 5 * q + 5)
                pool.sem_inc(h_split, 1)
            pool.wait_ge(tail_stored, 32)
            pool.wait_ge(loaded["weights"], 21 * 16)

        @block.scalar
        def _(act):
            act.preload_act_table_set(EXP_LN)
            act.wait_ge(pool_step, 14)
            act.wait_ge(hi_ready, 1)
            for n, (key, hi) in enumerate((("src", hi_src), ("dst", hi_dst))):
                act.wait_ge(hi_ready, n + 1)
                with act.Fori(0, NBU + 1) as b:
                    nc.scalar.activation(sign_junk[:, :], hi[:, :], ACT.Sign, bias=thresholds[:, bass.ds(b, 1)],
                                         accum_out=sgn[key][:, bass.ds(b, 1)]).then_inc(sign_step, 1)
                    act.wait_ge(sign_step, b + (n * (NBU + 1) + 1))
                act.sem_inc(signs_ready, 1)
            for q in range(NBP // 4):
                act.wait_ge(xT_made, q + 1)
                if q >= 2:
                    act.wait_ge(h_made, q - 1)
                nc.scalar.copy(xT[q % 2][:, :], psT[q % 2][:, :]).then_inc(xT_copied, 1)
                act.wait_ge(h_made, q + 1)
                if q >= 2:
                    act.wait_ge(h_split, q - 1)
                nc.scalar.copy(h[q % 2][:, :, :], psH[q % 2][:, :, :]).then_inc(h_copied, 1)

        @block.tensor
        def _(pe):
            pe.wait_ge(pool_step, 14)
            for n, key in enumerate(("src", "dst")):
                pe.wait_ge(below_ready, n + 1)
                nc.tensor.matmul(ps_tot[key][:, 0, 0:NBU + 1], t.ones[:, :], below[key][:, :], start=True, stop=True)
                nc.tensor.matmul(ps_tot[key][:, 1, 0:NBU], t.before[:, :], count[key][:, :], start=True, stop=True).then_inc(totals_in, 1)
            pe.wait_ge(loaded["weights"], 21 * 16)
            nc.tensor.matmul(ps_small[0:1, 0, :], t.ones[:, 0:1], t.weights[:, 1, :], start=True, stop=True)
            nc.tensor.matmul(ps_small[0:1, 1, :], t.ones[:, 0:1], t.weights[:, 3, :], start=True, stop=True).then_inc(small_made, 1)
            pe.wait_ge(loaded["x"], 64)
            for q in range(NBP // 4):
                if q >= 2:
                    pe.wait_ge(xT_copied, q - 1)
                for k in range(4):
                    last = nc.tensor.transpose(psT[q % 2][:, k * P:(k + 1) * P], t.x_nodes[:, 4 * q + k, :], t.ident[:, :])
                last.then_inc(xT_made, 1)
                pe.wait_ge(xT_copied, q + 1)
                if q >= 2:
                    pe.wait_ge(h_copied, q - 1)
                for k in range(4):
                    last = nc.tensor.matmul(psH[q % 2][:, k, :], xT[q % 2][:, k * P:(k + 1) * P], t.weights[:, 0, :], start=True, stop=True)
                last.then_inc(h_made, 1)
            pe.wait_ge(meta_ready, 1)
            nc.tensor.matmul(ps_fell[:, 0:1], t.ones[:, :], fell_n[:, :], start=True, stop=True).then_inc(small_made, 1)

        @block.vector
        def _(dve):
            chain = Chain(dve, dve_step)
            v = nc.vector
            dve.wait_ge(loaded["src"], 16)
            chain.then(v.tensor_scalar(hi_i[:, :], src_i[:, :], 7, None, ALU.logical_shift_right))
            v.tensor_copy(hi_src[:, :], hi_i[:, :]).then_inc(hi_ready, 1)
            dve.wait_ge(hi_ready, 1)
            dve.wait_ge(loaded["dst"], 32)
            chain.then(v.tensor_scalar(hi_i[:, :], dst_i[:, :], 7, None, ALU.logical_shift_right))
            v.tensor_copy(hi_dst[:, :], hi_i[:, :]).then_inc(hi_ready, 1)
            dve.wait_ge(hi_ready, 2)
            chain.then(v.tensor_scalar(hi_i[:, :], next_i[:, :], 7, None, ALU.logical_shift_right))
            chain.then(v.tensor_copy(hi_next[:, :], hi_i[:, :]))
            chain.then(v.tensor_tensor(fell[:, :], hi_dst[:, :], hi_next[:, :], ALU.is_gt))
            chain.then(v.tensor_reduce(fell_n[:, :], fell[:, :], AX.X, ALU.add))
            dve.wait_ge(loaded["w"], 16)
            chain.then(v.tensor_copy(t.meta[:, :, 0], weight[:, :]))
            chain.then(v.tensor_copy(t.meta[:, :, 1], src_i[:, :]))
            chain.then(v.tensor_copy(t.meta[:, :, 2], dst_i[:, :]))
            dve.wait_ge(pool_step, 14)

            def places(n, key):
                dve.wait_ge(signs_ready, n + 1)
                chain.then(v.tensor_scalar(below[key][:, :], sgn[key][:, :], -0.5, COLS / 2.0, ALU.mult, ALU.add))
                v.tensor_tensor(count[key][:, :], below[key][:, 1:NBU + 1], below[key][:, 0:NBU], ALU.subtract).then_inc(below_ready, 1)
                dve.wait_ge(totals_in, n + 1)
                chain.then(v.tensor_copy(start[key][:, :], ps_tot[key][:, 0, 0:NBU + 1]))
                chain.then(v.tensor_tensor(base[key][:, :], start[key][:, 0:NBU], ps_tot[key][:, 1, 0:NBU], ALU.add))

            places(0, "src")
            rank_buckets(nc, dve, t, hi_src[:, :], base["src"], pos[:, :], fell[:, :].bitcast(U16),
                         next_i[:, :].bitcast(F32), rank_step)
            v.tensor_scalar(t.meta[:, :, 3], pos[:, :], -1.0, None, ALU.add).then_inc(meta_ready, 1)
            window_tables(nc, chain, sb, t, start["src"], G4, Q4, "src", weight)
            v.memset(t.dve_junk[:, 0:1], 0.0).then_inc(tables_ready, 1)
            places(1, "dst")
            window_tables(nc, chain, sb, t, start["dst"], G2, Q2, "dst", weight)
            v.memset(t.dve_junk[:, 1:2], 0.0).then_inc(tables_ready, 1)
            dve.wait_ge(small_made, 1)
            chain.then(v.scalar_tensor_tensor(b2row[:, :], ps_small[0:1, 0, :], -LOG2, t.rows[:, 0, :], ALU.mult, ALU.add))
            chain.then(v.scalar_tensor_tensor(t.bo2[:, :], ps_small[0:1, 1, :], -LOG2, t.rows[:, 1, :], ALU.mult, ALU.add))
            chain.then(v.tensor_tensor(t.bself_nb[:, :], t.rows[:, 2, :], t.rows[:, 3, :], ALU.add))
            chain.then(v.tensor_copy(b2part[:, 0, :], b2row[:, :]))
            chain.then(v.tensor_tensor(b2rest[:, :], b2row[:, :], b2part[:, 0, :], ALU.subtract))
            chain.then(v.tensor_copy(b2part[:, 1, :], b2rest[:, :]))
            v.tensor_tensor(b2part[:, 2, :], b2rest[:, :], b2part[:, 1, :], ALU.subtract).then_inc(b2_ready, 1)
            dve.wait_ge(small_made, 2)
            v.tensor_copy(flag[:, :], ps_fell[:, 0:1]).then_inc(dve_step, 1)


def order_by_dst(nc, t, a):
    with ExitStack() as ctx:
        def sb(name, shape, dt=F32):
            return ctx.enter_context(nc.sbuf_tensor(name, shape, dt))

        def sem(name):
            return ctx.enter_context(nc.semaphore(name))

        pos, place = sb("pos_dst", [P, COLS]), sb("place", [P, COLS], I32)
        mask, run = sb("mask", [P, COLS], U16), sb("run", [P, COLS])
        GROUP = 16
        place16, meta16 = sb("place16", [P, GROUP], I32), sb("meta16", [P, GROUP, 4])
        filt16 = sb("filt16", [P, GROUP, RBF])
        stored, ranked, placed, taken, moved, filt_in = (sem(x) for x in ("meta_stored", "ranked", "placed", "taken", "moved", "filt_in"))
        block = ctx.enter_context(nc.Block())

        @block.sync
        def _(sp):
            unordered = sp.value_load(t.flag[0:1, 0:1], min_val=0, max_val=ET)
            with sp.If(unordered == 0):
                sp.dma_start(t.meta_by_dst.rearrange("(p c) k -> p (c k)", p=P), t.meta[:, :, :].rearrange("p c k -> p (c k)")).then_inc(stored, 16)
                sp.wait_ge(stored, 16)
            sp.nop()

        @block.vector
        def _(dve):
            unordered = dve.value_load(t.flag[0:1, 0:1], min_val=0, max_val=ET)
            with dve.If(unordered > 0):
                rank_buckets(nc, dve, t, t.hi_dst[:, :], t.base_dst, pos[:, :], mask[:, :], run[:, :], ranked)
                nc.vector.tensor_scalar(place[:, :], pos[:, :], -1.0, None, ALU.add).then_inc(placed, 1)
                dve.wait_ge(placed, 1)
            dve.nop()

        @block.gpsimd
        def _(pool):
            unordered = pool.value_load(t.flag[0:1, 0:1], min_val=0, max_val=ET)
            with pool.If(unordered > 0):
                g = nc.gpsimd
                pool.wait_ge(placed, 1)
                with pool.Fori(0, COLS // GROUP) as j:
                    src = a["edge_attr"].rearrange("(p c) f -> p c f", p=P)
                    pool.dma_start(filt16[:, :, :], src[:, bass.ds(j * GROUP, GROUP), :]).then_inc(filt_in, 16)
                    g.tensor_copy(place16[:, :], place[:, bass.ds(j * GROUP, GROUP)]).then_inc(taken, 1)
                    g.tensor_copy(meta16[:, :, :], t.meta[:, bass.ds(j * GROUP, GROUP), :]).then_inc(taken, 1)
                    pool.wait_ge(taken, 2 * j + 2)
                    pool.sem_inc(t.ticks, 1)
                    pool.wait_ge(filt_in, 16 * j + 16)
                    pool.sem_inc(t.ticks, 1)
                    for c in range(GROUP):
                        to = bass.IndirectOffsetOnAxis(ap=place16[:, c:c + 1], axis=0)
                        pool.indirect_dma_start(t.meta_by_dst, to, meta16[:, c, :], None).then_inc(moved, 16)
                        pool.indirect_dma_start(t.filters_by_dst, to, filt16[:, c, :], None).then_inc(moved, 16)
                    pool.wait_ge(moved, 32 * GROUP * j + 32 * GROUP)
                    pool.sem_inc(t.ticks, 1)
            pool.nop()


def steps(eng, n, *stages):
    def step(j, u):
        for lag, stage in stages:
            back = -(-(lag - u) // BODY) if lag > u else 0
            j0, u0 = j - BODY * back, u - lag + BODY * back
            if isinstance(j0, int) and not 0 <= j0 + u0 < n:
                continue
            stage(j0, u0)

    first = BODY - (-max(lag for lag, _ in stages) // BODY) * BODY
    for j in range(0, first, BODY):
        for u in range(BODY):
            step(j, u)
    with eng.Fori(first, n, BODY) as j:
        for u in range(BODY):
            step(j, u)
    for u in range(max(lag for lag, _ in stages)):
        step(n, u)


def wait(eng, sem, value):
    if not isinstance(value, int) or value > 0:
        eng.wait_ge(sem, value)


def rounds(j, back, n):
    return j * (16 * n // BODY) + 16 * n * (1 - back)


def load_rows(nc, sp, tab, row, first, n, most):
    _, values = nc.values_load_multi_w_load_instructions(tab[0:1, row, bass.ds(first, n)], engines=[sp.engine], min_val=0,
                                                         max_val=most, skip_runtime_bounds_check_because=ROWS_OK)
    return values


def messages(nc, t):
    with ExitStack() as ctx:
        def sb(name, shape, dt=F32):
            return ctx.enter_context(nc.sbuf_tensor(name, shape, dt))

        def ps(name, shape, dt=F32):
            return ctx.enter_context(nc.psum_tensor(name, shape, dt))

        def sem(name):
            return ctx.enter_context(nc.semaphore(name))

        W, K = STEP // 2, 2
        N = NW2 // W
        meta = [sb(f"meta{u}", [P, STEP, 4]) for u in range(BODY)]
        filt = t.f_ones
        place = [sb(f"place{u}", [P, STEP], I32) for u in range(BODY)]
        local, outside = [sb(f"local{u}", [P, STEP]) for u in range(2)], [sb(f"outside{u}", [P, STEP]) for u in range(2)]
        member = [sb(f"member{u}", [P, STEP, P], BF16) for u in range(2)]
        filtT = [sb(f"filtT{u}", [P, P]) for u in range(2)]
        memberT = [sb(f"memberT{u}", [P, STEP, P], BF16) for u in range(2)]
        grown, soft, act1 = ([sb(f"{x}{u}", [P, STEP * P]) for u in range(2)] for x in ("grown", "soft", "act1"))
        hdst = [sb(f"hdst{u}", [P, STEP, D]) for u in range(2)]
        msg = [sb(f"msg{u}", [P, STEP, MSG]) for u in range(BODY)]
        ps_filtT, ps_memberT = ps("ps_filtT", [P, STEP * P]), ps("ps_memberT", [P, 2 * STEP, P], BF16)
        ps_pre, ps_filter, ps_hdst = ([ps(f"{x}{u}", [P, STEP, P]) for u in range(2)] for x in ("ps_pre", "ps_filter", "ps_hdst"))

        loaded, scattered = [sem(f"loaded{u}") for u in range(BODY)], [sem(f"scattered{u}") for u in range(BODY)]
        (local_ok, outside_ok, member_ok, place_ok, filtT_made, memberT_made, filtT_ok, memberT_ok, pre_made, hdst_made,
         grown_ok, soft_ok, hdst_ok, act1_ok, filter_made, msg_ok) = (sem(x) for x in (
             "local_ok", "outside_ok", "member_ok", "place_ok", "filtT_made", "memberT_made", "filtT_ok", "memberT_ok", "pre_made",
             "hdst_made", "grown_ok", "soft_ok", "hdst_ok", "act1_ok", "filter_made", "msg_ok"))
        block = ctx.enter_context(nc.Block())

        @block.sync
        def _(sp):
            def load(j, u):
                i = j + u
                wait(sp, filtT_made, i - BODY + 1)
                wait(sp, msg_ok, i - BODY + 1)
                for w, row in enumerate(load_rows(nc, sp, t.regs["dst"], 0, W * i, W, ET - G2)):
                    sp.dma_start(filt[:, u, K * w:K * w + K, 0:RBF], t.filters_by_dst[bass.ds(row, G2), :].rearrange("(p k) f -> p k f", p=P)).then_inc(loaded[u], 16)
                    sp.dma_start(meta[u][:, K * w:K * w + K, :], t.meta_by_dst[bass.ds(row, G2), :].rearrange("(p k) f -> p k f", p=P)).then_inc(loaded[u], 16)

            steps(sp, N, (0, load))

        @block.vector
        def _(dve):
            v = nc.vector

            def classify(j, u):
                i, b = j + u, u % 2
                dve.wait_ge(loaded[u], rounds(j, 0, 2 * W))
                v.tensor_tensor(local[b][:, :].rearrange("p (w k) -> p w k", w=W), meta[u][:, :, 2].rearrange("p (w k) -> p w k", w=W),
                                t.first["dst"][:, bass.ds(W * i, W)][:, :, None].to_broadcast([P, W, K]), ALU.subtract).then_inc(local_ok, 1)
                dve.wait_ge(local_ok, i + 1)
                wait(dve, memberT_made, i - 1)
                for k in range(STEP):
                    last = v.tensor_scalar(member[b][:, k, :], t.ids16[:, :], local[b][:, k:k + 1], None, ALU.is_equal)
                last.then_inc(member_ok, 1)
                v.tensor_scalar(outside[b][:, :], local[b][:, :], P - 0.5, SKIP, ALU.is_gt, ALU.mult).then_inc(outside_ok, 1)
                dve.wait_ge(outside_ok, i + 1)
                wait(dve, scattered[u], rounds(j, 1, STEP))
                v.tensor_tensor(place[u][:, :], outside[b][:, :], meta[u][:, :, 3], ALU.add).then_inc(place_ok, 1)

            def softplus(j, u):
                i, b = j + u, u % 2
                dve.wait_ge(soft_ok, i + 1)
                wait(dve, filter_made, i - 1)
                v.scalar_tensor_tensor(act1[b][:, :], soft[b][:, :], CAP, ps_pre[b][:, :, :].rearrange("p k e -> p (k e)"), ALU.min, ALU.max).then_inc(act1_ok, 1)

            def product(j, u):
                i, b = j + u, u % 2
                dve.wait_ge(filter_made, i + 1)
                dve.wait_ge(hdst_ok, i + 1)
                wait(dve, scattered[u], rounds(j, 1, STEP))
                for k in range(STEP):
                    v.scalar_tensor_tensor(msg[u][:, k, 0:D], ps_filter[b][:, k, :], meta[u][:, k, 0:1], hdst[b][:, k, :], ALU.mult, ALU.mult)
                v.tensor_copy(msg[u][:, :, D], meta[u][:, :, 1]).then_inc(msg_ok, 1)

            steps(dve, N, (0, classify), (4, product), (3, softplus))

        @block.tensor
        def _(pe):
            def transposes(j, u):
                i, b = j + u, u % 2
                pe.wait_ge(loaded[u], rounds(j, 0, 2 * W))
                wait(pe, filtT_ok, i)
                nc.tensor.transpose(ps_filtT[:, 0:P], filt[:, u, :, :], t.ident[:, :]).then_inc(filtT_made, 1)
                pe.wait_ge(member_ok, i + 1)
                wait(pe, memberT_ok, i)
                for k in range(STEP):
                    last = nc.tensor.transpose(ps_memberT[:, k, :], member[b][:, k, :], t.ident16[:, :])
                last.then_inc(memberT_made, 1)

            def first_filter(j, u):
                i, b = j + u, u % 2
                pe.wait_ge(filtT_ok, i + 1)
                wait(pe, act1_ok, i - 1)
                for k in range(STEP):
                    last = nc.tensor.matmul(ps_pre[b][:, k, :], t.w1[:, k, :], filtT[b][:, :], start=True, stop=True)
                last.then_inc(pre_made, 1)
                pe.wait_ge(memberT_ok, i + 1)
                wait(pe, hdst_ok, i - 1)
                blocks = load_rows(nc, pe, t.regs["dst"], 2, W * i, W, (NBLK - 1) * 3 * D)
                table = t.h3[:, :, :, :].rearrange("p b k d -> p (b k d)")
                for k in range(STEP):
                    for part in range(3):
                        last = nc.tensor.matmul(ps_hdst[b][:, k, :], memberT[b][:, k, :], table[:, bass.ds(blocks[k // K] + part * D, D)],
                                                start=(part == 0), stop=(part == 2))
                last.then_inc(hdst_made, 1)

            def second_filter(j, u):
                i, b = j + u, u % 2
                wait(pe, msg_ok, i - 1)
                nc.tensor.matmul(ps_filter[b][:, :, :], t.ones3[:, :], t.b2_rows[:, :, :], start=True, stop=False, skip_group_check=True)
                pe.wait_ge(act1_ok, i + 1)
                for k in range(STEP):
                    last = nc.tensor.matmul(ps_filter[b][:, k, :], act1[b][:, k * P:(k + 1) * P], t.weights[:, 1, :],
                                            start=False, stop=True, skip_group_check=True)
                last.then_inc(filter_made, 1)

            steps(pe, N, (4, second_filter), (1, transposes), (2, first_filter))

        @block.scalar
        def _(act):
            s = nc.scalar
            act.preload_act_table_set(EXP_LN)

            def evacuate(j, u):
                i, b = j + u, u % 2
                act.wait_ge(filtT_made, i + 1)
                wait(act, pre_made, i - 1)
                s.copy(filtT[b][:, :], ps_filtT[:, 0:P]).then_inc(filtT_ok, 1)
                act.wait_ge(memberT_made, i + 1)
                wait(act, hdst_made, i - 1)
                s.copy(memberT[b][:, :, :], ps_memberT[:, 0:STEP, :]).then_inc(memberT_ok, 1)

            def softplus(j, u):
                i, b = j + u, u % 2
                act.wait_ge(pre_made, i + 1)
                s.activation(grown[b][:, :], ps_pre[b][:, :, :].rearrange("p k e -> p (k e)"), ACT.Exp).then_inc(grown_ok, 1)
                act.wait_ge(hdst_made, i + 1)
                wait(act, msg_ok, i - 1)
                s.copy(hdst[b][:, :, :], ps_hdst[b][:, :, :]).then_inc(hdst_ok, 1)
                act.wait_ge(grown_ok, i + 1)
                wait(act, act1_ok, i - 1)
                s.activation(soft[b][:, :], grown[b][:, :], ACT.Ln, bias=1.0).then_inc(soft_ok, 1)

            steps(act, N, (3, softplus), (1, evacuate))

        @block.gpsimd
        def _(pool):
            def scatter(j, u):
                i = j + u
                pool.wait_ge(msg_ok, i + 1)
                pool.sem_inc(t.ticks, 1)
                for k in range(STEP):
                    pool.indirect_dma_start(t.messages, bass.IndirectOffsetOnAxis(ap=place[u][:, k:k + 1], axis=0), msg[u][:, k, :], None,
                                            bounds_check=ET - 1, oob_is_err=False).then_inc(scattered[u], 16)

            steps(pool, N, (0, scatter))
            for u in range(BODY):
                pool.wait_ge(scattered[u], 16 * STEP * N // BODY)


def sum_messages(nc, t):
    with ExitStack() as ctx:
        def sb(name, shape, dt=F32):
            return ctx.enter_context(nc.sbuf_tensor(name, shape, dt))

        def sem(name):
            return ctx.enter_context(nc.semaphore(name))

        msg = [sb(f"msg_in{u}", [P, STEP, MSG]) for u in range(BODY)]
        local, member = [sb(f"local_src{u}", [P, STEP]) for u in range(2)], [sb(f"member_src{u}", [P, STEP, P]) for u in range(2)]
        ps_sum = [ctx.enter_context(nc.psum_tensor(f"ps_sum{u}", [P, 4 * P], F32)) for u in range(2)]
        loaded = [sem(f"msg_loaded{u}") for u in range(BODY)]
        cleared, local_ok, member_ok, sum_made, sum_added = (sem(x) for x in ("cleared", "local_src_ok", "member_src_ok", "sum_made", "sum_added"))
        block = ctx.enter_context(nc.Block())

        @block.sync
        def _(sp):
            def load(j, u):
                i = j + u
                wait(sp, sum_made, i - BODY + 1)
                row, = load_rows(nc, sp, t.regs["src"], 0, i, 1, ET - G4)
                sp.dma_start(msg[u][:, :, :].rearrange("p k d -> p (k d)"), t.messages[bass.ds(row, G4), :].rearrange("(p k) d -> p (k d)", p=P)).then_inc(loaded[u], 16)

            steps(sp, NW4, (0, load))

        @block.vector
        def _(dve):
            v = nc.vector

            def classify(j, u):
                i, b = j + u, u % 2
                dve.wait_ge(loaded[u], rounds(j, 0, 1))
                v.tensor_tensor(local[b][:, :], msg[u][:, :, D], t.first["src"][:, bass.ds(i, 1)].to_broadcast([P, STEP]), ALU.subtract).then_inc(local_ok, 1)
                dve.wait_ge(local_ok, i + 1)
                wait(dve, sum_made, i - 1)
                for k in range(STEP):
                    last = v.tensor_scalar(member[b][:, k, :], t.ids16[:, :], local[b][:, k:k + 1], None, ALU.is_equal)
                last.then_inc(member_ok, 1)

            def add(j, u):
                i, b = j + u, u % 2
                at, = load_rows(nc, dve, t.regs["src"], 1, i, 1, (NBLK - 1) * MSG)
                dve.wait_ge(sum_made, i + 1)
                wait(dve, sum_added, i)
                v.tensor_tensor(t.sums[:, bass.ds(at, D)], t.sums[:, bass.ds(at, D)], ps_sum[b][:, 0:D], ALU.add).then_inc(sum_added, 1)

            v.memset(t.sums[:, :], 0.0).then_inc(cleared, 1)
            dve.wait_ge(cleared, 1)
            steps(dve, NW4, (0, classify), (3, add))

        @block.tensor
        def _(pe):
            def total(j, u):
                i, b = j + u, u % 2
                pe.wait_ge(member_ok, i + 1)
                wait(pe, sum_added, i - 1)
                for k in range(STEP):
                    last = nc.tensor.matmul(ps_sum[b][:, 0:D], member[b][:, k, :], msg[u][:, k, 0:D], start=(k == 0), stop=(k == STEP - 1))
                last.then_inc(sum_made, 1)

            steps(pe, NW4, (1, total))


class Table:

    def __init__(self, nc, dve, ctx, tag, asked, made):
        self.nc, self.dve, self.asked, self.made, self.n = nc, dve, asked, made, 0
        self.chain = Chain(dve, ctx.enter_context(nc.semaphore(f"{tag}_step")))

    def reduce(self, out, table):
        self.chain.then(self.nc.vector.tensor_reduce(out, table, AX.X, ALU.add))

    def by_node(self, out, table, column, op):
        self.chain.then(self.nc.vector.tensor_tensor(out, table, column[:, :, None].to_broadcast([P, NBP, D]), op))

    def inverse_root(self, sums, roots, column, scale, under, over):
        v = self.nc.vector
        v.tensor_scalar(sums, sums, scale, under, ALU.mult, ALU.add).then_inc(self.asked, 1)
        self.n += 1
        self.dve.wait_ge(self.made, self.n)
        self.chain.then(v.tensor_scalar(column, roots, over, None, ALU.add))
        self.chain.then(v.reciprocal(column, column))

    def normalize(self, out, table, scratch, small, over, scale, under):
        self.chain.then(self.nc.vector.tensor_tensor(scratch, table, table, ALU.mult))
        self.reduce(small[0], scratch)
        self.inverse_root(small[0], small[1], small[2], scale, under, over)
        self.by_node(out, table, small[2], ALU.mult)

    def layer_norm(self, table, scratch, small):
        self.reduce(small[0], table)
        self.chain.then(self.nc.vector.tensor_scalar(small[2], small[0], 1.0 / D, None, ALU.mult))
        self.by_node(table, table, small[2], ALU.subtract)
        self.normalize(table, table, scratch, small, 0.0, 1.0 / D, LN_EPS)


def roots(nc, act, small, asked, made, n):
    for k in range(n):
        act.wait_ge(asked, k + 1)
        nc.scalar.activation(small[1], small[0], ACT.Sqrt).then_inc(made, 1)


def first_layer_out(nc, t):
    with ExitStack() as ctx:
        def sb(name, shape, dt=F32):
            return ctx.enter_context(nc.sbuf_tensor(name, shape, dt))

        def ps(name):
            return [ctx.enter_context(nc.psum_tensor(f"{name}{u}", [P, 4 * P], F32)) for u in range(2)]

        def sem(name):
            return ctx.enter_context(nc.semaphore(name))

        B = NBP // 4
        aggT, grown, soft, act1 = ([sb(f"{x}{u}", [P, 4 * P]) for u in range(2)] for x in ("aggT", "grown_o", "soft_o", "act1_o"))
        squares = sb("squares", [P, NBP, D])
        small = [sb(f"small{k}", [P, NBP])[:, :] for k in range(3)]
        ps_aggT, ps_pre, ps_out = ps("ps_aggT"), ps("ps_pre_o"), ps("ps_out")
        aggT_made, aggT_ok, pre_made, grown_ok, soft_ok, capped, act1_ok, out_made, out_added, asked, made, x1_ready, x1_stored = (
            sem(x) for x in ("aggT_made", "aggT_ok", "pre_o_made", "grown_o_ok", "soft_o_ok", "capped", "act1_o_ok", "out_made",
                             "out_added", "root_asked", "root_made", "x1_ready", "x1_stored"))
        block = ctx.enter_context(nc.Block())

        @block.tensor
        def _(pe):
            for q in range(B + 2):
                if q < B:
                    wait(pe, aggT_ok, q - 1)
                    for k in range(4):
                        at = (4 * q + k) * MSG
                        last = nc.tensor.transpose(ps_aggT[q % 2][:, k * P:(k + 1) * P], t.sums[:, at:at + D], t.ident[:, :])
                    last.then_inc(aggT_made, 1)
                if 1 <= q <= B:
                    r = q - 1
                    pe.wait_ge(aggT_ok, r + 1)
                    wait(pe, act1_ok, r - 1)
                    nc.tensor.matmul(ps_pre[r % 2][:, :], t.weights[:, 2, :], aggT[r % 2][:, :], start=True, stop=True).then_inc(pre_made, 1)
                if q >= 2:
                    r = q - 2
                    pe.wait_ge(act1_ok, r + 1)
                    wait(pe, out_added, r - 1)
                    for k in range(4):
                        nc.tensor.matmul(ps_out[r % 2][:, k * P:(k + 1) * P], act1[r % 2][:, k * P:(k + 1) * P], t.weights[:, 3, :], start=True, stop=False)
                        last = nc.tensor.matmul(ps_out[r % 2][:, k * P:(k + 1) * P], t.ones[0:1, :], t.bo2[:, :], start=False, stop=True)
                    last.then_inc(out_made, 1)

        @block.scalar
        def _(act):
            s = nc.scalar
            act.preload_act_table_set(EXP_LN)
            for q in range(B):
                act.wait_ge(aggT_made, q + 1)
                wait(act, pre_made, q - 1)
                s.copy(aggT[q % 2][:, :], ps_aggT[q % 2][:, :]).then_inc(aggT_ok, 1)
                act.wait_ge(pre_made, q + 1)
                s.activation(grown[q % 2][:, :], ps_pre[q % 2][:, :], ACT.Exp, bias=t.b_o1[:, 0:1]).then_inc(grown_ok, 1)
                act.wait_ge(grown_ok, q + 1)
                wait(act, act1_ok, q - 1)
                s.activation(soft[q % 2][:, :], grown[q % 2][:, :], ACT.Ln, bias=1.0).then_inc(soft_ok, 1)
            roots(nc, act, small, asked, made, 1)

        @block.vector
        def _(dve):
            v = nc.vector
            for q in range(B + 1):
                if q < B:
                    dve.wait_ge(soft_ok, q + 1)
                    v.tensor_scalar(soft[q % 2][:, :], soft[q % 2][:, :], CAP, None, ALU.min).then_inc(capped, 1)
                    dve.wait_ge(capped, q + 1)
                    wait(dve, out_made, q - 1)
                    v.scalar_tensor_tensor(act1[q % 2][:, :], ps_pre[q % 2][:, :], t.b_o1[:, 0:1], soft[q % 2][:, :], ALU.add, ALU.max).then_inc(act1_ok, 1)
                if q >= 1:
                    r = q - 1
                    dve.wait_ge(out_made, r + 1)
                    x = t.x_nodes[:, 4 * r:4 * r + 4, :].rearrange("p b d -> p (b d)")
                    v.tensor_tensor(x, x, ps_out[r % 2][:, :], ALU.add).then_inc(out_added, 1)
            dve.wait_ge(out_added, B)
            table = Table(nc, dve, ctx, "x1", asked, made)
            table.layer_norm(t.x_nodes[:, :, :], squares[:, :, :], small)
            v.memset(t.dve_junk[:, :], 0.0).then_inc(x1_ready, 1)

        @block.sync
        def _(sp):
            sp.wait_ge(x1_ready, 1)
            for b in range(0, NBP, B):
                sp.dma_start(t.x1_dram[b * P:(b + B) * P, :].rearrange("(b p) d -> p b d", p=P), t.x_nodes[:, b:b + B, :]).then_inc(x1_stored, 16)
            sp.wait_ge(x1_stored, 64)


def attention(nc, t):
    with ExitStack() as ctx:
        def sb(name, shape, dt=F32):
            return ctx.enter_context(nc.sbuf_tensor(name, shape, dt))

        def ps(name):
            return [ctx.enter_context(nc.psum_tensor(f"{name}{u}", [P, 4 * P], F32)) for u in range(2)]

        def sem(name):
            return ctx.enter_context(nc.semaphore(name))

        W, K = STEP // 2, 2
        N = NW2 // W
        NONE = BIG / 2
        meta = [sb(f"meta_l1{u}", [P, STEP, 4]) for u in range(BODY)]
        source = [sb(f"source{u}", [P, STEP], I32) for u in range(BODY)]
        xg = [sb(f"xg{u}", [P, STEP, MSG]) for u in range(BODY)]
        local = [sb(f"local_l1{u}", [P, STEP]) for u in range(2)]
        other = [sb(f"other{u}", [P, STEP, P], BF16) for u in range(2)]
        top = [sb(f"top{u}", [P, W]) for u in range(BODY)]
        below = [sb(f"minus_top{u}", [P, W]) for u in range(BODY)]
        new, diff, shrink = ([sb(f"{x}{u}", [P, W]) for u in range(BODY)] for x in ("new_max", "diff", "shrink"))
        fresh = sb("fresh", [P, P * Q2])
        grown, share = [sb(f"ew{u}", [P, STEP * P]) for u in range(2)], [sb(f"ewT{u}", [P, STEP, P]) for u in range(2)]
        ps_w, ps_ewT, ps_sum = ps("ps_w"), ps("ps_ewT"), ps("ps_l1")
        loaded, gathered = [sem(f"meta_l1_loaded{u}") for u in range(BODY)], [sem(f"gathered{u}") for u in range(BODY)]
        (source_ok, local_ok, other_ok, w_made, top_ok, below_ok, new_ok, diff_ok, ew_ok, ewT_made, ewT_ok, sum_made, sum_added,
         start_ok) = (sem(x) for x in ("source_ok", "local_l1_ok", "other_ok", "w_made", "top_ok", "minus_top_ok", "new_ok", "diff_ok", "ew_ok",
                                       "ewT_made", "ewT_ok", "l1_sum_made", "l1_sum_added", "start_ok"))
        block = ctx.enter_context(nc.Block())

        @block.sync
        def _(sp):
            def load(j, u):
                i = j + u
                wait(sp, w_made, i - BODY + 1)
                rows = load_rows(nc, sp, t.regs["dst"], 0, W * i, W, ET - G2)
                for w in range(W):
                    sp.dma_start(meta[u][:, K * w:K * w + K, :].rearrange("p k d -> p (k d)"),
                                 t.meta_by_dst[bass.ds(rows[w], G2), :].rearrange("(p k) d -> p (k d)", p=P)).then_inc(loaded[u], 16)

            steps(sp, N, (0, load))

        @block.gpsimd
        def _(pool):
            for u in range(BODY):
                nc.gpsimd.memset(xg[u][:, :, D:MSG], 1.0).then_inc(start_ok, 1)
            pool.wait_ge(start_ok, BODY)

            def gather(j, u):
                i = j + u
                pool.wait_ge(source_ok, i + 1)
                pool.sem_inc(t.ticks, 1)
                if not isinstance(j, int) or i >= BODY:
                    pool.wait_ge(sum_made, i - BODY + 1)
                    pool.sem_inc(t.ticks, 1)
                for k in range(STEP):
                    pool.indirect_dma_start(xg[u][:, k, 0:D], None, t.x1_dram, bass.IndirectOffsetOnAxis(ap=source[u][:, k:k + 1], axis=0),
                                            bounds_check=NBP * P - 1, oob_is_err=False).then_inc(gathered[u], 16)

            steps(pool, N, (0, gather))
            for u in range(BODY):
                pool.wait_ge(gathered[u], 16 * STEP * N // BODY)

        @block.vector
        def _(dve):
            v = nc.vector
            chain = Chain(dve, sem("l1_start"))
            chain.then(v.memset(t.sums[:, :], 0.0))
            chain.then(v.memset(new[BODY - 1][:, :], NONE))
            chain.then(v.memset(fresh[:, 0:1], 1.0))
            chain.then(v.tensor_tensor(fresh[:, 1:], t.first["dst"][:, 1:], t.first["dst"][:, 0:P * Q2 - 1], ALU.not_equal))
            chain.then(v.tensor_scalar(fresh[:, :], fresh[:, :], 2 * NONE, -NONE, ALU.mult, ALU.add))

            def classify(j, u):
                i, b = j + u, u % 2
                dve.wait_ge(loaded[u], rounds(j, 0, W))
                wait(dve, gathered[u], rounds(j, 1, STEP))
                v.tensor_copy(source[u][:, :], meta[u][:, :, 1]).then_inc(source_ok, 1)
                v.tensor_tensor(local[b][:, :].rearrange("p (w k) -> p w k", w=W), meta[u][:, :, 2].rearrange("p (w k) -> p w k", w=W),
                                t.first["dst"][:, bass.ds(W * i, W)][:, :, None].to_broadcast([P, W, K]), ALU.subtract).then_inc(local_ok, 1)
                dve.wait_ge(local_ok, i + 1)
                wait(dve, w_made, i - 1)
                for k in range(STEP):
                    last = v.tensor_scalar(other[b][:, k, :], t.ids16[:, :], local[b][:, k:k + 1], None, ALU.not_equal)
                last.then_inc(other_ok, 1)

            def maxima(j, u):
                i, b = j + u, u % 2
                dve.wait_ge(w_made, i + 1)
                v.tensor_reduce(top[u][:, :], ps_w[b][:, :].rearrange("p (w e) -> p w e", w=W), AX.X, ALU.max).then_inc(top_ok, 1)
                dve.wait_ge(top_ok, i + 1)
                v.tensor_scalar(below[u][:, :], top[u][:, :], -1.0, NONE, ALU.mult, ALU.min).then_inc(below_ok, 1)
                dve.wait_ge(below_ok, i + 1)
                before = new[(u - 1) % BODY][:, W - 1:W]
                v.tensor_tensor_scan(new[u][:, :], fresh[:, bass.ds(W * i, W)], below[u][:, :], before, ALU.max, ALU.min).then_inc(new_ok, 1)
                dve.wait_ge(new_ok, i + 1)
                v.tensor_scalar(diff[u][:, 0:1], new[u][:, 0:1], before, 0.0, ALU.subtract, ALU.min)
                v.tensor_scalar(diff[u][:, 1:2], new[u][:, 1:2], new[u][:, 0:1], 0.0, ALU.subtract, ALU.min).then_inc(diff_ok, 1)

            def add(j, u):
                i, b = j + u, u % 2
                at = load_rows(nc, dve, t.regs["dst"], 1, W * i, W, (NBLK - 1) * MSG)
                dve.wait_ge(sum_made, i + 1)
                for w in range(W):
                    wait(dve, sum_added, i * W + w)
                    sums = t.sums[:, bass.ds(at[w], MSG)]
                    v.scalar_tensor_tensor(sums, sums, shrink[u][:, w:w + 1], ps_sum[b][:, w * 256:w * 256 + MSG], ALU.mult, ALU.add).then_inc(sum_added, 1)

            steps(dve, N, (2, maxima), (0, classify), (6, add))

        @block.tensor
        def _(pe):
            def weights(j, u):
                i, b = j + u, u % 2
                pe.wait_ge(other_ok, i + 1)
                wait(pe, ew_ok, i - 1)
                for k in range(STEP):
                    to = ps_w[b][:, k * P:(k + 1) * P]
                    nc.tensor.matmul(to, meta[u][:, k, 0:1].to_broadcast([P, P]), t.ident[:, :], start=True, stop=False, skip_group_check=True)
                    last = nc.tensor.matmul(to, other[b][:, k, :], t.minus_big[:, :], start=False, stop=True, skip_group_check=True)
                last.then_inc(w_made, 1)

            def transposes(j, u):
                i, b = j + u, u % 2
                pe.wait_ge(ew_ok, i + 1)
                wait(pe, ewT_ok, i - 1)
                for k in range(STEP):
                    last = nc.tensor.transpose(ps_ewT[b][:, k * P:(k + 1) * P], grown[b][:, k * P:(k + 1) * P], t.ident[:, :])
                last.then_inc(ewT_made, 1)

            def total(j, u):
                i, b = j + u, u % 2
                pe.wait_ge(ewT_ok, i + 1)
                pe.wait_ge(gathered[u], rounds(j, 0, STEP))
                wait(pe, sum_added, W * (i - 1))
                for k in range(STEP):
                    at = k // K * 256
                    last = nc.tensor.matmul(ps_sum[b][:, at:at + MSG], share[b][:, k, :], xg[u][:, k, :], start=(k % K == 0), stop=(k % K == K - 1))
                last.then_inc(sum_made, 1)

            pe.wait_ge(start_ok, BODY)
            steps(pe, N, (4, transposes), (1, weights), (5, total))

        @block.scalar
        def _(act):
            s = nc.scalar
            act.preload_act_table_set(EXP_LN)

            def exponentials(j, u):
                i, b = j + u, u % 2
                act.wait_ge(diff_ok, i + 1)
                wait(act, ewT_made, i - 1)
                for w in range(W):
                    cols = slice(w * K * P, (w + 1) * K * P)
                    s.activation(grown[b][:, cols], ps_w[b][:, cols], ACT.Exp, bias=new[u][:, w:w + 1])
                s.activation(shrink[u][:, :], diff[u][:, :], ACT.Exp).then_inc(ew_ok, 1)

            def evacuate(j, u):
                i, b = j + u, u % 2
                act.wait_ge(ewT_made, i + 1)
                wait(act, sum_made, i - 1)
                s.copy(share[b][:, :, :].rearrange("p k n -> p (k n)"), ps_ewT[b][:, :]).then_inc(ewT_ok, 1)

            steps(act, N, (3, exponentials), (4, evacuate))


def second_layer_out(nc, t, out):
    with ExitStack() as ctx:
        def sb(name, shape, dt=F32):
            return ctx.enter_context(nc.sbuf_tensor(name, shape, dt))

        def ps(name):
            return [ctx.enter_context(nc.psum_tensor(f"{name}{u}", [P, 4 * P], F32)) for u in range(2)]

        def sem(name):
            return ctx.enter_context(nc.semaphore(name))

        B = NBP // 4
        squares = sb("squares2", [P, NBP, D])
        comb = sb("comb", [P, NBP, D])
        small = [sb(f"small2{k}", [P, NBP])[:, :] for k in range(3)]
        xT, nT = ([sb(f"{x}{u}", [P, 4 * P]) for u in range(2)] for x in ("x1T", "nT"))
        ps_xT, ps_nT, ps_comb = ps("ps_x1T"), ps("ps_nT"), ps("ps_comb")
        unit_ok, T_made, T_ok, comb_made, comb_ok, asked, made, out_ready, out_stored = (
            sem(x) for x in ("unit_ok", "T_made", "T_ok", "comb_made", "comb_ok", "root2_asked", "root2_made", "out_ready", "out_stored"))
        block = ctx.enter_context(nc.Block())

        @block.vector
        def _(dve):
            v = nc.vector
            table = Table(nc, dve, ctx, "out", asked, made)
            chain = table.chain
            sums = t.sums[:, :].rearrange("p (b d) -> p b d", d=MSG)
            agg = sums[:, :, 0:D]
            chain.then(v.tensor_scalar(small[2], sums[:, :, D], 0.5, None, ALU.max))
            chain.then(v.reciprocal(small[2], small[2]))
            table.by_node(agg, agg, small[2], ALU.mult)
            table.normalize(agg, agg, squares[:, :, :], small, EPS, 1.0, 0.0)
            v.memset(t.dve_junk[:, :], 0.0).then_inc(unit_ok, 1)
            dve.wait_ge(comb_ok, B)
            x = comb[:, :, :]
            table.normalize(x, x, squares[:, :, :], small, EPS, 1.0, 0.0)
            table.layer_norm(x, squares[:, :, :], small)
            wide = [P, NBP, D]
            chain.then(v.tensor_tensor(x, x, t.gb[:, 0, :][:, None, :].to_broadcast(wide), ALU.mult))
            chain.then(v.tensor_tensor(x, x, t.gb[:, 1, :][:, None, :].to_broadcast(wide), ALU.add))
            chain.then(v.tensor_tensor(x, x, t.x_nodes[:, :, :], ALU.add))
            table.layer_norm(x, squares[:, :, :], small)
            v.memset(t.dve_junk[:, :], 0.0).then_inc(out_ready, 1)

        @block.tensor
        def _(pe):
            pe.wait_ge(unit_ok, 1)
            for q in range(B + 1):
                if q < B:
                    wait(pe, T_ok, 2 * (q - 1))
                    for k in range(4):
                        at, cols = (4 * q + k) * MSG, slice(k * P, (k + 1) * P)
                        nc.tensor.transpose(ps_xT[q % 2][:, cols], t.x_nodes[:, 4 * q + k, :], t.ident[:, :])
                        last = nc.tensor.transpose(ps_nT[q % 2][:, cols], t.sums[:, at:at + D], t.ident[:, :])
                    last.then_inc(T_made, 1)
                if q >= 1:
                    r = q - 1
                    pe.wait_ge(T_ok, 2 * (r + 1))
                    wait(pe, comb_ok, r - 1)
                    for k in range(4):
                        cols = slice(k * P, (k + 1) * P)
                        nc.tensor.matmul(ps_comb[r % 2][:, cols], xT[r % 2][:, cols], t.weights[:, 4, :], start=True, stop=False)
                        nc.tensor.matmul(ps_comb[r % 2][:, cols], nT[r % 2][:, cols], t.weights[:, 5, :], start=False, stop=False)
                        last = nc.tensor.matmul(ps_comb[r % 2][:, cols], t.ones[0:1, :], t.bself_nb[:, :], start=False, stop=True)
                    last.then_inc(comb_made, 1)

        @block.scalar
        def _(act):
            s = nc.scalar
            roots(nc, act, small, asked, made, 1)
            for q in range(B + 1):
                if q < B:
                    act.wait_ge(T_made, q + 1)
                    wait(act, comb_made, q - 1)
                    s.copy(xT[q % 2][:, :], ps_xT[q % 2][:, :]).then_inc(T_ok, 1)
                    s.copy(nT[q % 2][:, :], ps_nT[q % 2][:, :]).then_inc(T_ok, 1)
                if q >= 1:
                    act.wait_ge(comb_made, q)
                    s.activation(comb[:, 4 * (q - 1):4 * q, :].rearrange("p b d -> p (b d)"), ps_comb[(q - 1) % 2][:, :], ACT.Copy, scale=0.5).then_inc(comb_ok, 1)
            for k in range(1, 4):
                act.wait_ge(asked, k + 1)
                s.activation(small[1], small[0], ACT.Sqrt).then_inc(made, 1)

        @block.sync
        def _(sp):
            sp.wait_ge(out_ready, 1)
            for b in range(0, NBP, B):
                sp.dma_start(out[b * P:(b + B) * P, :].rearrange("(b p) d -> p b d", p=P), comb[:, b:b + B, :]).then_inc(out_stored, 16)
            sp.wait_ge(out_stored, 64)


def build(nc, a, out):
    with ExitStack() as ctx:
        def sb(name, shape, dt=F32):
            return ctx.enter_context(nc.sbuf_tensor(name, shape, dt))

        def dram(name, shape, dt=F32):
            return nc.dram_tensor(name, shape, dt, kind="Internal").ap()

        t = Program()
        t.ticks = ctx.enter_context(nc.semaphore("ticks"))
        t.ones, t.ident, t.before, t.ids = (sb(x, [P, P]) for x in ("ones", "ident", "before", "ids"))
        t.ident16, t.ids16, t.minus_big = (sb(x, [P, P], BF16) for x in ("ident16", "ids16", "minus_big"))
        t.ones_row, t.ones3 = sb("ones_row", [P, COLS], BF16), sb("ones3", [3, P], BF16)
        t.bucket_ids = sb("bucket_ids", [P, NBU + 1])
        t.pool_junk, t.dve_junk = sb("pool_junk", [P, 1]), sb("dve_junk", [P, 2])
        t.w1, t.weights, t.rows = sb("w1", [P, STEP, D]), sb("weights", [P, 6, D]), sb("rows", [1, 4, D])
        t.gb, t.b_o1, t.bo2, t.bself_nb = sb("gb", [P, 2, D]), sb("b_o1", [P, 1]), sb("bo2", [1, D]), sb("bself_nb", [1, D])
        t.b2_rows = sb("b2_rows", [3, STEP, D], BF16)
        t.x_nodes = sb("x_nodes", [P, NBP, D])
        t.window_ids = {"src": sb("window_ids_src", [P, Q4]), "dst": sb("window_ids_dst", [P, Q2])}
        t.window_ints = {"src": sb("window_ints_src", [P, 2, Q4], I32), "dst": sb("window_ints_dst", [P, 3, Q2], I32)}
        t.window_nodes = {"src": sb("window_nodes_src", [P, Q4]), "dst": sb("window_nodes_dst", [P, Q2])}
        t.regs = {"src": sb("regs_src", [1, 2, P * Q4], I32), "dst": sb("regs_dst", [1, 3, P * Q2], I32)}
        t.first = {"src": sb("first_src", [P, P * Q4]), "dst": sb("first_dst", [P, P * Q2])}
        t.ints_dram = {"src": dram("ints_src", [2, P * Q4], I32), "dst": dram("ints_dst", [3, P * Q2], I32)}
        t.nodes_dram = {"src": dram("nodes_src", [P * Q4]), "dst": dram("nodes_dst", [P * Q2])}
        t.b2_dram = dram("b2_parts", [3, D], BF16)
        t.flag = sb("flag", [P, 1], I32)
        t.filters_by_dst, t.meta_by_dst = dram("filters_by_dst", [ET, RBF]), dram("meta_by_dst", [ET, 4])
        t.messages = dram("messages", [ET, MSG])
        t.x1_dram = dram("x1_nodes", [NBP * P, D])
        t.f_ones = sb("f_ones", [P, BODY, STEP, P // STEP])

        with ExitStack() as c1:
            t.h3 = c1.enter_context(nc.sbuf_tensor("h3", [P, NBP, 3, D], BF16))
            with ExitStack() as c2:
                t.meta = c2.enter_context(nc.sbuf_tensor("meta", [P, COLS, 4], F32))
                t.hi_dst = c2.enter_context(nc.sbuf_tensor("hi_dst", [P, COLS], BF16))
                t.base_dst = c2.enter_context(nc.sbuf_tensor("base_dst", [P, NBU], F32))
                prologue(nc, t, a)
                order_by_dst(nc, t, a)
            messages(nc, t)
        t.sums = sb("sums", [P, NBP * MSG])
        sum_messages(nc, t)
        first_layer_out(nc, t)
        attention(nc, t)
        second_layer_out(nc, t, out)


def kernel(x, src, dst, edge_attr_20, edge_weight, L0_gnn_W_in2f, L0_gnn_W_f1, L0_gnn_b_f1, L0_gnn_W_f2, L0_gnn_b_f2,
           L0_gnn_W_o1, L0_gnn_b_o1, L0_gnn_W_o2, L0_gnn_b_o2, L1_gnn_W_self, L1_gnn_b_self, L1_gnn_W_nb, L1_gnn_b_nb,
           L1_gnn_gamma, L1_gnn_beta):
    import numpy as np
    import concourse.bacc as bacc
    from concourse.bass_utils import run_bass_kernel_spmd

    def padded(v, rows, fill=0):
        v = np.asarray(v)
        wide = np.full((rows,) + v.shape[1:], fill, v.dtype)
        wide[:v.shape[0]] = v
        return wide

    arrays = {
        "x": padded(x, NBP * P), "src": padded(src, ET, PAD_NODE), "dst": padded(dst, ET + 1, PAD_NODE),
        "edge_attr": padded(edge_attr_20, ET), "edge_weight": padded(edge_weight, ET),
        "W_in2f": L0_gnn_W_in2f, "W_f1": L0_gnn_W_f1, "b_f1": L0_gnn_b_f1, "W_f2": L0_gnn_W_f2, "b_f2": L0_gnn_b_f2,
        "W_o1": L0_gnn_W_o1, "b_o1": L0_gnn_b_o1, "W_o2": L0_gnn_W_o2, "b_o2": L0_gnn_b_o2,
        "W_self": L1_gnn_W_self, "b_self": L1_gnn_b_self, "W_nb": L1_gnn_W_nb, "b_nb": L1_gnn_b_nb,
        "gamma": L1_gnn_gamma, "beta": L1_gnn_beta,
    }
    arrays = {f"in_{k}": np.ascontiguousarray(v) for k, v in arrays.items()}
    nc = bacc.Bacc("TRN2", target_bir_lowering=False, num_devices=1)
    a = {k[3:]: nc.dram_tensor(k, v.shape, mybir.dt.from_np(v.dtype), kind="ExternalInput").ap() for k, v in arrays.items()}
    out = nc.dram_tensor("out_x", (NBP * P, D), F32, kind="ExternalOutput").ap()
    build(nc, a, out)
    results = run_bass_kernel_spmd(nc, [arrays], core_ids=[0])
    return results.results[0]["out_x"][:NODES]
```

```python
import concourse.bass as bass
from concourse import mybir
from contextlib import ExitStack

F32, BF16, I32, U16 = mybir.dt.float32, mybir.dt.bfloat16, mybir.dt.int32, mybir.dt.uint16
ALU = mybir.AluOpType
ACT = mybir.ActivationFunctionType
AX = mybir.AxisListType

P = 128
NODES, EDGES, D, RBF = 6250, 206250, 128, 20
NBLK = -(-NODES // P)
NBP = 52
COLS = 1616
ET = P * COLS
NBU = NBLK + 1
PAD_NODE = NBLK * P
G2, G4 = 2 * P, 4 * P
BODY = 8
STEP = 4


def windows(rows, unit):
    most = (EDGES - NBLK) // rows + NBLK
    return -(-most // unit) * unit


NW2 = windows(G2, 2 * BODY)
NW4 = windows(G4, BODY)
Q2, Q4 = -(-NW2 // P), -(-NW4 // P)
SKIP = float(1 << 22)
FAR = 1.0e6
LOG2 = 0.6931471805599453
CAP = 20.0
EXP_LN = "natural_log_exp_and_others"
BIG = 2.0 ** 127
LN_EPS, EPS = 1e-5, 1e-9
MSG = D + 1
ROWS_OK = "the tables hold rows clamped to the arrays' length"


class Program:
    pass


class Chain:

    def __init__(self, eng, sem):
        self.eng, self.sem, self.n = eng, sem, 0

    def then(self, instruction):
        instruction.then_inc(self.sem, 1)
        self.n += 1
        self.eng.wait_ge(self.sem, self.n)


def rank_buckets(nc, eng, t, hi, base, pos, masks, runs, sem):
    v = nc.vector
    v.memset(pos, 0.0).then_inc(sem, 1)
    eng.wait_ge(sem, 1)
    with eng.Fori(0, NBU, 2) as b:
        for k in range(2):
            if k == 1:
                eng.wait_ge(sem, 3 * b + 1)
            v.tensor_scalar(masks[k], hi, t.bucket_ids[:, bass.ds(b + k, 1)], None, ALU.is_equal).then_inc(sem, 1)
        for k in range(2):
            eng.wait_ge(sem, 3 * b + (2 + k))
            v.tensor_tensor_scan(runs[k], t.ones_row[:, :], masks[k], base[:, bass.ds(b + k, 1)], ALU.mult, ALU.add).then_inc(sem, 1)
        for k in range(2):
            eng.wait_ge(sem, 3 * b + (4 + k))
            eng.sem_inc(t.ticks, 1)
            if k == 1:
                eng.wait_ge(sem, 3 * b + 6)
                eng.sem_inc(t.ticks, 1)
            v.copy_predicated(pos, masks[k], runs[k]).then_inc(sem, 1)
    eng.wait_ge(sem, 3 * NBU + 1)


def window_tables(nc, chain, sb, t, start, rows, q, tag, scratch):
    shift = rows.bit_length() - 1
    n, ni, ng, gend = (sb(f"{x}_{tag}", [P, NBLK], dt) for x, dt in (("n", F32), ("ni", I32), ("ng", F32), ("gend", F32)))
    a, a2 = sb(f"a_{tag}", [P, NBLK], F32), sb(f"a2_{tag}", [P, NBLK], F32)
    gi, g = sb(f"gi_{tag}", [P, q], I32), t.window_ids[tag]
    cmp_, pick = (scratch[:, k * q * NBLK:(k + 1) * q * NBLK].rearrange("p (q b) -> p q b", q=q) for k in range(2))
    wb, bc, pad, s, s2, b2 = (sb(f"{x}_{tag}", [P, q], F32) for x in ("wb", "bc", "pad", "s", "s2", "b2"))
    ints, first_node = t.window_ints[tag], t.window_nodes[tag]
    v = nc.vector
    chain.then(v.tensor_tensor(n[:, :], start[:, 1:NBLK + 1], start[:, 0:NBLK], ALU.subtract))
    chain.then(v.tensor_scalar(ni[:, :], n[:, :], float(rows - 1), None, ALU.add))
    chain.then(v.tensor_scalar(ni[:, :], ni[:, :], shift, None, ALU.logical_shift_right))
    chain.then(v.tensor_copy(ng[:, :], ni[:, :]))
    chain.then(v.tensor_tensor_scan(gend[:, :], t.ones_row[:, 0:NBLK], ng[:, :], 0.0, ALU.mult, ALU.add))
    chain.then(v.tensor_tensor(a[:, :], ng[:, :], gend[:, :], ALU.subtract))
    chain.then(v.scalar_tensor_tensor(a2[:, :], a[:, :], float(rows), start[:, 0:NBLK], ALU.mult, ALU.add))
    wide = [P, q, NBLK]
    chain.then(v.tensor_tensor(cmp_[:, :, :], gend[:, None, :].to_broadcast(wide), g[:, :, None].to_broadcast(wide), ALU.is_le))
    chain.then(v.tensor_reduce(wb[:, :], cmp_[:, :, :], AX.X, ALU.add))
    chain.then(v.tensor_tensor(cmp_[:, :, :], t.bucket_ids[:, None, 0:NBLK].to_broadcast(wide),
                               wb[:, :, None].to_broadcast(wide), ALU.is_equal))
    chain.then(v.tensor_tensor(pick[:, :, :], cmp_[:, :, :], a2[:, None, :].to_broadcast(wide), ALU.mult))
    chain.then(v.tensor_reduce(s[:, :], pick[:, :, :], AX.X, ALU.add))
    chain.then(v.scalar_tensor_tensor(s2[:, :], g[:, :], float(rows), s[:, :], ALU.mult, ALU.add))
    chain.then(v.tensor_scalar(s[:, :], s2[:, :], float(ET - rows), None, ALU.min))
    chain.then(v.tensor_scalar(pad[:, :], wb[:, :], NBLK - 0.5, -FAR, ALU.is_gt, ALU.mult))
    chain.then(v.tensor_scalar(bc[:, :], wb[:, :], NBLK - 1.0, None, ALU.min))
    chain.then(v.scalar_tensor_tensor(first_node[:, :], bc[:, :], float(P), pad[:, :], ALU.mult, ALU.add))
    for k, scale in enumerate((None, MSG, 3 * D)[:ints.shape[1]]):
        if scale is None:
            chain.then(v.tensor_copy(ints[:, k, :], s[:, :]))
        else:
            chain.then(v.tensor_scalar(ints[:, k, :], bc[:, :], float(scale), None, ALU.mult))


def prologue(nc, t, a):
    with ExitStack() as ctx:
        def sb(name, shape, dt=F32):
            return ctx.enter_context(nc.sbuf_tensor(name, shape, dt))

        def ps(name, shape, dt=F32):
            return ctx.enter_context(nc.psum_tensor(name, shape, dt))

        def sem(name):
            return ctx.enter_context(nc.semaphore(name))

        src_i, dst_i, next_i = sb("src_i", [P, COLS], I32), sb("dst_i", [P, COLS], I32), sb("next_i", [P, COLS], I32)
        weight = sb("weight", [P, COLS])
        hi_i = sb("hi_i", [P, COLS], I32)
        hi_src, hi_dst, hi_next = sb("hi_src", [P, COLS], BF16), t.hi_dst, sb("hi_next", [P, COLS], BF16)
        pos = sb("pos", [P, COLS])
        fell = sb("fell", [P, COLS], BF16)
        fell_n, flag = sb("fell_n", [P, 1]), t.flag
        thresholds, sign_junk = sb("thresholds", [P, NBU + 1]), sb("sign_junk", [P, COLS], BF16)
        signs = sb("signs", [P, NBU + 1])
        below = {k: sb(f"below_{k}", [P, NBU + 1]) for k in ("src", "dst")}
        count = {k: sb(f"count_{k}", [P, NBU]) for k in ("src", "dst")}
        start = {k: sb(f"start_{k}", [P, NBU + 1]) for k in ("src", "dst")}
        base = {"src": sb("base_src", [P, NBU + 1]), "dst": t.base_dst}
        xT = [sb(f"xT{i}", [P, 4 * P]) for i in range(2)]
        h = [sb(f"h{i}", [P, 4, D]) for i in range(2)]
        rest = sb("rest", [P, 4, D])
        colsum = sb("colsum", [1, 2, D])
        b2row, b2rest, b2rest2, b2part = sb("b2row", [1, D]), sb("b2rest", [1, D]), sb("b2rest2", [1, D]), sb("b2part", [1, 3, D], BF16)
        zero_rows = sb("zero_rows", [P, 5 * MSG])
        psT, psH = [ps(f"psT{i}", [P, 4 * P]) for i in range(2)], [ps(f"psH{i}", [P, 4, D]) for i in range(2)]
        ps_tot = {k: ps(f"ps_tot_{k}", [P, 2, 64]) for k in ("src", "dst")}
        ps_small, ps_fell = ps("ps_small", [P, 4, D]), ps("ps_fell", [P, 4 * D])

        loaded = {k: sem(f"loaded_{k}") for k in ("x", "src", "dst", "w", "weights", "b2", "tables")}
        stored, tail_stored = sem("stored"), sem("tail_stored")
        consts_made, pool_step = sem("consts_made"), sem("pool_step")
        hi_ready, below_step, totals_in, below_ready, bases_ready = (sem(x) for x in ("hi_ready", "below_step", "totals_in", "below_ready", "bases_ready"))
        dve_step, rank_step, meta_ready, tables_ready = (sem(x) for x in ("dve_step", "rank_step", "meta_ready", "tables_ready"))
        xT_made, xT_copied, h_made, h_copied, h_split, pool_h = (sem(x) for x in ("xT_made", "xT_copied", "h_made", "h_copied", "h_split", "pool_h"))
        small_made, b2_ready, b2_stored, sign_step = sem("small_made"), sem("b2_ready"), sem("b2_stored"), sem("sign_step")
        block = ctx.enter_context(nc.Block())

        @block.sync
        def _(sp):
            flat = lambda x: x[0:ET].rearrange("(p c) -> p c", p=P)
            sp.dma_start(src_i[:, :], flat(a["src"])).then_inc(loaded["src"], 16)
            sp.dma_start(dst_i[:, :], flat(a["dst"])).then_inc(loaded["dst"], 16)
            sp.dma_start(next_i[:, :], a["dst"][1:ET + 1].rearrange("(p c) -> p c", p=P)).then_inc(loaded["dst"], 16)
            sp.dma_start(weight[:, :], flat(a["edge_weight"])).then_inc(loaded["w"], 16)
            for b in range(0, NBP, NBP // 4):
                sp.dma_start(t.x_nodes[:, b:b + NBP // 4, :], a["x"][b * P:(b + NBP // 4) * P, :].rearrange("(b p) d -> p b d", p=P)).then_inc(loaded["x"], 16)
            sp.dma_start(t.filters_by_dst.rearrange("(p c) f -> p (c f)", p=P), a["edge_attr"].rearrange("(p c) f -> p (c f)", p=P)).then_inc(stored, 16)
            sp.wait_ge(meta_ready, 1)
            sp.dma_start(t.meta_by_dst.rearrange("(p c) k -> p (c k)", p=P), t.meta[:, :, :].rearrange("p c k -> p (c k)")).then_inc(stored, 16)
            for n, (tag, nw) in enumerate((("src", NW4), ("dst", NW2))):
                sp.wait_ge(tables_ready, n + 1)
                q = t.window_ids[tag].shape[1]
                for k in range(n + 2):
                    sp.dma_start(t.ints_dram[tag][k, :].rearrange("(p q) -> p q", p=P), t.window_ints[tag][:, k, :]).then_inc(loaded["tables"], 16)
                sp.dma_start(t.nodes_dram[tag].rearrange("(p q) -> p q", p=P), t.window_nodes[tag][:, :]).then_inc(loaded["tables"], 16)
                sp.wait_ge(loaded["tables"], n * 96 + 16 * (n + 3))
                for k in range(n + 2):
                    sp.dma_start(t.regs[tag][0:1, k, :], t.ints_dram[tag][k:k + 1, :]).then_inc(loaded["tables"], 16)
                sp.dma_start(t.first[tag][:, :], t.nodes_dram[tag][None, :].to_broadcast([P, q * P])).then_inc(loaded["tables"], 16)
                sp.wait_ge(loaded["tables"], n * 96 + 32 * (n + 3))
            sp.wait_ge(b2_ready, 1)
            sp.dma_start(t.b2_dram.rearrange("(a k) d -> a k d", a=1), b2part[:, :, :]).then_inc(b2_stored, 16)
            sp.wait_ge(b2_stored, 16)
            for k in range(STEP):
                sp.dma_start(t.b2_rows[:, k, :], t.b2_dram).then_inc(b2_stored, 16)
            sp.wait_ge(b2_stored, 80)
            sp.wait_ge(stored, 32)

        @block.gpsimd
        def _(pool):
            g = nc.gpsimd
            g.memset(t.ones[:, :], 1.0).then_inc(pool_step, 1)
            g.memset(t.ones_row[:, :], 1.0).then_inc(pool_step, 1)
            g.memset(t.ones3[:, :], 1.0).then_inc(pool_step, 1)
            g.memset(zero_rows[:, :], 0.0).then_inc(pool_step, 1)
            pool.wait_ge(pool_step, 4)
            g.affine_select(out=t.ident[:, :], in_=t.ones[:, :], compare_op=ALU.is_equal, fill=0.0, base=0,
                            pattern=[[-1, P]], channel_multiplier=1).then_inc(pool_step, 1)
            g.affine_select(out=t.before[:, :], in_=t.ones[:, :], compare_op=ALU.is_gt, fill=0.0, base=0,
                            pattern=[[1, P]], channel_multiplier=-1).then_inc(pool_step, 1)
            g.iota(t.ids[:, :], pattern=[[1, P]], base=0, channel_multiplier=0,
                   allow_small_or_imprecise_dtypes=True).then_inc(pool_step, 1)
            g.iota(t.bucket_ids[:, :], pattern=[[1, NBU + 1]], base=0, channel_multiplier=0,
                   allow_small_or_imprecise_dtypes=True).then_inc(pool_step, 1)
            for tag, q in (("src", Q4), ("dst", Q2)):
                g.iota(t.window_ids[tag][:, :], pattern=[[1, q]], base=0, channel_multiplier=q,
                       allow_small_or_imprecise_dtypes=True).then_inc(pool_step, 1)
            pool.wait_ge(pool_step, 10)
            g.tensor_scalar(thresholds[:, :], t.bucket_ids[:, :], -1.0, 0.5, ALU.mult, ALU.add).then_inc(pool_step, 1)
            g.tensor_copy(t.ident16[:, :], t.ident[:, :]).then_inc(pool_step, 1)
            g.tensor_copy(t.ids16[:, :], t.ids[:, :]).then_inc(pool_step, 1)
            g.tensor_scalar(t.minus_big[:, :], t.ident[:, :], -BIG, 0.0, ALU.mult, ALU.add).then_inc(pool_step, 1)
            pool.wait_ge(pool_step, 14)
            g.memset(t.f_ones[:, :, :, :], 1.0).then_inc(consts_made, 1)
            g.memset(t.w1[:, :, :], 0.0).then_inc(consts_made, 1)
            pool.wait_ge(consts_made, 2)
            for k in range(STEP):
                row = k * (P // STEP)
                pool.dma_start(t.w1[row:row + RBF, k, :], a["W_f1"]).then_inc(loaded["weights"], 16)
                pool.dma_start(t.w1[row + RBF:row + RBF + 1, k, :], a["b_f1"][None, :]).then_inc(loaded["weights"], 16)
            for k, w in enumerate((a["W_in2f"], a["W_f2"], a["W_o1"], a["W_o2"], a["W_self"], a["W_nb"])):
                pool.dma_start(t.weights[:, k, :], w).then_inc(loaded["weights"], 16)
            for k, v in enumerate((a["b_f2"], a["b_o2"], a["b_self"], a["b_nb"])):
                pool.dma_start(t.rows[:, k, :], v[None, :]).then_inc(loaded["weights"], 16)
            for k, v in enumerate((a["gamma"], a["beta"])):
                pool.dma_start(t.gb[:, k, :], v[None, :].to_broadcast([P, D])).then_inc(loaded["weights"], 16)
            pool.dma_start(t.b_o1[:, :], a["b_o1"][:, None]).then_inc(loaded["weights"], 16)
            n_tail = ET - EDGES
            head = n_tail // P * P
            pool.dma_start(t.messages[EDGES:EDGES + head, :].rearrange("(p k) d -> p (k d)", p=P), zero_rows[:, 0:head // P * MSG]).then_inc(tail_stored, 16)
            pool.dma_start(t.messages[EDGES + head:ET, :], zero_rows[0:n_tail - head, 0:MSG]).then_inc(tail_stored, 16)
            for q in range(NBP // 4):
                pool.wait_ge(h_copied, q + 1)
                hq, part = h[q % 2][:, :, :], lambda k: t.h3[:, 4 * q:4 * q + 4, k, :]
                g.tensor_copy(part(0), hq).then_inc(pool_h, 1)
                pool.wait_ge(pool_h, 5 * q + 1)
                g.tensor_tensor(rest[:, :, :], hq, part(0), ALU.subtract).then_inc(pool_h, 1)
                pool.wait_ge(pool_h, 5 * q + 2)
                g.tensor_copy(part(1), rest[:, :, :]).then_inc(pool_h, 1)
                pool.wait_ge(pool_h, 5 * q + 3)
                g.tensor_tensor(part(2), rest[:, :, :], part(1), ALU.subtract).then_inc(pool_h, 1)
                pool.wait_ge(pool_h, 5 * q + 4)
                g.memset(t.pool_junk[:, :], 0.0).then_inc(pool_h, 1)
                pool.wait_ge(pool_h, 5 * q + 5)
                pool.sem_inc(h_split, 1)
            pool.wait_ge(tail_stored, 32)
            pool.wait_ge(loaded["weights"], 21 * 16)

        @block.scalar
        def _(act):
            act.preload_act_table_set(EXP_LN)
            for q in range(NBP // 4):
                act.wait_ge(xT_made, q + 1)
                if q >= 2:
                    act.wait_ge(h_made, q - 1)
                nc.scalar.copy(xT[q % 2][:, :], psT[q % 2][:, :]).then_inc(xT_copied, 1)
                act.wait_ge(h_made, q + 1)
                if q >= 2:
                    act.wait_ge(h_split, q - 1)
                nc.scalar.copy(h[q % 2][:, :, :], psH[q % 2][:, :, :]).then_inc(h_copied, 1)
            act.wait_ge(pool_step, 14)
            act.wait_ge(hi_ready, 2)
            with act.Fori(0, NBU + 1) as b:
                nc.scalar.activation(sign_junk[:, :], hi_dst[:, :], ACT.Sign, bias=thresholds[:, bass.ds(b, 1)],
                                     accum_out=signs[:, bass.ds(b, 1)]).then_inc(sign_step, 1)
                act.wait_ge(sign_step, b + 1)

        @block.tensor
        def _(pe):
            def totals(n, key):
                pe.wait_ge(below_ready, n + 1)
                nc.tensor.matmul(ps_tot[key][:, 0, 0:NBU + 1], t.ones[:, :], below[key][:, :], start=True, stop=True)
                nc.tensor.matmul(ps_tot[key][:, 1, 0:NBU], t.before[:, :], count[key][:, :], start=True, stop=True).then_inc(totals_in, 1)

            pe.wait_ge(pool_step, 14)
            totals(0, "src")
            pe.wait_ge(loaded["weights"], 21 * 16)
            nc.tensor.matmul(ps_small[0:1, 0, :], t.ones[:, 0:1], t.weights[:, 1, :], start=True, stop=True)
            nc.tensor.matmul(ps_small[0:1, 1, :], t.ones[:, 0:1], t.weights[:, 3, :], start=True, stop=True).then_inc(small_made, 1)
            pe.wait_ge(loaded["x"], 64)
            for q in range(NBP // 4):
                if q >= 2:
                    pe.wait_ge(xT_copied, q - 1)
                for k in range(4):
                    last = nc.tensor.transpose(psT[q % 2][:, k * P:(k + 1) * P], t.x_nodes[:, 4 * q + k, :], t.ident[:, :])
                last.then_inc(xT_made, 1)
                pe.wait_ge(xT_copied, q + 1)
                if q >= 2:
                    pe.wait_ge(h_copied, q - 1)
                for k in range(4):
                    last = nc.tensor.matmul(psH[q % 2][:, k, :], xT[q % 2][:, k * P:(k + 1) * P], t.weights[:, 0, :], start=True, stop=True)
                last.then_inc(h_made, 1)
            totals(1, "dst")
            pe.wait_ge(meta_ready, 1)
            nc.tensor.matmul(ps_fell[:, 0:1], t.ones[:, :], fell_n[:, :], start=True, stop=True).then_inc(small_made, 1)

        @block.vector
        def _(dve):
            chain = Chain(dve, dve_step)
            v = nc.vector
            dve.wait_ge(loaded["src"], 16)
            chain.then(v.tensor_scalar(hi_i[:, :], src_i[:, :], 7, None, ALU.logical_shift_right))
            v.tensor_copy(hi_src[:, :], hi_i[:, :]).then_inc(hi_ready, 1)
            dve.wait_ge(hi_ready, 1)
            dve.wait_ge(loaded["dst"], 32)
            chain.then(v.tensor_scalar(hi_i[:, :], dst_i[:, :], 7, None, ALU.logical_shift_right))
            v.tensor_copy(hi_dst[:, :], hi_i[:, :]).then_inc(hi_ready, 1)
            dve.wait_ge(hi_ready, 2)
            chain.then(v.tensor_scalar(hi_i[:, :], next_i[:, :], 7, None, ALU.logical_shift_right))
            chain.then(v.tensor_copy(hi_next[:, :], hi_i[:, :]))
            chain.then(v.tensor_tensor(fell[:, :], hi_dst[:, :], hi_next[:, :], ALU.is_gt))
            chain.then(v.tensor_reduce(fell_n[:, :], fell[:, :], AX.X, ALU.add))
            dve.wait_ge(loaded["w"], 16)
            chain.then(v.tensor_copy(t.meta[:, :, 0], weight[:, :]))
            chain.then(v.tensor_copy(t.meta[:, :, 1], src_i[:, :]))
            chain.then(v.tensor_copy(t.meta[:, :, 2], dst_i[:, :]))
            dve.wait_ge(pool_step, 14)

            def places(n, key):
                v.tensor_tensor(count[key][:, :], below[key][:, 1:NBU + 1], below[key][:, 0:NBU], ALU.subtract).then_inc(below_ready, 1)
                dve.wait_ge(totals_in, n + 1)
                chain.then(v.tensor_copy(start[key][:, :], ps_tot[key][:, 0, 0:NBU + 1]))
                chain.then(v.tensor_tensor(base[key][:, 0:NBU], start[key][:, 0:NBU], ps_tot[key][:, 1, 0:NBU], ALU.add))

            with dve.Fori(0, NBU + 1) as b:
                v.tensor_scalar(fell[:, :], hi_src[:, :], t.bucket_ids[:, bass.ds(b, 1)], 0.0, ALU.is_lt, ALU.add,
                                accum_out=below["src"][:, bass.ds(b, 1)]).then_inc(below_step, 1)
                dve.wait_ge(below_step, b + 1)
            places(0, "src")
            rank_buckets(nc, dve, t, hi_src[:, :], base["src"], pos[:, :], [fell[:, :].bitcast(U16), hi_next[:, :].bitcast(U16)],
                         [next_i[:, :].bitcast(F32), hi_i[:, :].bitcast(F32)], rank_step)
            v.tensor_scalar(t.meta[:, :, 3], pos[:, :], -1.0, None, ALU.add).then_inc(meta_ready, 1)
            window_tables(nc, chain, sb, t, start["src"], G4, Q4, "src", weight)
            v.memset(t.dve_junk[:, 0:1], 0.0).then_inc(tables_ready, 1)
            dve.wait_ge(sign_step, NBU + 1)
            chain.then(v.tensor_scalar(below["dst"][:, :], signs[:, :], -0.5, COLS / 2.0, ALU.mult, ALU.add))
            places(1, "dst")
            window_tables(nc, chain, sb, t, start["dst"], G2, Q2, "dst", weight)
            v.memset(t.dve_junk[:, 1:2], 0.0).then_inc(tables_ready, 1)
            dve.wait_ge(small_made, 1)
            chain.then(v.scalar_tensor_tensor(b2row[:, :], ps_small[0:1, 0, :], -LOG2, t.rows[:, 0, :], ALU.mult, ALU.add))
            chain.then(v.scalar_tensor_tensor(t.bo2[:, :], ps_small[0:1, 1, :], -LOG2, t.rows[:, 1, :], ALU.mult, ALU.add))
            chain.then(v.tensor_tensor(t.bself_nb[:, :], t.rows[:, 2, :], t.rows[:, 3, :], ALU.add))
            chain.then(v.tensor_copy(b2part[:, 0, :], b2row[:, :]))
            chain.then(v.tensor_tensor(b2rest[:, :], b2row[:, :], b2part[:, 0, :], ALU.subtract))
            chain.then(v.tensor_copy(b2part[:, 1, :], b2rest[:, :]))
            v.tensor_tensor(b2part[:, 2, :], b2rest[:, :], b2part[:, 1, :], ALU.subtract).then_inc(b2_ready, 1)
            dve.wait_ge(small_made, 2)
            v.tensor_copy(flag[:, :], ps_fell[:, 0:1]).then_inc(dve_step, 1)


def order_by_dst(nc, t, a):
    with ExitStack() as ctx:
        def sb(name, shape, dt=F32):
            return ctx.enter_context(nc.sbuf_tensor(name, shape, dt))

        def sem(name):
            return ctx.enter_context(nc.semaphore(name))

        pos, place = sb("pos_dst", [P, COLS]), sb("place", [P, COLS], I32)
        masks, runs = [sb(f"mask{k}", [P, COLS], U16) for k in range(2)], [sb(f"run{k}", [P, COLS]) for k in range(2)]
        GROUP = 16
        place16, meta16 = sb("place16", [P, GROUP], I32), sb("meta16", [P, GROUP, 4])
        filt16 = sb("filt16", [P, GROUP, RBF])
        ranked, placed, taken, moved, filt_in = (sem(x) for x in ("ranked", "placed", "taken", "moved", "filt_in"))
        block = ctx.enter_context(nc.Block())

        @block.vector
        def _(dve):
            unordered = dve.value_load(t.flag[0:1, 0:1], min_val=0, max_val=ET)
            with dve.If(unordered > 0):
                rank_buckets(nc, dve, t, t.hi_dst[:, :], t.base_dst, pos[:, :], [m[:, :] for m in masks], [r[:, :] for r in runs], ranked)
                nc.vector.tensor_scalar(place[:, :], pos[:, :], -1.0, None, ALU.add).then_inc(placed, 1)
                dve.wait_ge(placed, 1)
            dve.nop()

        @block.gpsimd
        def _(pool):
            unordered = pool.value_load(t.flag[0:1, 0:1], min_val=0, max_val=ET)
            with pool.If(unordered > 0):
                g = nc.gpsimd
                pool.wait_ge(placed, 1)
                with pool.Fori(0, COLS // GROUP) as j:
                    src = a["edge_attr"].rearrange("(p c) f -> p c f", p=P)
                    pool.dma_start(filt16[:, :, :], src[:, bass.ds(j * GROUP, GROUP), :]).then_inc(filt_in, 16)
                    g.tensor_copy(place16[:, :], place[:, bass.ds(j * GROUP, GROUP)]).then_inc(taken, 1)
                    g.tensor_copy(meta16[:, :, :], t.meta[:, bass.ds(j * GROUP, GROUP), :]).then_inc(taken, 1)
                    pool.wait_ge(taken, 2 * j + 2)
                    pool.sem_inc(t.ticks, 1)
                    pool.wait_ge(filt_in, 16 * j + 16)
                    pool.sem_inc(t.ticks, 1)
                    for c in range(GROUP):
                        to = bass.IndirectOffsetOnAxis(ap=place16[:, c:c + 1], axis=0)
                        pool.indirect_dma_start(t.meta_by_dst, to, meta16[:, c, :], None).then_inc(moved, 16)
                        pool.indirect_dma_start(t.filters_by_dst, to, filt16[:, c, :], None).then_inc(moved, 16)
                    pool.wait_ge(moved, 32 * GROUP * j + 32 * GROUP)
                    pool.sem_inc(t.ticks, 1)
            pool.nop()


def steps(eng, n, *stages):
    def step(j, u):
        for lag, stage in stages:
            back = -(-(lag - u) // BODY) if lag > u else 0
            j0, u0 = j - BODY * back, u - lag + BODY * back
            if isinstance(j0, int) and not 0 <= j0 + u0 < n:
                continue
            stage(j0, u0)

    first = BODY - (-max(lag for lag, _ in stages) // BODY) * BODY
    for j in range(0, first, BODY):
        for u in range(BODY):
            step(j, u)
    with eng.Fori(first, n, BODY) as j:
        for u in range(BODY):
            step(j, u)
    for u in range(max(lag for lag, _ in stages)):
        step(n, u)


def wait(eng, sem, value):
    if not isinstance(value, int) or value > 0:
        eng.wait_ge(sem, value)


def rounds(j, back, n):
    return j * (16 * n // BODY) + 16 * n * (1 - back)


def load_rows(nc, sp, tab, row, first, n, most):
    _, values = nc.values_load_multi_w_load_instructions(tab[0:1, row, bass.ds(first, n)], engines=[sp.engine], min_val=0,
                                                         max_val=most, skip_runtime_bounds_check_because=ROWS_OK)
    return values


def messages(nc, t):
    with ExitStack() as ctx:
        def sb(name, shape, dt=F32):
            return ctx.enter_context(nc.sbuf_tensor(name, shape, dt))

        def ps(name, shape, dt=F32):
            return ctx.enter_context(nc.psum_tensor(name, shape, dt))

        def sem(name):
            return ctx.enter_context(nc.semaphore(name))

        W, K = STEP // 2, 2
        N = NW2 // W
        meta = [sb(f"meta{u}", [P, STEP, 4]) for u in range(BODY)]
        filt = t.f_ones
        place = [sb(f"place{u}", [P, STEP], I32) for u in range(BODY)]
        local, outside = [sb(f"local{u}", [P, STEP]) for u in range(2)], [sb(f"outside{u}", [P, STEP]) for u in range(2)]
        member = [sb(f"member{u}", [P, STEP, P], BF16) for u in range(2)]
        filtT = [sb(f"filtT{u}", [P, P]) for u in range(2)]
        memberT = [sb(f"memberT{u}", [P, STEP, P], BF16) for u in range(2)]
        grown, soft, act1 = ([sb(f"{x}{u}", [P, STEP * P]) for u in range(2)] for x in ("grown", "soft", "act1"))
        hdst = [sb(f"hdst{u}", [P, STEP, D]) for u in range(2)]
        msg = [sb(f"msg{u}", [P, STEP, MSG]) for u in range(BODY)]
        ps_filtT, ps_memberT = ps("ps_filtT", [P, STEP * P]), ps("ps_memberT", [P, 2 * STEP, P], BF16)
        ps_pre, ps_filter, ps_hdst = ([ps(f"{x}{u}", [P, STEP, P]) for u in range(2)] for x in ("ps_pre", "ps_filter", "ps_hdst"))

        loaded, scattered = [sem(f"loaded{u}") for u in range(BODY)], [sem(f"scattered{u}") for u in range(BODY)]
        (local_ok, outside_ok, member_ok, place_ok, filtT_made, memberT_made, filtT_ok, memberT_ok, pre_made, hdst_made,
         grown_ok, soft_ok, hdst_ok, act1_ok, filter_made, msg_ok) = (sem(x) for x in (
             "local_ok", "outside_ok", "member_ok", "place_ok", "filtT_made", "memberT_made", "filtT_ok", "memberT_ok", "pre_made",
             "hdst_made", "grown_ok", "soft_ok", "hdst_ok", "act1_ok", "filter_made", "msg_ok"))
        block = ctx.enter_context(nc.Block())

        @block.sync
        def _(sp):
            def load(j, u):
                i = j + u
                wait(sp, filtT_made, i - BODY + 1)
                wait(sp, msg_ok, i - BODY + 1)
                for w, row in enumerate(load_rows(nc, sp, t.regs["dst"], 0, W * i, W, ET - G2)):
                    sp.dma_start(filt[:, u, K * w:K * w + K, 0:RBF], t.filters_by_dst[bass.ds(row, G2), :].rearrange("(p k) f -> p k f", p=P)).then_inc(loaded[u], 16)
                    sp.dma_start(meta[u][:, K * w:K * w + K, :], t.meta_by_dst[bass.ds(row, G2), :].rearrange("(p k) f -> p k f", p=P)).then_inc(loaded[u], 16)

            steps(sp, N, (0, load))

        @block.vector
        def _(dve):
            v = nc.vector

            def classify(j, u):
                i, b = j + u, u % 2
                dve.wait_ge(loaded[u], rounds(j, 0, 2 * W))
                v.tensor_tensor(local[b][:, :].rearrange("p (w k) -> p w k", w=W), meta[u][:, :, 2].rearrange("p (w k) -> p w k", w=W),
                                t.first["dst"][:, bass.ds(W * i, W)][:, :, None].to_broadcast([P, W, K]), ALU.subtract).then_inc(local_ok, 1)
                dve.wait_ge(local_ok, i + 1)
                wait(dve, memberT_made, i - 1)
                for k in range(STEP):
                    last = v.tensor_scalar(member[b][:, k, :], t.ids16[:, :], local[b][:, k:k + 1], None, ALU.is_equal)
                last.then_inc(member_ok, 1)
                v.tensor_scalar(outside[b][:, :], local[b][:, :], P - 0.5, SKIP, ALU.is_gt, ALU.mult).then_inc(outside_ok, 1)
                dve.wait_ge(outside_ok, i + 1)
                wait(dve, scattered[u], rounds(j, 1, STEP))
                v.tensor_tensor(place[u][:, :], outside[b][:, :], meta[u][:, :, 3], ALU.add).then_inc(place_ok, 1)

            def softplus(j, u):
                i, b = j + u, u % 2
                dve.wait_ge(soft_ok, i + 1)
                wait(dve, filter_made, i - 1)
                v.scalar_tensor_tensor(act1[b][:, :], soft[b][:, :], CAP, ps_pre[b][:, :, :].rearrange("p k e -> p (k e)"), ALU.min, ALU.max).then_inc(act1_ok, 1)

            def product(j, u):
                i, b = j + u, u % 2
                dve.wait_ge(filter_made, i + 1)
                dve.wait_ge(hdst_ok, i + 1)
                wait(dve, scattered[u], rounds(j, 1, STEP))
                for k in range(STEP):
                    v.scalar_tensor_tensor(msg[u][:, k, 0:D], ps_filter[b][:, k, :], meta[u][:, k, 0:1], hdst[b][:, k, :], ALU.mult, ALU.mult)
                v.tensor_copy(msg[u][:, :, D], meta[u][:, :, 1]).then_inc(msg_ok, 1)

            steps(dve, N, (0, classify), (4, product), (3, softplus))

        @block.tensor
        def _(pe):
            def transposes(j, u):
                i, b = j + u, u % 2
                pe.wait_ge(loaded[u], rounds(j, 0, 2 * W))
                wait(pe, filtT_ok, i)
                nc.tensor.transpose(ps_filtT[:, 0:P], filt[:, u, :, :], t.ident[:, :]).then_inc(filtT_made, 1)
                pe.wait_ge(member_ok, i + 1)
                wait(pe, memberT_ok, i)
                for k in range(STEP):
                    last = nc.tensor.transpose(ps_memberT[:, k, :], member[b][:, k, :], t.ident16[:, :])
                last.then_inc(memberT_made, 1)

            def first_filter(j, u):
                i, b = j + u, u % 2
                pe.wait_ge(filtT_ok, i + 1)
                wait(pe, act1_ok, i - 1)
                for k in range(STEP):
                    last = nc.tensor.matmul(ps_pre[b][:, k, :], t.w1[:, k, :], filtT[b][:, :], start=True, stop=True)
                last.then_inc(pre_made, 1)
                pe.wait_ge(memberT_ok, i + 1)
                wait(pe, hdst_ok, i - 1)
                blocks = load_rows(nc, pe, t.regs["dst"], 2, W * i, W, (NBLK - 1) * 3 * D)
                table = t.h3[:, :, :, :].rearrange("p b k d -> p (b k d)")
                for k in range(STEP):
                    for part in range(3):
                        last = nc.tensor.matmul(ps_hdst[b][:, k, :], memberT[b][:, k, :], table[:, bass.ds(blocks[k // K] + part * D, D)],
                                                start=(part == 0), stop=(part == 2))
                last.then_inc(hdst_made, 1)

            def second_filter(j, u):
                i, b = j + u, u % 2
                wait(pe, msg_ok, i - 1)
                nc.tensor.matmul(ps_filter[b][:, :, :], t.ones3[:, :], t.b2_rows[:, :, :], start=True, stop=False, skip_group_check=True)
                pe.wait_ge(act1_ok, i + 1)
                for k in range(STEP):
                    last = nc.tensor.matmul(ps_filter[b][:, k, :], act1[b][:, k * P:(k + 1) * P], t.weights[:, 1, :],
                                            start=False, stop=True, skip_group_check=True)
                last.then_inc(filter_made, 1)

            steps(pe, N, (4, second_filter), (1, transposes), (2, first_filter))

        @block.scalar
        def _(act):
            s = nc.scalar
            act.preload_act_table_set(EXP_LN)

            def evacuate(j, u):
                i, b = j + u, u % 2
                act.wait_ge(filtT_made, i + 1)
                wait(act, pre_made, i - 1)
                s.copy(filtT[b][:, :], ps_filtT[:, 0:P]).then_inc(filtT_ok, 1)
                act.wait_ge(memberT_made, i + 1)
                wait(act, hdst_made, i - 1)
                s.copy(memberT[b][:, :, :], ps_memberT[:, 0:STEP, :]).then_inc(memberT_ok, 1)

            def softplus(j, u):
                i, b = j + u, u % 2
                act.wait_ge(pre_made, i + 1)
                s.activation(grown[b][:, :], ps_pre[b][:, :, :].rearrange("p k e -> p (k e)"), ACT.Exp).then_inc(grown_ok, 1)
                act.wait_ge(hdst_made, i + 1)
                wait(act, msg_ok, i - 1)
                s.copy(hdst[b][:, :, :], ps_hdst[b][:, :, :]).then_inc(hdst_ok, 1)
                act.wait_ge(grown_ok, i + 1)
                wait(act, act1_ok, i - 1)
                s.activation(soft[b][:, :], grown[b][:, :], ACT.Ln, bias=1.0).then_inc(soft_ok, 1)

            steps(act, N, (3, softplus), (1, evacuate))

        @block.gpsimd
        def _(pool):
            def scatter(j, u):
                i = j + u
                pool.wait_ge(msg_ok, i + 1)
                pool.sem_inc(t.ticks, 1)
                for k in range(STEP):
                    pool.indirect_dma_start(t.messages, bass.IndirectOffsetOnAxis(ap=place[u][:, k:k + 1], axis=0), msg[u][:, k, :], None,
                                            bounds_check=ET - 1, oob_is_err=False).then_inc(scattered[u], 16)

            steps(pool, N, (0, scatter))
            for u in range(BODY):
                pool.wait_ge(scattered[u], 16 * STEP * N // BODY)


def sum_messages(nc, t):
    with ExitStack() as ctx:
        def sb(name, shape, dt=F32):
            return ctx.enter_context(nc.sbuf_tensor(name, shape, dt))

        def sem(name):
            return ctx.enter_context(nc.semaphore(name))

        msg = [sb(f"msg_in{u}", [P, STEP, MSG]) for u in range(BODY)]
        B = 4
        local, member = [sb(f"local_src{u}", [P, STEP], BF16) for u in range(B)], [sb(f"member_src{u}", [P, STEP, P]) for u in range(B)]
        ps_sum = [ctx.enter_context(nc.psum_tensor(f"ps_sum{u}", [P, 4 * P], F32)) for u in range(B)]
        loaded = [sem(f"msg_loaded{u}") for u in range(BODY)]
        cleared, local_ok, member_ok, sum_made, sum_added = (sem(x) for x in ("cleared", "local_src_ok", "member_src_ok", "sum_made", "sum_added"))
        block = ctx.enter_context(nc.Block())

        @block.sync
        def _(sp):
            def load(j, u):
                i = j + u
                wait(sp, sum_made, i - BODY + 1)
                row, = load_rows(nc, sp, t.regs["src"], 0, i, 1, ET - G4)
                sp.dma_start(msg[u][:, :, :].rearrange("p k d -> p (k d)"), t.messages[bass.ds(row, G4), :].rearrange("(p k) d -> p (k d)", p=P)).then_inc(loaded[u], 16)

            steps(sp, NW4, (0, load))

        @block.vector
        def _(dve):
            v = nc.vector

            def classify(j, u):
                i, b = j + u, u % B
                dve.wait_ge(loaded[u], rounds(j, 0, 1))
                v.tensor_tensor(local[b][:, :], msg[u][:, :, D], t.first["src"][:, bass.ds(i, 1)].to_broadcast([P, STEP]), ALU.subtract).then_inc(local_ok, 1)
                dve.wait_ge(local_ok, i + 1)
                wait(dve, sum_made, i - B + 1)
                wide = [P, STEP, P]
                v.tensor_tensor(member[b][:, :, :], t.ids16[:, None, :].to_broadcast(wide), local[b][:, :, None].to_broadcast(wide), ALU.is_equal).then_inc(member_ok, 1)

            def add(j, u):
                i, b = j + u, u % B
                at, = load_rows(nc, dve, t.regs["src"], 1, i, 1, (NBLK - 1) * MSG)
                dve.wait_ge(sum_made, i + 1)
                wait(dve, sum_added, i)
                v.tensor_tensor(t.sums[:, bass.ds(at, D)], t.sums[:, bass.ds(at, D)], ps_sum[b][:, 0:D], ALU.add).then_inc(sum_added, 1)

            v.memset(t.sums[:, :], 0.0).then_inc(cleared, 1)
            dve.wait_ge(cleared, 1)
            steps(dve, NW4, (0, classify), (2, add))

        @block.tensor
        def _(pe):
            def total(j, u):
                i, b = j + u, u % B
                pe.wait_ge(member_ok, i + 1)
                wait(pe, sum_added, i - B + 1)
                for k in range(STEP):
                    last = nc.tensor.matmul(ps_sum[b][:, 0:D], member[b][:, k, :], msg[u][:, k, 0:D], start=(k == 0), stop=(k == STEP - 1))
                last.then_inc(sum_made, 1)

            steps(pe, NW4, (0, total))


QB = NBP // 4


def moments(nc, chain, stats, mean, var, scratch):
    v = nc.vector
    chain.then(v.tensor_tensor(mean, stats[:, :, 1], stats[:, :, 4], ALU.add))
    chain.then(v.tensor_scalar(mean, mean, 0.5, None, ALU.mult))
    chain.then(v.tensor_tensor(scratch, stats[:, :, 1], mean, ALU.subtract))
    chain.then(v.tensor_tensor(scratch, scratch, scratch, ALU.mult))
    chain.then(v.tensor_tensor(var, stats[:, :, 2], stats[:, :, 5], ALU.add))
    chain.then(v.scalar_tensor_tensor(var, var, 1.0 / D, scratch, ALU.mult, ALU.add))


def norms_squared(nc, chain, out, mean, var):
    v = nc.vector
    chain.then(v.tensor_tensor(out, mean, mean, ALU.mult))
    chain.then(v.tensor_tensor(out, out, var, ALU.add))
    chain.then(v.tensor_scalar(out, out, float(D), None, ALU.mult))


def square_roots(nc, act, squares, roots, asked, made, first, n):
    for k in range(first, first + n):
        act.wait_ge(asked, k + 1)
        nc.scalar.activation(roots, squares, ACT.Sqrt).then_inc(made, 1)


ACT_BLOCKS = 4


def first_layer_out(nc, t):
    with ExitStack() as ctx:
        def sb(name, shape, dt=F32):
            return ctx.enter_context(nc.sbuf_tensor(name, shape, dt))

        def ps(name):
            return [ctx.enter_context(nc.psum_tensor(f"{name}{u}", [P, 4 * P], F32)) for u in range(2)]

        def sem(name):
            return ctx.enter_context(nc.semaphore(name))

        B = QB
        aggT, grown, soft, act1 = ([sb(f"{x}{u}", [P, 4 * P]) for u in range(2)] for x in ("aggT", "grown_o", "soft_o", "act1_o"))
        stats = sb("stats", [P, NBP, 6])
        mean, var, scratch, roots, rstd, shift = (sb(f"{x}_x1", [P, NBP])[:, :] for x in ("mean", "var", "scratch", "roots", "rstd", "shift"))
        ps_aggT, ps_pre, ps_out = ps("ps_aggT"), ps("ps_pre_o"), ps("ps_out")
        (aggT_made, aggT_ok, pre_made, grown_ok, soft_ok, capped, act1_ok, out_made, out_added, stats_ok, asked, made, rstd_ok,
         dve_normal, act_normal, x1_stored, dve_step) = (sem(x) for x in (
             "aggT_made", "aggT_ok", "pre_o_made", "grown_o_ok", "soft_o_ok", "capped", "act1_o_ok", "out_made", "out_added", "stats_ok",
             "root_asked", "root_made", "rstd_ok", "dve_normal", "act_normal", "x1_stored", "x1_step"))
        block = ctx.enter_context(nc.Block())

        @block.tensor
        def _(pe):
            for q in range(B + 3):
                if q < B:
                    wait(pe, aggT_ok, q - 1)
                    for k in range(4):
                        at = (4 * q + k) * MSG
                        last = nc.tensor.transpose(ps_aggT[q % 2][:, k * P:(k + 1) * P], t.sums[:, at:at + D], t.ident[:, :])
                    last.then_inc(aggT_made, 1)
                if 0 <= q - 1 < B:
                    r = q - 1
                    pe.wait_ge(aggT_ok, r + 1)
                    wait(pe, act1_ok, r - 1)
                    nc.tensor.matmul(ps_pre[r % 2][:, :], t.weights[:, 2, :], aggT[r % 2][:, :], start=True, stop=True).then_inc(pre_made, 1)
                if 0 <= q - 3 < B:
                    r = q - 3
                    pe.wait_ge(act1_ok, r + 1)
                    wait(pe, out_added, r - 1)
                    for k in range(4):
                        nc.tensor.matmul(ps_out[r % 2][:, k * P:(k + 1) * P], act1[r % 2][:, k * P:(k + 1) * P], t.weights[:, 3, :], start=True, stop=False)
                        last = nc.tensor.matmul(ps_out[r % 2][:, k * P:(k + 1) * P], t.ones[0:1, :], t.bo2[:, :], start=False, stop=True)
                    last.then_inc(out_made, 1)

        @block.scalar
        def _(act):
            s = nc.scalar
            act.preload_act_table_set(EXP_LN)
            for q in range(B + 1):
                if q < B:
                    act.wait_ge(aggT_made, q + 1)
                    wait(act, pre_made, q - 1)
                    s.copy(aggT[q % 2][:, :], ps_aggT[q % 2][:, :]).then_inc(aggT_ok, 1)
                if q >= 1:
                    r = q - 1
                    act.wait_ge(pre_made, r + 1)
                    s.activation(grown[r % 2][:, :], ps_pre[r % 2][:, :], ACT.Exp, bias=t.b_o1[:, 0:1]).then_inc(grown_ok, 1)
                    act.wait_ge(grown_ok, r + 1)
                    wait(act, act1_ok, r - 1)
                    s.activation(soft[r % 2][:, :], grown[r % 2][:, :], ACT.Ln, bias=1.0).then_inc(soft_ok, 1)
            square_roots(nc, act, var, roots, asked, made, 0, 1)
            act.wait_ge(rstd_ok, 1)
            for q in range(4):
                for b in range((q + 1) * QB - ACT_BLOCKS, (q + 1) * QB):
                    last = s.activation(t.x_nodes[:, b, :], t.x_nodes[:, b, :], ACT.Identity, bias=shift[:, b:b + 1], scale=rstd[:, b:b + 1])
                last.then_inc(act_normal, 1)

        @block.vector
        def _(dve):
            v = nc.vector
            chain = Chain(dve, dve_step)
            for q in range(B + 2):
                if q < B:
                    dve.wait_ge(soft_ok, q + 1)
                    v.tensor_scalar(soft[q % 2][:, :], soft[q % 2][:, :], CAP, None, ALU.min).then_inc(capped, 1)
                if q >= 2:
                    r = q - 2
                    dve.wait_ge(out_made, r + 1)
                    x = t.x_nodes[:, 4 * r:4 * r + 4, :].rearrange("p b d -> p (b d)")
                    v.tensor_tensor(x, x, ps_out[r % 2][:, :], ALU.add).then_inc(out_added, 1)
                if q < B:
                    dve.wait_ge(capped, q + 1)
                    wait(dve, out_made, q - 1)
                    v.scalar_tensor_tensor(act1[q % 2][:, :], ps_pre[q % 2][:, :], t.b_o1[:, 0:1], soft[q % 2][:, :], ALU.add, ALU.max).then_inc(act1_ok, 1)
                if q >= 2:
                    dve.wait_ge(out_added, q - 1)
                    for k in range(4):
                        last = v.bn_stats(stats[:, 4 * (q - 2) + k, :], t.x_nodes[:, 4 * (q - 2) + k, :])
                    last.then_inc(stats_ok, 1)
            dve.wait_ge(stats_ok, B)
            moments(nc, chain, stats, mean, var, scratch)
            v.tensor_scalar(var, var, LN_EPS, None, ALU.add).then_inc(asked, 1)
            dve.wait_ge(made, 1)
            chain.then(v.reciprocal(rstd, roots))
            v.scalar_tensor_tensor(shift, mean, -1.0, rstd, ALU.mult, ALU.mult).then_inc(rstd_ok, 1)
            for q in range(4):
                for b in range(q * QB, (q + 1) * QB - ACT_BLOCKS):
                    last = v.tensor_scalar(t.x_nodes[:, b, :], t.x_nodes[:, b, :], mean[:, b:b + 1], rstd[:, b:b + 1], ALU.subtract, ALU.mult)
                last.then_inc(dve_normal, 1)

        @block.sync
        def _(sp):
            for q in range(4):
                sp.wait_ge(dve_normal, q + 1)
                sp.wait_ge(act_normal, q + 1)
                sp.dma_start(t.x1_dram[q * QB * P:(q + 1) * QB * P, :].rearrange("(b p) d -> p b d", p=P), t.x_nodes[:, q * QB:(q + 1) * QB, :]).then_inc(x1_stored, 16)
            sp.wait_ge(x1_stored, 64)


def attention(nc, t):
    with ExitStack() as ctx:
        def sb(name, shape, dt=F32):
            return ctx.enter_context(nc.sbuf_tensor(name, shape, dt))

        def ps(name):
            return [ctx.enter_context(nc.psum_tensor(f"{name}{u}", [P, 4 * P], F32)) for u in range(2)]

        def sem(name):
            return ctx.enter_context(nc.semaphore(name))

        W, K = STEP // 2, 2
        N = NW2 // W
        NONE = BIG / 2
        meta = [sb(f"meta_l1{u}", [P, STEP, 4]) for u in range(BODY)]
        source = [sb(f"source{u}", [P, STEP], I32) for u in range(BODY)]
        xg = [sb(f"xg{u}", [P, STEP, MSG]) for u in range(BODY)]
        local = [sb(f"local_l1{u}", [P, STEP]) for u in range(2)]
        other = [sb(f"other{u}", [P, STEP, P], BF16) for u in range(2)]
        top = [sb(f"top{u}", [P, W]) for u in range(BODY)]
        below = [sb(f"minus_top{u}", [P, W]) for u in range(BODY)]
        new, diff, shrink = ([sb(f"{x}{u}", [P, W]) for u in range(BODY)] for x in ("new_max", "diff", "shrink"))
        fresh = sb("fresh", [P, P * Q2])
        grown, share = [sb(f"ew{u}", [P, STEP * P]) for u in range(2)], [sb(f"ewT{u}", [P, STEP, P]) for u in range(2)]
        ps_w, ps_ewT, ps_sum = ps("ps_w"), ps("ps_ewT"), ps("ps_l1")
        loaded, gathered = [sem(f"meta_l1_loaded{u}") for u in range(BODY)], [sem(f"gathered{u}") for u in range(BODY)]
        (source_ok, local_ok, other_ok, w_made, top_ok, below_ok, new_ok, diff_ok, ew_ok, ewT_made, ewT_ok, sum_made, sum_added,
         start_ok) = (sem(x) for x in ("source_ok", "local_l1_ok", "other_ok", "w_made", "top_ok", "minus_top_ok", "new_ok", "diff_ok", "ew_ok",
                                       "ewT_made", "ewT_ok", "l1_sum_made", "l1_sum_added", "start_ok"))
        block = ctx.enter_context(nc.Block())

        @block.sync
        def _(sp):
            def load(j, u):
                i = j + u
                wait(sp, w_made, i - BODY + 1)
                rows = load_rows(nc, sp, t.regs["dst"], 0, W * i, W, ET - G2)
                for w in range(W):
                    sp.dma_start(meta[u][:, K * w:K * w + K, :].rearrange("p k d -> p (k d)"),
                                 t.meta_by_dst[bass.ds(rows[w], G2), :].rearrange("(p k) d -> p (k d)", p=P)).then_inc(loaded[u], 16)

            steps(sp, N, (0, load))

        @block.gpsimd
        def _(pool):
            for u in range(BODY):
                nc.gpsimd.memset(xg[u][:, :, D:MSG], 1.0).then_inc(start_ok, 1)
            pool.wait_ge(start_ok, BODY)

            def gather(j, u):
                i = j + u
                pool.wait_ge(source_ok, i + 1)
                pool.sem_inc(t.ticks, 1)
                if not isinstance(j, int) or i >= BODY:
                    pool.wait_ge(sum_made, i - BODY + 1)
                    pool.sem_inc(t.ticks, 1)
                for k in range(STEP):
                    pool.indirect_dma_start(xg[u][:, k, 0:D], None, t.x1_dram, bass.IndirectOffsetOnAxis(ap=source[u][:, k:k + 1], axis=0),
                                            bounds_check=NBP * P - 1, oob_is_err=False).then_inc(gathered[u], 16)

            steps(pool, N, (0, gather))
            for u in range(BODY):
                pool.wait_ge(gathered[u], 16 * STEP * N // BODY)

        @block.vector
        def _(dve):
            v = nc.vector
            chain = Chain(dve, sem("l1_start"))
            chain.then(v.memset(t.sums[:, :], 0.0))
            chain.then(v.memset(new[BODY - 1][:, :], NONE))
            chain.then(v.memset(fresh[:, 0:1], 1.0))
            chain.then(v.tensor_tensor(fresh[:, 1:], t.first["dst"][:, 1:], t.first["dst"][:, 0:P * Q2 - 1], ALU.not_equal))
            chain.then(v.tensor_scalar(fresh[:, :], fresh[:, :], 2 * NONE, -NONE, ALU.mult, ALU.add))

            def classify(j, u):
                i, b = j + u, u % 2
                dve.wait_ge(loaded[u], rounds(j, 0, W))
                wait(dve, gathered[u], rounds(j, 1, STEP))
                v.tensor_copy(source[u][:, :], meta[u][:, :, 1]).then_inc(source_ok, 1)
                v.tensor_tensor(local[b][:, :].rearrange("p (w k) -> p w k", w=W), meta[u][:, :, 2].rearrange("p (w k) -> p w k", w=W),
                                t.first["dst"][:, bass.ds(W * i, W)][:, :, None].to_broadcast([P, W, K]), ALU.subtract).then_inc(local_ok, 1)
                dve.wait_ge(local_ok, i + 1)
                wait(dve, w_made, i - 1)
                for k in range(STEP):
                    last = v.tensor_scalar(other[b][:, k, :], t.ids16[:, :], local[b][:, k:k + 1], None, ALU.not_equal)
                last.then_inc(other_ok, 1)

            def maxima(j, u):
                i, b = j + u, u % 2
                dve.wait_ge(w_made, i + 1)
                v.tensor_reduce(top[u][:, :], ps_w[b][:, :].rearrange("p (w e) -> p w e", w=W), AX.X, ALU.max).then_inc(top_ok, 1)
                dve.wait_ge(top_ok, i + 1)
                v.tensor_scalar(below[u][:, :], top[u][:, :], -1.0, NONE, ALU.mult, ALU.min).then_inc(below_ok, 1)
                dve.wait_ge(below_ok, i + 1)
                before = new[(u - 1) % BODY][:, W - 1:W]
                v.tensor_tensor_scan(new[u][:, :], fresh[:, bass.ds(W * i, W)], below[u][:, :], before, ALU.max, ALU.min).then_inc(new_ok, 1)
                dve.wait_ge(new_ok, i + 1)
                v.tensor_scalar(diff[u][:, 0:1], new[u][:, 0:1], before, 0.0, ALU.subtract, ALU.min)
                v.tensor_scalar(diff[u][:, 1:2], new[u][:, 1:2], new[u][:, 0:1], 0.0, ALU.subtract, ALU.min).then_inc(diff_ok, 1)

            def add(j, u):
                i, b = j + u, u % 2
                at = load_rows(nc, dve, t.regs["dst"], 1, W * i, W, (NBLK - 1) * MSG)
                dve.wait_ge(sum_made, i + 1)
                for w in range(W):
                    wait(dve, sum_added, i * W + w)
                    sums = t.sums[:, bass.ds(at[w], MSG)]
                    v.scalar_tensor_tensor(sums, sums, shrink[u][:, w:w + 1], ps_sum[b][:, w * 256:w * 256 + MSG], ALU.mult, ALU.add).then_inc(sum_added, 1)

            steps(dve, N, (2, maxima), (0, classify), (6, add))

        @block.tensor
        def _(pe):
            def weights(j, u):
                i, b = j + u, u % 2
                pe.wait_ge(other_ok, i + 1)
                wait(pe, ew_ok, i - 1)
                for k in range(STEP):
                    to = ps_w[b][:, k * P:(k + 1) * P]
                    nc.tensor.matmul(to, meta[u][:, k, 0:1].to_broadcast([P, P]), t.ident[:, :], start=True, stop=False, skip_group_check=True)
                    last = nc.tensor.matmul(to, other[b][:, k, :], t.minus_big[:, :], start=False, stop=True, skip_group_check=True)
                last.then_inc(w_made, 1)

            def transposes(j, u):
                i, b = j + u, u % 2
                pe.wait_ge(ew_ok, i + 1)
                wait(pe, ewT_ok, i - 1)
                for k in range(STEP):
                    last = nc.tensor.transpose(ps_ewT[b][:, k * P:(k + 1) * P], grown[b][:, k * P:(k + 1) * P], t.ident[:, :])
                last.then_inc(ewT_made, 1)

            def total(j, u):
                i, b = j + u, u % 2
                pe.wait_ge(ewT_ok, i + 1)
                pe.wait_ge(gathered[u], rounds(j, 0, STEP))
                wait(pe, sum_added, W * (i - 1))
                for k in range(STEP):
                    at = k // K * 256
                    last = nc.tensor.matmul(ps_sum[b][:, at:at + MSG], share[b][:, k, :], xg[u][:, k, :], start=(k % K == 0), stop=(k % K == K - 1))
                last.then_inc(sum_made, 1)

            pe.wait_ge(start_ok, BODY)
            steps(pe, N, (4, transposes), (1, weights), (5, total))

        @block.scalar
        def _(act):
            s = nc.scalar
            act.preload_act_table_set(EXP_LN)

            def exponentials(j, u):
                i, b = j + u, u % 2
                act.wait_ge(diff_ok, i + 1)
                wait(act, ewT_made, i - 1)
                for w in range(W):
                    cols = slice(w * K * P, (w + 1) * K * P)
                    s.activation(grown[b][:, cols], ps_w[b][:, cols], ACT.Exp, bias=new[u][:, w:w + 1])
                s.activation(shrink[u][:, :], diff[u][:, :], ACT.Exp).then_inc(ew_ok, 1)

            def evacuate(j, u):
                i, b = j + u, u % 2
                act.wait_ge(ewT_made, i + 1)
                wait(act, sum_made, i - 1)
                s.copy(share[b][:, :, :].rearrange("p k n -> p (k n)"), ps_ewT[b][:, :]).then_inc(ewT_ok, 1)

            steps(act, N, (3, exponentials), (4, evacuate))


def second_layer_out(nc, t, out):
    with ExitStack() as ctx:
        def sb(name, shape, dt=F32):
            return ctx.enter_context(nc.sbuf_tensor(name, shape, dt))

        def ps(name, n=2):
            return [ctx.enter_context(nc.psum_tensor(f"{name}{u}", [P, 4 * P], F32)) for u in range(n)]

        def sem(name):
            return ctx.enter_context(nc.semaphore(name))

        B = QB
        comb, x_beta, stats = sb("comb", [P, NBP, D]), sb("x_beta", [P, NBP, D]), sb("stats2", [P, NBP, 6])
        mean, var, scratch, squares, roots, factor, unit, gain, shift = (sb(f"{x}_out", [P, NBP])[:, :] for x in (
            "mean", "var", "scratch", "squares", "roots", "factor", "unit", "gain", "shift"))
        xT, nT = ([sb(f"{x}{u}", [P, 4 * P]) for u in range(2)] for x in ("x1T", "nT"))
        ps_xT, ps_nT, ps_self, ps_nb = ps("ps_x1T"), ps("ps_nT"), ps("ps_self"), ps("ps_nb")
        (T_made, T_ok, comb_made, nb_added, comb_ok, stats_ok, asked, made, x_beta_ok, centred, y_ok, gain_ok, dve_normal, act_normal,
         out_stored, dve_step) = (sem(x) for x in (
             "T_made", "T_ok", "comb_made", "nb_added", "comb_ok", "stats2_ok", "root2_asked", "root2_made", "x_beta_ok", "centred", "y_ok", "gain_ok",
             "dve_normal2", "act_normal2", "out_stored", "out_step"))
        block = ctx.enter_context(nc.Block())

        @block.gpsimd
        def _(pool):
            for q in range(4):
                rows = slice(q * QB, (q + 1) * QB)
                nc.gpsimd.tensor_tensor(x_beta[:, rows, :], t.x_nodes[:, rows, :], t.gb[:, 1, :][:, None, :].to_broadcast([P, QB, D]), ALU.add).then_inc(x_beta_ok, 1)

        @block.vector
        def _(dve):
            v = nc.vector
            chain = Chain(dve, dve_step)
            sums = t.sums[:, :].rearrange("p (b d) -> p b d", d=MSG)
            for b in range(NBP):
                last = v.bn_stats(stats[:, b, :], sums[:, b, 0:D])
            last.then_inc(stats_ok, 1)
            dve.wait_ge(stats_ok, 1)
            moments(nc, chain, stats, mean, var, scratch)
            norms_squared(nc, chain, scratch, mean, var)
            v.tensor_scalar(squares, scratch, 1.0, None, ALU.mult).then_inc(asked, 1)
            chain.then(v.tensor_scalar(factor, sums[:, :, D], 0.5, EPS, ALU.max, ALU.mult))
            dve.wait_ge(made, 1)
            chain.then(v.tensor_tensor(factor, factor, roots, ALU.add))
            chain.then(v.reciprocal(factor, factor))
            for q in range(B + 1):
                if q < B:
                    dve.wait_ge(comb_made, q + 1)
                    for k in range(4):
                        b = 4 * q + k
                        last = v.tensor_scalar(comb[:, b, :], ps_nb[q % 2][:, k * P:(k + 1) * P], factor[:, b:b + 1], None, ALU.mult)
                    last.then_inc(nb_added, 1)
                    dve.wait_ge(nb_added, q + 1)
                    c = comb[:, 4 * q:4 * q + 4, :].rearrange("p b d -> p (b d)")
                    v.tensor_tensor(c, c, ps_self[q % 2][:, :], ALU.add).then_inc(comb_ok, 1)
                if q >= 1:
                    dve.wait_ge(comb_ok, q)
                    for b in range(4 * (q - 1), 4 * q):
                        last = v.bn_stats(stats[:, b, :], comb[:, b, :])
                    last.then_inc(stats_ok, 1)
            dve.wait_ge(stats_ok, B + 1)
            moments(nc, chain, stats, mean, var, scratch)
            norms_squared(nc, chain, scratch, mean, var)
            v.tensor_scalar(squares, scratch, 1.0, None, ALU.mult).then_inc(asked, 1)
            dve.wait_ge(made, 2)
            chain.then(v.tensor_scalar(unit, roots, 2.0 * EPS, None, ALU.add))
            chain.then(v.reciprocal(unit, unit))
            chain.then(v.tensor_tensor(scratch, unit, unit, ALU.mult))
            chain.then(v.tensor_tensor(scratch, scratch, var, ALU.mult))
            v.tensor_scalar(squares, scratch, LN_EPS, None, ALU.add).then_inc(asked, 1)
            dve.wait_ge(made, 3)
            chain.then(v.reciprocal(gain, roots))
            chain.then(v.tensor_tensor(gain, gain, unit, ALU.mult))
            for q in range(4 + 1):
                if q < 4:
                    for b in range(q * QB, (q + 1) * QB):
                        last = v.scalar_tensor_tensor(comb[:, b, :], comb[:, b, :], mean[:, b:b + 1], t.gb[:, 0, :], ALU.subtract, ALU.mult)
                    last.then_inc(centred, 1)
                    dve.wait_ge(centred, q + 1)
                    dve.wait_ge(x_beta_ok, q + 1)
                    for b in range(q * QB, (q + 1) * QB):
                        last = v.scalar_tensor_tensor(comb[:, b, :], comb[:, b, :], gain[:, b:b + 1], x_beta[:, b, :], ALU.mult, ALU.add)
                    last.then_inc(y_ok, 1)
                if q >= 1:
                    dve.wait_ge(y_ok, q)
                    for b in range((q - 1) * QB, q * QB):
                        last = v.bn_stats(stats[:, b, :], comb[:, b, :])
                    last.then_inc(stats_ok, 1)
            dve.wait_ge(stats_ok, B + 5)
            moments(nc, chain, stats, mean, var, scratch)
            v.tensor_scalar(squares, var, LN_EPS, None, ALU.add).then_inc(asked, 1)
            dve.wait_ge(made, 4)
            chain.then(v.reciprocal(gain, roots))
            v.scalar_tensor_tensor(shift, mean, -1.0, gain, ALU.mult, ALU.mult).then_inc(gain_ok, 1)
            for q in range(4):
                for b in range(q * QB, (q + 1) * QB - ACT_BLOCKS):
                    last = v.tensor_scalar(comb[:, b, :], comb[:, b, :], mean[:, b:b + 1], gain[:, b:b + 1], ALU.subtract, ALU.mult)
                last.then_inc(dve_normal, 1)

        @block.tensor
        def _(pe):
            for q in range(B + 1):
                if q < B:
                    wait(pe, T_ok, 2 * (q - 1))
                    for k in range(4):
                        at, cols = (4 * q + k) * MSG, slice(k * P, (k + 1) * P)
                        nc.tensor.transpose(ps_xT[q % 2][:, cols], t.x_nodes[:, 4 * q + k, :], t.ident[:, :])
                        last = nc.tensor.transpose(ps_nT[q % 2][:, cols], t.sums[:, at:at + D], t.ident[:, :])
                    last.then_inc(T_made, 1)
                if q >= 1:
                    r = q - 1
                    pe.wait_ge(T_ok, 2 * (r + 1))
                    wait(pe, comb_ok, r - 1)
                    for k in range(4):
                        cols = slice(k * P, (k + 1) * P)
                        nc.tensor.matmul(ps_self[r % 2][:, cols], xT[r % 2][:, cols], t.weights[:, 4, :], start=True, stop=False)
                        nc.tensor.matmul(ps_self[r % 2][:, cols], t.ones[0:1, :], t.bself_nb[:, :], start=False, stop=True)
                        last = nc.tensor.matmul(ps_nb[r % 2][:, cols], nT[r % 2][:, cols], t.weights[:, 5, :], start=True, stop=True)
                    last.then_inc(comb_made, 1)

        @block.scalar
        def _(act):
            s = nc.scalar
            for q in range(B):
                act.wait_ge(T_made, q + 1)
                wait(act, comb_made, q - 1)
                s.copy(xT[q % 2][:, :], ps_xT[q % 2][:, :]).then_inc(T_ok, 1)
                s.copy(nT[q % 2][:, :], ps_nT[q % 2][:, :]).then_inc(T_ok, 1)
                if q == 1:
                    square_roots(nc, act, squares, roots, asked, made, 0, 1)
            square_roots(nc, act, squares, roots, asked, made, 1, 3)
            act.wait_ge(gain_ok, 1)
            for q in range(4):
                for b in range((q + 1) * QB - ACT_BLOCKS, (q + 1) * QB):
                    last = s.activation(comb[:, b, :], comb[:, b, :], ACT.Identity, bias=shift[:, b:b + 1], scale=gain[:, b:b + 1])
                last.then_inc(act_normal, 1)

        @block.sync
        def _(sp):
            for q in range(4):
                sp.wait_ge(dve_normal, q + 1)
                sp.wait_ge(act_normal, q + 1)
                sp.dma_start(out[q * QB * P:(q + 1) * QB * P, :].rearrange("(b p) d -> p b d", p=P), comb[:, q * QB:(q + 1) * QB, :]).then_inc(out_stored, 16)
            sp.wait_ge(out_stored, 64)


def build(nc, a, out):
    with ExitStack() as ctx:
        def sb(name, shape, dt=F32):
            return ctx.enter_context(nc.sbuf_tensor(name, shape, dt))

        def dram(name, shape, dt=F32):
            return nc.dram_tensor(name, shape, dt, kind="Internal").ap()

        t = Program()
        t.ticks = ctx.enter_context(nc.semaphore("ticks"))
        t.ones, t.ident, t.before, t.ids = (sb(x, [P, P]) for x in ("ones", "ident", "before", "ids"))
        t.ident16, t.ids16, t.minus_big = (sb(x, [P, P], BF16) for x in ("ident16", "ids16", "minus_big"))
        t.ones_row, t.ones3 = sb("ones_row", [P, COLS], BF16), sb("ones3", [3, P], BF16)
        t.bucket_ids = sb("bucket_ids", [P, NBU + 1])
        t.pool_junk, t.dve_junk = sb("pool_junk", [P, 1]), sb("dve_junk", [P, 2])
        t.w1, t.weights, t.rows = sb("w1", [P, STEP, D]), sb("weights", [P, 6, D]), sb("rows", [1, 4, D])
        t.gb, t.b_o1, t.bo2, t.bself_nb = sb("gb", [P, 2, D]), sb("b_o1", [P, 1]), sb("bo2", [1, D]), sb("bself_nb", [1, D])
        t.b2_rows = sb("b2_rows", [3, STEP, D], BF16)
        t.x_nodes = sb("x_nodes", [P, NBP, D])
        t.window_ids = {"src": sb("window_ids_src", [P, Q4]), "dst": sb("window_ids_dst", [P, Q2])}
        t.window_ints = {"src": sb("window_ints_src", [P, 2, Q4], I32), "dst": sb("window_ints_dst", [P, 3, Q2], I32)}
        t.window_nodes = {"src": sb("window_nodes_src", [P, Q4]), "dst": sb("window_nodes_dst", [P, Q2])}
        t.regs = {"src": sb("regs_src", [1, 2, P * Q4], I32), "dst": sb("regs_dst", [1, 3, P * Q2], I32)}
        t.first = {"src": sb("first_src", [P, P * Q4]), "dst": sb("first_dst", [P, P * Q2])}
        t.ints_dram = {"src": dram("ints_src", [2, P * Q4], I32), "dst": dram("ints_dst", [3, P * Q2], I32)}
        t.nodes_dram = {"src": dram("nodes_src", [P * Q4]), "dst": dram("nodes_dst", [P * Q2])}
        t.b2_dram = dram("b2_parts", [3, D], BF16)
        t.flag = sb("flag", [P, 1], I32)
        t.filters_by_dst, t.meta_by_dst = dram("filters_by_dst", [ET, RBF]), dram("meta_by_dst", [ET, 4])
        t.messages = dram("messages", [ET, MSG])
        t.x1_dram = dram("x1_nodes", [NBP * P, D])
        t.f_ones = sb("f_ones", [P, BODY, STEP, P // STEP])

        with ExitStack() as c1:
            t.h3 = c1.enter_context(nc.sbuf_tensor("h3", [P, NBP, 3, D], BF16))
            with ExitStack() as c2:
                t.meta = c2.enter_context(nc.sbuf_tensor("meta", [P, COLS, 4], F32))
                t.hi_dst = c2.enter_context(nc.sbuf_tensor("hi_dst", [P, COLS], BF16))
                t.base_dst = c2.enter_context(nc.sbuf_tensor("base_dst", [P, NBU + 1], F32))
                prologue(nc, t, a)
                order_by_dst(nc, t, a)
            messages(nc, t)
        t.sums = sb("sums", [P, NBP * MSG])
        sum_messages(nc, t)
        first_layer_out(nc, t)
        attention(nc, t)
        second_layer_out(nc, t, out)


def kernel(x, src, dst, edge_attr_20, edge_weight, L0_gnn_W_in2f, L0_gnn_W_f1, L0_gnn_b_f1, L0_gnn_W_f2, L0_gnn_b_f2,
           L0_gnn_W_o1, L0_gnn_b_o1, L0_gnn_W_o2, L0_gnn_b_o2, L1_gnn_W_self, L1_gnn_b_self, L1_gnn_W_nb, L1_gnn_b_nb,
           L1_gnn_gamma, L1_gnn_beta):
    import numpy as np
    import concourse.bacc as bacc
    from concourse.bass_utils import run_bass_kernel_spmd

    def padded(v, rows, fill=0):
        v = np.asarray(v)
        wide = np.full((rows,) + v.shape[1:], fill, v.dtype)
        wide[:v.shape[0]] = v
        return wide

    arrays = {
        "x": padded(x, NBP * P), "src": padded(src, ET, PAD_NODE), "dst": padded(dst, ET + 1, PAD_NODE),
        "edge_attr": padded(edge_attr_20, ET), "edge_weight": padded(edge_weight, ET),
        "W_in2f": L0_gnn_W_in2f, "W_f1": L0_gnn_W_f1, "b_f1": L0_gnn_b_f1, "W_f2": L0_gnn_W_f2, "b_f2": L0_gnn_b_f2,
        "W_o1": L0_gnn_W_o1, "b_o1": L0_gnn_b_o1, "W_o2": L0_gnn_W_o2, "b_o2": L0_gnn_b_o2,
        "W_self": L1_gnn_W_self, "b_self": L1_gnn_b_self, "W_nb": L1_gnn_W_nb, "b_nb": L1_gnn_b_nb,
        "gamma": L1_gnn_gamma, "beta": L1_gnn_beta,
    }
    arrays = {f"in_{k}": np.ascontiguousarray(v) for k, v in arrays.items()}
    nc = bacc.Bacc("TRN2", target_bir_lowering=False, num_devices=1)
    a = {k[3:]: nc.dram_tensor(k, v.shape, mybir.dt.from_np(v.dtype), kind="ExternalInput").ap() for k, v in arrays.items()}
    out = nc.dram_tensor("out_x", (NBP * P, D), F32, kind="ExternalOutput").ap()
    build(nc, a, out)
    results = run_bass_kernel_spmd(nc, [arrays], core_ids=[0])
    return results.results[0]["out_x"][:NODES]
```

```python
import concourse.bass as bass
from concourse import mybir
from contextlib import ExitStack

F32, BF16, I32, U16 = mybir.dt.float32, mybir.dt.bfloat16, mybir.dt.int32, mybir.dt.uint16
ALU = mybir.AluOpType
ACT = mybir.ActivationFunctionType
AX = mybir.AxisListType

P = 128
NODES, EDGES, D, RBF = 6250, 206250, 128, 20
NBLK = -(-NODES // P)
NBP = 52
COLS = 1616
ET = P * COLS
NBU = NBLK + 1
PAD_NODE = NBLK * P
G2, G4 = 2 * P, 4 * P
BODY = 8
STEP = 4


def windows(rows, unit):
    most = (EDGES - NBLK) // rows + NBLK
    return -(-most // unit) * unit


NW2 = windows(G2, 2)
NW4 = windows(G4, 1)
Q2, Q4 = -(-NW2 // P), -(-NW4 // P)
SKIP = float(1 << 22)
FAR = 1.0e6
LOG2 = 0.6931471805599453
EXP_LN = "natural_log_exp_and_others"
BIG = 2.0 ** 127
LN_EPS, EPS = 1e-5, 1e-9
MSG = D + 1
ROWS_OK = "the tables hold rows clamped to the arrays' length"


class Program:
    pass


class Chain:

    def __init__(self, eng, sem):
        self.eng, self.sem, self.n = eng, sem, 0

    def then(self, instruction):
        instruction.then_inc(self.sem, 1)
        self.n += 1
        self.eng.wait_ge(self.sem, self.n)


def rank_buckets(nc, eng, t, hi, base, pos, masks, runs, sem):
    v = nc.vector
    v.memset(pos, 0.0).then_inc(sem, 1)
    eng.wait_ge(sem, 1)
    with eng.Fori(0, NBU, 2) as b:
        for k in range(2):
            if k == 1:
                eng.wait_ge(sem, 3 * b + 1)
            v.tensor_scalar(masks[k], hi, t.bucket_ids[:, bass.ds(b + k, 1)], None, ALU.is_equal).then_inc(sem, 1)
        for k in range(2):
            eng.wait_ge(sem, 3 * b + (2 + k))
            v.tensor_tensor_scan(runs[k], t.ones_row[:, :], masks[k], base[:, bass.ds(b + k, 1)], ALU.mult, ALU.add).then_inc(sem, 1)
        for k in range(2):
            eng.wait_ge(sem, 3 * b + (4 + k))
            eng.sem_inc(t.ticks, 1)
            if k == 1:
                eng.wait_ge(sem, 3 * b + 6)
                eng.sem_inc(t.ticks, 1)
            v.copy_predicated(pos, masks[k], runs[k]).then_inc(sem, 1)
    eng.wait_ge(sem, 3 * NBU + 1)


def window_tables(nc, chain, sb, t, start, rows, q, tag, scratch):
    shift = rows.bit_length() - 1
    n, ni, ng, gend = (sb(f"{x}_{tag}", [P, NBLK], dt) for x, dt in (("n", F32), ("ni", I32), ("ng", F32), ("gend", F32)))
    a, a2 = sb(f"a_{tag}", [P, NBLK], F32), sb(f"a2_{tag}", [P, NBLK], F32)
    gi, g = sb(f"gi_{tag}", [P, q], I32), t.window_ids[tag]
    cmp_, pick = (scratch[:, k * q * NBLK:(k + 1) * q * NBLK].rearrange("p (q b) -> p q b", q=q) for k in range(2))
    wb, bc, pad, s, s2, b2 = (sb(f"{x}_{tag}", [P, q], F32) for x in ("wb", "bc", "pad", "s", "s2", "b2"))
    ints, first_node = t.window_ints[tag], t.window_nodes[tag]
    v = nc.vector
    chain.then(v.tensor_tensor(n[:, :], start[:, 1:NBLK + 1], start[:, 0:NBLK], ALU.subtract))
    chain.then(v.tensor_scalar(ni[:, :], n[:, :], float(rows - 1), None, ALU.add))
    chain.then(v.tensor_scalar(ni[:, :], ni[:, :], shift, None, ALU.logical_shift_right))
    chain.then(v.tensor_copy(ng[:, :], ni[:, :]))
    chain.then(v.tensor_tensor_scan(gend[:, :], t.ones_row[:, 0:NBLK], ng[:, :], 0.0, ALU.mult, ALU.add))
    chain.then(v.tensor_tensor(a[:, :], ng[:, :], gend[:, :], ALU.subtract))
    chain.then(v.scalar_tensor_tensor(a2[:, :], a[:, :], float(rows), start[:, 0:NBLK], ALU.mult, ALU.add))
    wide = [P, q, NBLK]
    chain.then(v.tensor_tensor(cmp_[:, :, :], gend[:, None, :].to_broadcast(wide), g[:, :, None].to_broadcast(wide), ALU.is_le))
    chain.then(v.tensor_reduce(wb[:, :], cmp_[:, :, :], AX.X, ALU.add))
    chain.then(v.tensor_tensor(cmp_[:, :, :], t.bucket_ids[:, None, 0:NBLK].to_broadcast(wide),
                               wb[:, :, None].to_broadcast(wide), ALU.is_equal))
    chain.then(v.tensor_tensor(pick[:, :, :], cmp_[:, :, :], a2[:, None, :].to_broadcast(wide), ALU.mult))
    chain.then(v.tensor_reduce(s[:, :], pick[:, :, :], AX.X, ALU.add))
    chain.then(v.scalar_tensor_tensor(s2[:, :], g[:, :], float(rows), s[:, :], ALU.mult, ALU.add))
    chain.then(v.tensor_scalar(s[:, :], s2[:, :], float(ET - rows), None, ALU.min))
    chain.then(v.tensor_scalar(pad[:, :], wb[:, :], NBLK - 0.5, -FAR, ALU.is_gt, ALU.mult))
    chain.then(v.tensor_scalar(bc[:, :], wb[:, :], NBLK - 1.0, None, ALU.min))
    chain.then(v.scalar_tensor_tensor(first_node[:, :], bc[:, :], float(P), pad[:, :], ALU.mult, ALU.add))
    for k, scale in enumerate((None, MSG, 3 * D)[:ints.shape[1]]):
        if scale is None:
            chain.then(v.tensor_copy(ints[:, k, :], s[:, :]))
        else:
            chain.then(v.tensor_scalar(ints[:, k, :], bc[:, :], float(scale), None, ALU.mult))


def prologue(nc, t, a):
    with ExitStack() as ctx:
        def sb(name, shape, dt=F32):
            return ctx.enter_context(nc.sbuf_tensor(name, shape, dt))

        def ps(name, shape, dt=F32):
            return ctx.enter_context(nc.psum_tensor(name, shape, dt))

        def sem(name):
            return ctx.enter_context(nc.semaphore(name))

        src_i, dst_i, next_i = sb("src_i", [P, COLS], I32), sb("dst_i", [P, COLS], I32), sb("next_i", [P, COLS], I32)
        weight = sb("weight", [P, COLS])
        hi_i = sb("hi_i", [P, COLS], I32)
        hi_src, hi_dst, hi_next = sb("hi_src", [P, COLS], BF16), t.hi_dst, sb("hi_next", [P, COLS], BF16)
        pos = sb("pos", [P, COLS])
        fell = sb("fell", [P, COLS], BF16)
        fell_n, flag = sb("fell_n", [P, 1]), t.flag
        thresholds, sign_junk = sb("thresholds", [P, NBU + 3]), sb("sign_junk", [P, COLS], BF16)
        signs, signs_src = sb("signs", [P, NBU + 3]), sb("signs_src", [P, NBU + 3])
        SPLIT = 30
        below = {k: sb(f"below_{k}", [P, NBU + 1]) for k in ("src", "dst")}
        count = {k: sb(f"count_{k}", [P, NBU]) for k in ("src", "dst")}
        start = {k: sb(f"start_{k}", [P, NBU + 1]) for k in ("src", "dst")}
        base = {"src": sb("base_src", [P, NBU + 1]), "dst": t.base_dst}
        xT = [sb(f"xT{i}", [P, 4 * P]) for i in range(2)]
        h = [sb(f"h{i}", [P, 4, D]) for i in range(2)]
        rest = sb("rest", [P, 4, D])
        colsum = sb("colsum", [1, 2, D])
        b2row, b2rest, b2rest2, b2part = sb("b2row", [1, D]), sb("b2rest", [1, D]), sb("b2rest2", [1, D]), sb("b2part", [1, 3, D], BF16)
        zero_rows = sb("zero_rows", [P, 5 * MSG])
        psT, psH = [ps(f"psT{i}", [P, 4 * P]) for i in range(2)], [ps(f"psH{i}", [P, 4, D]) for i in range(2)]
        ps_tot = {k: ps(f"ps_tot_{k}", [P, 2, 64]) for k in ("src", "dst")}
        ps_small, ps_fell = ps("ps_small", [P, 4, D]), ps("ps_fell", [P, 4 * D])

        loaded = {k: sem(f"loaded_{k}") for k in ("x", "src", "dst", "w", "weights", "b2", "tables")}
        stored, tail_stored = sem("stored"), sem("tail_stored")
        consts_made, pool_step = sem("consts_made"), sem("pool_step")
        hi_ready, below_step, totals_in, below_ready, bases_ready = (sem(x) for x in ("hi_ready", "below_step", "totals_in", "below_ready", "bases_ready"))
        dve_step, rank_step, meta_ready, tables_ready = (sem(x) for x in ("dve_step", "rank_step", "meta_ready", "tables_ready"))
        xT_made, xT_copied, h_made, h_copied, h_split, pool_h = (sem(x) for x in ("xT_made", "xT_copied", "h_made", "h_copied", "h_split", "pool_h"))
        small_made, b2_ready, b2_stored, sign_step = sem("small_made"), sem("b2_ready"), sem("b2_stored"), sem("sign_step")
        block = ctx.enter_context(nc.Block())

        @block.sync
        def _(sp):
            flat = lambda x: x[0:ET].rearrange("(p c) -> p c", p=P)
            sp.dma_start(src_i[:, :], flat(a["src"])).then_inc(loaded["src"], 16)
            sp.dma_start(dst_i[:, :], flat(a["dst"])).then_inc(loaded["dst"], 16)
            sp.dma_start(next_i[:, :], a["dst"][1:ET + 1].rearrange("(p c) -> p c", p=P)).then_inc(loaded["dst"], 16)
            sp.dma_start(weight[:, :], flat(a["edge_weight"])).then_inc(loaded["w"], 16)
            for b in range(0, NBP, NBP // 4):
                sp.dma_start(t.x_nodes[:, b:b + NBP // 4, :], a["x"][b * P:(b + NBP // 4) * P, :].rearrange("(b p) d -> p b d", p=P)).then_inc(loaded["x"], 16)
            sp.dma_start(t.filters_by_dst.rearrange("(p c) f -> p (c f)", p=P), a["edge_attr"].rearrange("(p c) f -> p (c f)", p=P)).then_inc(stored, 16)
            for n, (tag, nw) in enumerate((("src", NW4), ("dst", NW2))):
                if tag == "dst":
                    sp.wait_ge(meta_ready, 1)
                    sp.dma_start(t.meta_by_dst.rearrange("(p c) k -> p (c k)", p=P), t.meta[:, :, :].rearrange("p c k -> p (c k)")).then_inc(stored, 16)
                sp.wait_ge(tables_ready, n + 1)
                q = t.window_ids[tag].shape[1]
                for k in range(n + 2):
                    sp.dma_start(t.ints_dram[tag][k, :].rearrange("(p q) -> p q", p=P), t.window_ints[tag][:, k, :]).then_inc(loaded["tables"], 16)
                sp.dma_start(t.nodes_dram[tag].rearrange("(p q) -> p q", p=P), t.window_nodes[tag][:, :]).then_inc(loaded["tables"], 16)
                sp.wait_ge(loaded["tables"], n * 96 + 16 * (n + 3))
                for k in range(n + 2):
                    sp.dma_start(t.regs[tag][0:1, k, :], t.ints_dram[tag][k:k + 1, :]).then_inc(loaded["tables"], 16)
                sp.dma_start(t.first[tag][:, :], t.nodes_dram[tag][None, :].to_broadcast([P, q * P])).then_inc(loaded["tables"], 16)
                sp.wait_ge(loaded["tables"], n * 96 + 32 * (n + 3))
            sp.wait_ge(b2_ready, 1)
            sp.dma_start(t.b2_dram.rearrange("(a k) d -> a k d", a=1), b2part[:, :, :]).then_inc(b2_stored, 16)
            sp.wait_ge(b2_stored, 16)
            for k in range(STEP):
                sp.dma_start(t.b2_rows[:, k, :], t.b2_dram).then_inc(b2_stored, 16)
            sp.wait_ge(b2_stored, 80)
            sp.wait_ge(stored, 32)

        @block.gpsimd
        def _(pool):
            g = nc.gpsimd
            g.memset(t.ones[:, :], 1.0).then_inc(pool_step, 1)
            g.memset(t.ones_row[:, :], 1.0).then_inc(pool_step, 1)
            g.memset(t.ones3[:, :], 1.0).then_inc(pool_step, 1)
            g.memset(zero_rows[:, :], 0.0).then_inc(pool_step, 1)
            pool.wait_ge(pool_step, 4)
            g.affine_select(out=t.ident[:, :], in_=t.ones[:, :], compare_op=ALU.is_equal, fill=0.0, base=0,
                            pattern=[[-1, P]], channel_multiplier=1).then_inc(pool_step, 1)
            g.affine_select(out=t.before[:, :], in_=t.ones[:, :], compare_op=ALU.is_gt, fill=0.0, base=0,
                            pattern=[[1, P]], channel_multiplier=-1).then_inc(pool_step, 1)
            g.iota(t.ids[:, :], pattern=[[1, P]], base=0, channel_multiplier=0,
                   allow_small_or_imprecise_dtypes=True).then_inc(pool_step, 1)
            g.iota(t.bucket_ids[:, :], pattern=[[1, NBU + 1]], base=0, channel_multiplier=0,
                   allow_small_or_imprecise_dtypes=True).then_inc(pool_step, 1)
            for tag, q in (("src", Q4), ("dst", Q2)):
                g.iota(t.window_ids[tag][:, :], pattern=[[1, q]], base=0, channel_multiplier=q,
                       allow_small_or_imprecise_dtypes=True).then_inc(pool_step, 1)
            pool.wait_ge(pool_step, 10)
            g.tensor_scalar(thresholds[:, 0:NBU + 1], t.bucket_ids[:, :], -1.0, 0.5, ALU.mult, ALU.add).then_inc(pool_step, 1)
            g.tensor_copy(t.ident16[:, :], t.ident[:, :]).then_inc(pool_step, 1)
            g.tensor_copy(t.ids16[:, :], t.ids[:, :]).then_inc(pool_step, 1)
            g.tensor_scalar(t.minus_big[:, :], t.ident[:, :], -BIG, 0.0, ALU.mult, ALU.add).then_inc(pool_step, 1)
            pool.wait_ge(pool_step, 14)
            g.memset(t.f_ones[:, :, :, :], 1.0).then_inc(consts_made, 1)
            g.memset(t.w1[:, :, :], 0.0).then_inc(consts_made, 1)
            pool.wait_ge(consts_made, 2)
            for k in range(STEP):
                row = k * (P // STEP)
                pool.dma_start(t.w1[row:row + RBF, k, :], a["W_f1"]).then_inc(loaded["weights"], 16)
                pool.dma_start(t.w1[row + RBF:row + RBF + 1, k, :], a["b_f1"][None, :]).then_inc(loaded["weights"], 16)
            for k, w in enumerate((a["W_in2f"], a["W_f2"], a["W_o1"], a["W_o2"], a["W_self"], a["W_nb"])):
                pool.dma_start(t.weights[:, k, :], w).then_inc(loaded["weights"], 16)
            for k, v in enumerate((a["b_f2"], a["b_o2"])):
                pool.dma_start(t.rows[:, k, :], v[None, :]).then_inc(loaded["weights"], 16)
            for k, v in enumerate((a["gamma"], a["beta"], a["b_self"], a["b_nb"])):
                pool.dma_start(t.gb[:, k, :], v[None, :].to_broadcast([P, D])).then_inc(loaded["weights"], 16)
            pool.dma_start(t.b_o1[:, :], a["b_o1"][:, None]).then_inc(loaded["weights"], 16)
            n_tail = ET - EDGES
            head = n_tail // P * P
            pool.dma_start(t.messages[EDGES:EDGES + head, :].rearrange("(p k) d -> p (k d)", p=P), zero_rows[:, 0:head // P * MSG]).then_inc(tail_stored, 16)
            pool.dma_start(t.messages[EDGES + head:ET, :], zero_rows[0:n_tail - head, 0:MSG]).then_inc(tail_stored, 16)
            for q in range(NBP // 4):
                pool.wait_ge(h_copied, q + 1)
                hq, part = h[q % 2][:, :, :], lambda k: t.h3[:, 4 * q:4 * q + 4, k, :]
                g.tensor_copy(part(0), hq).then_inc(pool_h, 1)
                pool.wait_ge(pool_h, 5 * q + 1)
                g.tensor_tensor(rest[:, :, :], hq, part(0), ALU.subtract).then_inc(pool_h, 1)
                pool.wait_ge(pool_h, 5 * q + 2)
                g.tensor_copy(part(1), rest[:, :, :]).then_inc(pool_h, 1)
                pool.wait_ge(pool_h, 5 * q + 3)
                g.tensor_tensor(part(2), rest[:, :, :], part(1), ALU.subtract).then_inc(pool_h, 1)
                pool.wait_ge(pool_h, 5 * q + 4)
                g.memset(t.pool_junk[:, :], 0.0).then_inc(pool_h, 1)
                pool.wait_ge(pool_h, 5 * q + 5)
                pool.sem_inc(h_split, 1)
            pool.wait_ge(tail_stored, 32)
            pool.wait_ge(loaded["weights"], 21 * 16)

        @block.scalar
        def _(act):
            act.preload_act_table_set(EXP_LN)
            act.wait_ge(pool_step, 14)
            act.wait_ge(hi_ready, 1)
            with act.Fori(SPLIT, NBU + 1, 3) as b:
                for k in range(3):
                    last = nc.scalar.activation(sign_junk[:, :], hi_src[:, :], ACT.Sign, bias=thresholds[:, bass.ds(b + k, 1)],
                                                accum_out=signs_src[:, bass.ds(b + k, 1)])
                    last.then_inc(sign_step, 1)
                    act.wait_ge(sign_step, b + (k + 1 - SPLIT))
            for q in range(NBP // 4):
                act.wait_ge(xT_made, q + 1)
                if q >= 2:
                    act.wait_ge(h_made, q - 1)
                nc.scalar.copy(xT[q % 2][:, :], psT[q % 2][:, :]).then_inc(xT_copied, 1)
                act.wait_ge(h_made, q + 1)
                if q >= 2:
                    act.wait_ge(h_split, q - 1)
                nc.scalar.copy(h[q % 2][:, :, :], psH[q % 2][:, :, :]).then_inc(h_copied, 1)
            act.wait_ge(hi_ready, 2)
            with act.Fori(0, NBU + 1) as b:
                nc.scalar.activation(sign_junk[:, :], hi_dst[:, :], ACT.Sign, bias=thresholds[:, bass.ds(b, 1)],
                                     accum_out=signs[:, bass.ds(b, 1)]).then_inc(sign_step, 1)
                act.wait_ge(sign_step, b + (NBU + 2 - SPLIT))

        @block.tensor
        def _(pe):
            def totals(n, key):
                pe.wait_ge(below_ready, n + 1)
                nc.tensor.matmul(ps_tot[key][:, 0, 0:NBU + 1], t.ones[:, :], below[key][:, :], start=True, stop=True)
                nc.tensor.matmul(ps_tot[key][:, 1, 0:NBU], t.before[:, :], count[key][:, :], start=True, stop=True).then_inc(totals_in, 1)

            pe.wait_ge(pool_step, 14)
            totals(0, "src")
            pe.wait_ge(loaded["weights"], 21 * 16)
            nc.tensor.matmul(ps_small[0:1, 0, :], t.ones[:, 0:1], t.weights[:, 1, :], start=True, stop=True)
            nc.tensor.matmul(ps_small[0:1, 1, :], t.ones[:, 0:1], t.weights[:, 3, :], start=True, stop=True).then_inc(small_made, 1)
            pe.wait_ge(loaded["x"], 64)
            for q in range(NBP // 4):
                if q >= 2:
                    pe.wait_ge(xT_copied, q - 1)
                for k in range(4):
                    last = nc.tensor.transpose(psT[q % 2][:, k * P:(k + 1) * P], t.x_nodes[:, 4 * q + k, :], t.ident[:, :])
                last.then_inc(xT_made, 1)
                pe.wait_ge(xT_copied, q + 1)
                if q >= 2:
                    pe.wait_ge(h_copied, q - 1)
                for k in range(4):
                    last = nc.tensor.matmul(psH[q % 2][:, k, :], xT[q % 2][:, k * P:(k + 1) * P], t.weights[:, 0, :], start=True, stop=True)
                last.then_inc(h_made, 1)
            totals(1, "dst")
            pe.wait_ge(meta_ready, 1)
            nc.tensor.matmul(ps_fell[:, 0:1], t.ones[:, :], fell_n[:, :], start=True, stop=True).then_inc(small_made, 1)

        @block.vector
        def _(dve):
            chain = Chain(dve, dve_step)
            v = nc.vector
            dve.wait_ge(loaded["src"], 16)
            chain.then(v.tensor_scalar(hi_i[:, :], src_i[:, :], 7, None, ALU.logical_shift_right))
            v.tensor_copy(hi_src[:, :], hi_i[:, :]).then_inc(hi_ready, 1)
            dve.wait_ge(hi_ready, 1)
            dve.wait_ge(loaded["dst"], 32)
            chain.then(v.tensor_scalar(hi_i[:, :], dst_i[:, :], 7, None, ALU.logical_shift_right))
            v.tensor_copy(hi_dst[:, :], hi_i[:, :]).then_inc(hi_ready, 1)
            dve.wait_ge(hi_ready, 2)
            chain.then(v.tensor_scalar(hi_i[:, :], next_i[:, :], 7, None, ALU.logical_shift_right))
            chain.then(v.tensor_copy(hi_next[:, :], hi_i[:, :]))
            chain.then(v.tensor_tensor(fell[:, :], hi_dst[:, :], hi_next[:, :], ALU.is_gt))
            chain.then(v.tensor_reduce(fell_n[:, :], fell[:, :], AX.X, ALU.add))
            dve.wait_ge(loaded["w"], 16)
            chain.then(v.tensor_copy(t.meta[:, :, 0], weight[:, :]))
            chain.then(v.tensor_copy(t.meta[:, :, 1], src_i[:, :]))
            chain.then(v.tensor_copy(t.meta[:, :, 2], dst_i[:, :]))
            dve.wait_ge(pool_step, 14)

            def places(n, key):
                v.tensor_tensor(count[key][:, :], below[key][:, 1:NBU + 1], below[key][:, 0:NBU], ALU.subtract).then_inc(below_ready, 1)
                dve.wait_ge(totals_in, n + 1)
                chain.then(v.tensor_copy(start[key][:, :], ps_tot[key][:, 0, 0:NBU + 1]))
                chain.then(v.tensor_tensor(base[key][:, 0:NBU], start[key][:, 0:NBU], ps_tot[key][:, 1, 0:NBU], ALU.add))

            with dve.Fori(0, SPLIT, 3) as b:
                for k in range(3):
                    v.tensor_scalar(fell[:, :], hi_src[:, :], t.bucket_ids[:, bass.ds(b + k, 1)], 0.0, ALU.is_lt, ALU.add,
                                    accum_out=below["src"][:, bass.ds(b + k, 1)]).then_inc(below_step, 1)
                    dve.wait_ge(below_step, b + (k + 1))
            dve.wait_ge(sign_step, NBU + 1 - SPLIT)
            chain.then(v.tensor_scalar(below["src"][:, SPLIT:NBU + 1], signs_src[:, SPLIT:NBU + 1], -0.5, COLS / 2.0, ALU.mult, ALU.add))
            places(0, "src")
            window_tables(nc, chain, sb, t, start["src"], G4, Q4, "src", weight)
            v.memset(t.dve_junk[:, 0:1], 0.0).then_inc(tables_ready, 1)
            rank_buckets(nc, dve, t, hi_src[:, :], base["src"], pos[:, :], [fell[:, :].bitcast(U16), hi_next[:, :].bitcast(U16)],
                         [next_i[:, :].bitcast(F32), hi_i[:, :].bitcast(F32)], rank_step)
            v.tensor_scalar(t.meta[:, :, 3], pos[:, :], -1.0, None, ALU.add).then_inc(meta_ready, 1)
            dve.wait_ge(sign_step, 2 * (NBU + 1) - SPLIT)
            chain.then(v.tensor_scalar(below["dst"][:, :], signs[:, 0:NBU + 1], -0.5, COLS / 2.0, ALU.mult, ALU.add))
            places(1, "dst")
            window_tables(nc, chain, sb, t, start["dst"], G2, Q2, "dst", weight)
            v.memset(t.dve_junk[:, 1:2], 0.0).then_inc(tables_ready, 1)
            dve.wait_ge(small_made, 1)
            chain.then(v.scalar_tensor_tensor(b2row[:, :], ps_small[0:1, 0, :], -LOG2, t.rows[:, 0, :], ALU.mult, ALU.add))
            chain.then(v.scalar_tensor_tensor(t.bo2[:, :], ps_small[0:1, 1, :], -LOG2, t.rows[:, 1, :], ALU.mult, ALU.add))
            chain.then(v.tensor_tensor(t.b_comb[:, :], t.gb[:, 2, :], t.gb[:, 3, :], ALU.add))
            chain.then(v.tensor_copy(b2part[:, 0, :], b2row[:, :]))
            chain.then(v.tensor_tensor(b2rest[:, :], b2row[:, :], b2part[:, 0, :], ALU.subtract))
            chain.then(v.tensor_copy(b2part[:, 1, :], b2rest[:, :]))
            v.tensor_tensor(b2part[:, 2, :], b2rest[:, :], b2part[:, 1, :], ALU.subtract).then_inc(b2_ready, 1)
            dve.wait_ge(small_made, 2)
            v.tensor_copy(flag[:, :], ps_fell[:, 0:1]).then_inc(dve_step, 1)


def order_by_dst(nc, t, a):
    with ExitStack() as ctx:
        def sb(name, shape, dt=F32):
            return ctx.enter_context(nc.sbuf_tensor(name, shape, dt))

        def sem(name):
            return ctx.enter_context(nc.semaphore(name))

        pos, place = sb("pos_dst", [P, COLS]), sb("place", [P, COLS], I32)
        masks, runs = [sb(f"mask{k}", [P, COLS], U16) for k in range(2)], [sb(f"run{k}", [P, COLS]) for k in range(2)]
        GROUP = 16
        place16, meta16 = sb("place16", [P, GROUP], I32), sb("meta16", [P, GROUP, 4])
        filt16 = sb("filt16", [P, GROUP, RBF])
        ranked, placed, taken, moved, filt_in = (sem(x) for x in ("ranked", "placed", "taken", "moved", "filt_in"))
        block = ctx.enter_context(nc.Block())

        @block.vector
        def _(dve):
            unordered = dve.value_load(t.flag[0:1, 0:1], min_val=0, max_val=ET)
            with dve.If(unordered > 0):
                rank_buckets(nc, dve, t, t.hi_dst[:, :], t.base_dst, pos[:, :], [m[:, :] for m in masks], [r[:, :] for r in runs], ranked)
                nc.vector.tensor_scalar(place[:, :], pos[:, :], -1.0, None, ALU.add).then_inc(placed, 1)
                dve.wait_ge(placed, 1)
            dve.nop()

        @block.gpsimd
        def _(pool):
            unordered = pool.value_load(t.flag[0:1, 0:1], min_val=0, max_val=ET)
            with pool.If(unordered > 0):
                g = nc.gpsimd
                pool.wait_ge(placed, 1)
                with pool.Fori(0, COLS // GROUP) as j:
                    src = a["edge_attr"].rearrange("(p c) f -> p c f", p=P)
                    pool.dma_start(filt16[:, :, :], src[:, bass.ds(j * GROUP, GROUP), :]).then_inc(filt_in, 16)
                    g.tensor_copy(place16[:, :], place[:, bass.ds(j * GROUP, GROUP)]).then_inc(taken, 1)
                    g.tensor_copy(meta16[:, :, :], t.meta[:, bass.ds(j * GROUP, GROUP), :]).then_inc(taken, 1)
                    pool.wait_ge(taken, 2 * j + 2)
                    pool.sem_inc(t.ticks, 1)
                    pool.wait_ge(filt_in, 16 * j + 16)
                    pool.sem_inc(t.ticks, 1)
                    for c in range(GROUP):
                        to = bass.IndirectOffsetOnAxis(ap=place16[:, c:c + 1], axis=0)
                        pool.indirect_dma_start(t.meta_by_dst, to, meta16[:, c, :], None).then_inc(moved, 16)
                        pool.indirect_dma_start(t.filters_by_dst, to, filt16[:, c, :], None).then_inc(moved, 16)
                    pool.wait_ge(moved, 32 * GROUP * j + 32 * GROUP)
                    pool.sem_inc(t.ticks, 1)
            pool.nop()


def steps(eng, n, *stages):
    def step(j, u):
        for lag, stage in stages:
            back = -(-(lag - u) // BODY) if lag > u else 0
            j0, u0 = j - BODY * back, u - lag + BODY * back
            if isinstance(j0, int) and not 0 <= j0 + u0 < n:
                continue
            stage(j0, u0)

    most = max(lag for lag, _ in stages)
    first, last = BODY - (-most // BODY) * BODY, n - n % BODY
    for j in range(0, first, BODY):
        for u in range(BODY):
            step(j, u)
    with eng.Fori(first, last, BODY) as j:
        for u in range(BODY):
            step(j, u)
    for i in range(last, n + most):
        step(i // BODY * BODY, i % BODY)


def wait(eng, sem, value):
    if not isinstance(value, int) or value > 0:
        eng.wait_ge(sem, value)


def rounds(j, back, n):
    return j * (16 * n // BODY) + 16 * n * (1 - back)


def uses(n, u):
    return (n - u + BODY - 1) // BODY


def load_rows(nc, sp, tab, row, first, n, most):
    _, values = nc.values_load_multi_w_load_instructions(tab[0:1, row, bass.ds(first, n)], engines=[sp.engine], min_val=0,
                                                         max_val=most, skip_runtime_bounds_check_because=ROWS_OK)
    return values


def messages(nc, t):
    with ExitStack() as ctx:
        def sb(name, shape, dt=F32):
            return ctx.enter_context(nc.sbuf_tensor(name, shape, dt))

        def ps(name, shape, dt=F32):
            return ctx.enter_context(nc.psum_tensor(name, shape, dt))

        def sem(name):
            return ctx.enter_context(nc.semaphore(name))

        W, K = STEP // 2, 2
        N = NW2 // W
        meta = [sb(f"meta{u}", [P, STEP, 4]) for u in range(BODY)]
        filt = t.f_ones
        place = [sb(f"place{u}", [P, STEP], I32) for u in range(BODY)]
        local, outside = [sb(f"local{u}", [P, STEP]) for u in range(2)], [sb(f"outside{u}", [P, STEP]) for u in range(2)]
        member = [sb(f"member{u}", [P, STEP, P], BF16) for u in range(2)]
        filtT = [sb(f"filtT{u}", [P, P]) for u in range(2)]
        memberT = [sb(f"memberT{u}", [P, STEP, P], BF16) for u in range(2)]
        mag, grown, soft, act1 = ([sb(f"{x}{u}", [P, STEP * P]) for u in range(2)] for x in ("mag", "grown", "soft", "act1"))
        hdst = [sb(f"hdst{u}", [P, STEP, D]) for u in range(2)]
        msg = [sb(f"msg{u}", [P, STEP, MSG]) for u in range(BODY)]
        ps_filtT, ps_memberT = ps("ps_filtT", [P, STEP * P]), ps("ps_memberT", [P, 2 * STEP, P], BF16)
        ps_pre, ps_filter, ps_hdst = ([ps(f"{x}{u}", [P, STEP, P]) for u in range(2)] for x in ("ps_pre", "ps_filter", "ps_hdst"))

        loaded, scattered = [sem(f"loaded{u}") for u in range(BODY)], [sem(f"scattered{u}") for u in range(BODY)]
        (local_ok, outside_ok, member_ok, place_ok, filtT_made, memberT_made, filtT_ok, memberT_ok, pre_made, hdst_made,
         mag_ok, grown_ok, soft_ok, hdst_ok, act1_ok, filter_made, msg_ok) = (sem(x) for x in (
             "local_ok", "outside_ok", "member_ok", "place_ok", "filtT_made", "memberT_made", "filtT_ok", "memberT_ok", "pre_made",
             "hdst_made", "mag_ok", "grown_ok", "soft_ok", "hdst_ok", "act1_ok", "filter_made", "msg_ok"))
        block = ctx.enter_context(nc.Block())

        @block.sync
        def _(sp):
            def load(j, u):
                i = j + u
                wait(sp, filtT_made, i - BODY + 1)
                wait(sp, msg_ok, i - BODY + 1)
                for w, row in enumerate(load_rows(nc, sp, t.regs["dst"], 0, W * i, W, ET - G2)):
                    sp.dma_start(filt[:, u, K * w:K * w + K, 0:RBF], t.filters_by_dst[bass.ds(row, G2), :].rearrange("(p k) f -> p k f", p=P)).then_inc(loaded[u], 16)
                    sp.dma_start(meta[u][:, K * w:K * w + K, :], t.meta_by_dst[bass.ds(row, G2), :].rearrange("(p k) f -> p k f", p=P)).then_inc(loaded[u], 16)

            steps(sp, N, (0, load))

        @block.vector
        def _(dve):
            v = nc.vector

            def classify(j, u):
                i, b = j + u, u % 2
                dve.wait_ge(loaded[u], rounds(j, 0, 2 * W))
                v.tensor_tensor(local[b][:, :].rearrange("p (w k) -> p w k", w=W), meta[u][:, :, 2].rearrange("p (w k) -> p w k", w=W),
                                t.first["dst"][:, bass.ds(W * i, W)][:, :, None].to_broadcast([P, W, K]), ALU.subtract).then_inc(local_ok, 1)
                dve.wait_ge(local_ok, i + 1)
                wait(dve, memberT_made, i - 1)
                for k in range(STEP):
                    last = v.tensor_scalar(member[b][:, k, :], t.ids16[:, :], local[b][:, k:k + 1], None, ALU.is_equal)
                last.then_inc(member_ok, 1)
                v.tensor_scalar(outside[b][:, :], local[b][:, :], P - 0.5, SKIP, ALU.is_gt, ALU.mult).then_inc(outside_ok, 1)
                dve.wait_ge(outside_ok, i + 1)
                wait(dve, scattered[u], rounds(j, 1, STEP))
                v.tensor_tensor(place[u][:, :], outside[b][:, :], meta[u][:, :, 3], ALU.add).then_inc(place_ok, 1)

            def softplus(j, u):
                i, b = j + u, u % 2
                dve.wait_ge(soft_ok, i + 1)
                wait(dve, filter_made, i - 1)
                v.scalar_tensor_tensor(act1[b][:, :], ps_pre[b][:, :, :].rearrange("p k e -> p (k e)"), 0.0, soft[b][:, :], ALU.max, ALU.add).then_inc(act1_ok, 1)

            def product(j, u):
                i, b = j + u, u % 2
                dve.wait_ge(filter_made, i + 1)
                dve.wait_ge(hdst_ok, i + 1)
                wait(dve, scattered[u], rounds(j, 1, STEP))
                for k in range(STEP):
                    v.scalar_tensor_tensor(msg[u][:, k, 0:D], ps_filter[b][:, k, :], meta[u][:, k, 0:1], hdst[b][:, k, :], ALU.mult, ALU.mult)
                v.tensor_copy(msg[u][:, :, D], meta[u][:, :, 1]).then_inc(msg_ok, 1)

            steps(dve, N, (0, classify), (4, product), (3, softplus))

        @block.tensor
        def _(pe):
            def transposes(j, u):
                i, b = j + u, u % 2
                pe.wait_ge(loaded[u], rounds(j, 0, 2 * W))
                wait(pe, filtT_ok, i)
                nc.tensor.transpose(ps_filtT[:, 0:P], filt[:, u, :, :], t.ident[:, :]).then_inc(filtT_made, 1)
                pe.wait_ge(member_ok, i + 1)
                wait(pe, memberT_ok, i)
                for k in range(STEP):
                    last = nc.tensor.transpose(ps_memberT[:, k, :], member[b][:, k, :], t.ident16[:, :])
                last.then_inc(memberT_made, 1)

            def first_filter(j, u):
                i, b = j + u, u % 2
                pe.wait_ge(filtT_ok, i + 1)
                wait(pe, act1_ok, i - 1)
                for k in range(STEP):
                    last = nc.tensor.matmul(ps_pre[b][:, k, :], t.w1[:, k, :], filtT[b][:, :], start=True, stop=True)
                last.then_inc(pre_made, 1)
                pe.wait_ge(memberT_ok, i + 1)
                wait(pe, hdst_ok, i - 1)
                blocks = load_rows(nc, pe, t.regs["dst"], 2, W * i, W, (NBLK - 1) * 3 * D)
                table = t.h3[:, :, :, :].rearrange("p b k d -> p (b k d)")
                for k in range(STEP):
                    for part in range(3):
                        last = nc.tensor.matmul(ps_hdst[b][:, k, :], memberT[b][:, k, :], table[:, bass.ds(blocks[k // K] + part * D, D)],
                                                start=(part == 0), stop=(part == 2))
                last.then_inc(hdst_made, 1)

            def second_filter(j, u):
                i, b = j + u, u % 2
                wait(pe, msg_ok, i - 1)
                nc.tensor.matmul(ps_filter[b][:, :, :], t.ones3[:, :], t.b2_rows[:, :, :], start=True, stop=False, skip_group_check=True)
                pe.wait_ge(act1_ok, i + 1)
                for k in range(STEP):
                    last = nc.tensor.matmul(ps_filter[b][:, k, :], act1[b][:, k * P:(k + 1) * P], t.weights[:, 1, :],
                                            start=False, stop=True, skip_group_check=True)
                last.then_inc(filter_made, 1)

            steps(pe, N, (4, second_filter), (1, transposes), (2, first_filter))

        @block.scalar
        def _(act):
            s = nc.scalar
            act.preload_act_table_set(EXP_LN)

            def copy_filters(j, u):
                i, b = j + u, u % 2
                act.wait_ge(filtT_made, i + 1)
                wait(act, pre_made, i - 1)
                s.copy(filtT[b][:, :], ps_filtT[:, 0:P]).then_inc(filtT_ok, 1)

            def copy_members(j, u):
                i, b = j + u, u % 2
                act.wait_ge(memberT_made, i + 1)
                wait(act, hdst_made, i - 1)
                s.copy(memberT[b][:, :, :], ps_memberT[:, 0:STEP, :]).then_inc(memberT_ok, 1)

            def magnitude(j, u):
                i, b = j + u, u % 2
                act.wait_ge(pre_made, i + 1)
                wait(act, grown_ok, i - 1)
                s.activation(mag[b][:, :], ps_pre[b][:, :, :].rearrange("p k e -> p (k e)"), ACT.Abs).then_inc(mag_ok, 1)

            def exponential(j, u):
                i, b = j + u, u % 2
                act.wait_ge(mag_ok, i + 1)
                s.activation(grown[b][:, :], mag[b][:, :], ACT.Exp, scale=-1.0).then_inc(grown_ok, 1)

            def copy_hdst(j, u):
                i, b = j + u, u % 2
                act.wait_ge(hdst_made, i + 1)
                wait(act, msg_ok, i - 1)
                s.copy(hdst[b][:, :, :], ps_hdst[b][:, :, :]).then_inc(hdst_ok, 1)

            def logarithm(j, u):
                i, b = j + u, u % 2
                act.wait_ge(grown_ok, i + 1)
                wait(act, act1_ok, i - 1)
                s.activation(soft[b][:, :], grown[b][:, :], ACT.Ln, bias=1.0).then_inc(soft_ok, 1)

            steps(act, N, (3, magnitude), (1, copy_filters), (3, exponential), (3, copy_hdst), (3, logarithm), (1, copy_members))

        @block.gpsimd
        def _(pool):
            def scatter(j, u):
                i = j + u
                pool.wait_ge(msg_ok, i + 1)
                pool.sem_inc(t.ticks, 1)
                for k in range(STEP):
                    pool.indirect_dma_start(t.messages, bass.IndirectOffsetOnAxis(ap=place[u][:, k:k + 1], axis=0), msg[u][:, k, :], None,
                                            bounds_check=ET - 1, oob_is_err=False).then_inc(scattered[u], 16)

            steps(pool, N, (0, scatter))
            for u in range(BODY):
                pool.wait_ge(scattered[u], 16 * STEP * uses(N, u))


def sum_messages(nc, t):
    with ExitStack() as ctx:
        def sb(name, shape, dt=F32):
            return ctx.enter_context(nc.sbuf_tensor(name, shape, dt))

        def sem(name):
            return ctx.enter_context(nc.semaphore(name))

        msg = [sb(f"msg_in{u}", [P, STEP, MSG]) for u in range(BODY)]
        B = 4
        local, member, apart = [sb(f"local_src{u}", [P, STEP]) for u in range(B)], [sb(f"member_src{u}", [P, STEP, P]) for u in range(B)], [sb(f"apart{u}", [P, P]) for u in range(2)]
        ps_sum = [ctx.enter_context(nc.psum_tensor(f"ps_sum{u}", [P, 4 * P], F32)) for u in range(B)]
        loaded = [sem(f"msg_loaded{u}") for u in range(BODY)]
        cleared, local_ok, member_ok, apart_ok, member_act_ok, sum_made, sum_added = (sem(x) for x in (
            "cleared", "local_src_ok", "member_src_ok", "apart_ok", "member_act_ok", "sum_made", "sum_added"))
        block = ctx.enter_context(nc.Block())

        @block.sync
        def _(sp):
            def load(j, u):
                i = j + u
                wait(sp, sum_made, i - BODY + 1)
                row, = load_rows(nc, sp, t.regs["src"], 0, i, 1, ET - G4)
                sp.dma_start(msg[u][:, :, :].rearrange("p k d -> p (k d)"), t.messages[bass.ds(row, G4), :].rearrange("(p k) d -> p (k d)", p=P)).then_inc(loaded[u], 16)

            steps(sp, NW4, (0, load))

        @block.vector
        def _(dve):
            v = nc.vector

            pair = [None, None]

            def locate(j, u):
                i, b = j + u, u % B
                dve.wait_ge(loaded[u], rounds(j, 0, 1))
                wait(dve, sum_made, i - B + 1)
                v.tensor_tensor(local[b][:, :], msg[u][:, :, D], t.first["src"][:, bass.ds(i, 1)].to_broadcast([P, STEP]), ALU.subtract).then_inc(local_ok, 1)

            def classify(j, u):
                i, b = j + u, u % B
                dve.wait_ge(local_ok, i + 1)
                wide = [P, STEP - 1, P]
                v.tensor_tensor(member[b][:, 0:STEP - 1, :], t.ids16[:, None, :].to_broadcast(wide), local[b][:, 0:STEP - 1, None].to_broadcast(wide),
                                ALU.is_equal).then_inc(member_ok, 1)

            def add(j, u):
                i, b = j + u, u % B
                if u % 2 == 0:
                    pair[:] = load_rows(nc, dve, t.regs["src"], 1, i, 2, (NBLK - 1) * MSG)
                at = pair[u % 2]
                dve.wait_ge(sum_made, i + 1)
                wait(dve, sum_added, i)
                v.tensor_tensor(t.sums[:, bass.ds(at, D)], t.sums[:, bass.ds(at, D)], ps_sum[b][:, 0:D], ALU.add).then_inc(sum_added, 1)

            v.memset(t.sums[:, :], 0.0).then_inc(cleared, 1)
            dve.wait_ge(cleared, 1)
            steps(dve, NW4, (4, add), (0, locate), (1, classify))

        @block.scalar
        def _(act):
            def classify(j, u):
                i, b = j + u, u % B
                act.wait_ge(local_ok, i + 1)
                wait(act, sum_made, i - B + 1)
                nc.scalar.activation(apart[u % 2][:, :], t.ids[:, :], ACT.Square, bias=local[b][:, STEP - 1:STEP], scale=-1.0).then_inc(apart_ok, 1)
                act.wait_ge(apart_ok, i + 1)
                nc.scalar.activation(member[b][:, STEP - 1, :], apart[u % 2][:, :], ACT.Relu, bias=1.0, scale=-1.0).then_inc(member_act_ok, 1)

            steps(act, NW4, (0, classify))

        @block.tensor
        def _(pe):
            def total(j, u):
                i, b = j + u, u % B
                pe.wait_ge(member_ok, i + 1)
                pe.wait_ge(member_act_ok, i + 1)
                wait(pe, sum_added, i - B + 1)
                for k in range(STEP):
                    last = nc.tensor.matmul(ps_sum[b][:, 0:D], member[b][:, k, :], msg[u][:, k, 0:D], start=(k == 0), stop=(k == STEP - 1))
                last.then_inc(sum_made, 1)

            steps(pe, NW4, (0, total))


QB = NBP // 4


def moments(nc, chain, stats, mean, var, scratch):
    v = nc.vector
    chain.then(v.tensor_tensor(mean, stats[:, :, 1], stats[:, :, 4], ALU.add))
    chain.then(v.tensor_scalar(mean, mean, 0.5, None, ALU.mult))
    chain.then(v.tensor_tensor(scratch, stats[:, :, 1], mean, ALU.subtract))
    chain.then(v.tensor_tensor(scratch, scratch, scratch, ALU.mult))
    chain.then(v.tensor_tensor(var, stats[:, :, 2], stats[:, :, 5], ALU.add))
    chain.then(v.scalar_tensor_tensor(var, var, 1.0 / D, scratch, ALU.mult, ALU.add))


def norms_squared(nc, chain, out, mean, var):
    v = nc.vector
    chain.then(v.tensor_tensor(out, mean, mean, ALU.mult))
    chain.then(v.tensor_tensor(out, out, var, ALU.add))
    chain.then(v.tensor_scalar(out, out, float(D), None, ALU.mult))


def square_roots(nc, act, squares, roots, asked, made, first, n):
    for k in range(first, first + n):
        act.wait_ge(asked, k + 1)
        nc.scalar.activation(roots, squares, ACT.Sqrt).then_inc(made, 1)


ACT_BLOCKS = 4


def first_layer_out(nc, t):
    with ExitStack() as ctx:
        def sb(name, shape, dt=F32):
            return ctx.enter_context(nc.sbuf_tensor(name, shape, dt))

        def ps(name):
            return [ctx.enter_context(nc.psum_tensor(f"{name}{u}", [P, 4 * P], F32)) for u in range(2)]

        def sem(name):
            return ctx.enter_context(nc.semaphore(name))

        B = QB
        aggT, mag, grown, soft, positive, act1 = ([sb(f"{x}{u}", [P, 4 * P]) for u in range(2)] for x in (
            "aggT", "mag_o", "grown_o", "soft_o", "positive_o", "act1_o"))
        stats = sb("stats", [P, NBP, 6])
        mean, var, scratch, roots, rstd, shift = (sb(f"{x}_x1", [P, NBP])[:, :] for x in ("mean", "var", "scratch", "roots", "rstd", "shift"))
        ps_aggT, ps_pre, ps_out = ps("ps_aggT"), ps("ps_pre_o"), ps("ps_out")
        (aggT_made, aggT_ok, pre_made, mag_ok, grown_ok, soft_ok, positive_ok, act1_ok, out_made, out_added, stats_ok, asked, made, rstd_ok,
         dve_normal, act_normal, x1_stored, dve_step) = (sem(x) for x in (
             "aggT_made", "aggT_ok", "pre_o_made", "mag_o_ok", "grown_o_ok", "soft_o_ok", "positive_ok", "act1_o_ok", "out_made", "out_added", "stats_ok",
             "root_asked", "root_made", "rstd_ok", "dve_normal", "act_normal", "x1_stored", "x1_step"))
        block = ctx.enter_context(nc.Block())

        @block.tensor
        def _(pe):
            for q in range(B + 3):
                if q < B:
                    wait(pe, aggT_ok, q - 1)
                    for k in range(4):
                        at = (4 * q + k) * MSG
                        last = nc.tensor.transpose(ps_aggT[q % 2][:, k * P:(k + 1) * P], t.sums[:, at:at + D], t.ident[:, :])
                    last.then_inc(aggT_made, 1)
                if 0 <= q - 1 < B:
                    r = q - 1
                    pe.wait_ge(aggT_ok, r + 1)
                    wait(pe, act1_ok, r - 1)
                    nc.tensor.matmul(ps_pre[r % 2][:, :], t.weights[:, 2, :], aggT[r % 2][:, :], start=True, stop=True).then_inc(pre_made, 1)
                if 0 <= q - 3 < B:
                    r = q - 3
                    pe.wait_ge(act1_ok, r + 1)
                    wait(pe, out_added, r - 1)
                    for k in range(4):
                        nc.tensor.matmul(ps_out[r % 2][:, k * P:(k + 1) * P], act1[r % 2][:, k * P:(k + 1) * P], t.weights[:, 3, :], start=True, stop=False)
                        last = nc.tensor.matmul(ps_out[r % 2][:, k * P:(k + 1) * P], t.ones[0:1, :], t.bo2[:, :], start=False, stop=True)
                    last.then_inc(out_made, 1)

        @block.scalar
        def _(act):
            s = nc.scalar
            act.preload_act_table_set(EXP_LN)
            for q in range(B + 1):
                if q < B:
                    act.wait_ge(aggT_made, q + 1)
                    wait(act, pre_made, q - 1)
                    s.copy(aggT[q % 2][:, :], ps_aggT[q % 2][:, :]).then_inc(aggT_ok, 1)
                if q >= 1:
                    r = q - 1
                    act.wait_ge(pre_made, r + 1)
                    act.wait_ge(positive_ok, r + 1)
                    s.activation(mag[r % 2][:, :], ps_pre[r % 2][:, :], ACT.Abs, bias=t.b_o1[:, 0:1]).then_inc(mag_ok, 1)
                    act.wait_ge(mag_ok, r + 1)
                    s.activation(grown[r % 2][:, :], mag[r % 2][:, :], ACT.Exp, scale=-1.0).then_inc(grown_ok, 1)
                    act.wait_ge(grown_ok, r + 1)
                    wait(act, act1_ok, r - 1)
                    s.activation(soft[r % 2][:, :], grown[r % 2][:, :], ACT.Ln, bias=1.0).then_inc(soft_ok, 1)
            square_roots(nc, act, var, roots, asked, made, 0, 1)
            act.wait_ge(rstd_ok, 1)
            for q in range(4):
                for b in range((q + 1) * QB - ACT_BLOCKS, (q + 1) * QB):
                    last = s.activation(t.x_nodes[:, b, :], t.x_nodes[:, b, :], ACT.Identity, bias=shift[:, b:b + 1], scale=rstd[:, b:b + 1])
                last.then_inc(act_normal, 1)

        @block.vector
        def _(dve):
            v = nc.vector
            chain = Chain(dve, dve_step)
            for q in range(B + 3):
                if q < B:
                    dve.wait_ge(pre_made, q + 1)
                    wait(dve, act1_ok, q - 1)
                    v.tensor_scalar(positive[q % 2][:, :], ps_pre[q % 2][:, :], t.b_o1[:, 0:1], 0.0, ALU.add, ALU.max).then_inc(positive_ok, 1)
                if 1 <= q <= B:
                    r = q - 1
                    dve.wait_ge(positive_ok, r + 1)
                    dve.wait_ge(soft_ok, r + 1)
                    wait(dve, out_made, r - 1)
                    v.tensor_tensor(act1[r % 2][:, :], positive[r % 2][:, :], soft[r % 2][:, :], ALU.add).then_inc(act1_ok, 1)
                if q >= 3:
                    r = q - 3
                    dve.wait_ge(out_made, r + 1)
                    x = t.x_nodes[:, 4 * r:4 * r + 4, :].rearrange("p b d -> p (b d)")
                    v.tensor_tensor(x, x, ps_out[r % 2][:, :], ALU.add).then_inc(out_added, 1)
                    dve.wait_ge(out_added, r + 1)
                    for k in range(4):
                        last = v.bn_stats(stats[:, 4 * r + k, :], t.x_nodes[:, 4 * r + k, :])
                    last.then_inc(stats_ok, 1)
            dve.wait_ge(stats_ok, B)
            moments(nc, chain, stats, mean, var, scratch)
            v.tensor_scalar(var, var, LN_EPS, None, ALU.add).then_inc(asked, 1)
            dve.wait_ge(made, 1)
            chain.then(v.reciprocal(rstd, roots))
            v.scalar_tensor_tensor(shift, mean, -1.0, rstd, ALU.mult, ALU.mult).then_inc(rstd_ok, 1)
            for q in range(4):
                for b in range(q * QB, (q + 1) * QB - ACT_BLOCKS):
                    last = v.tensor_scalar(t.x_nodes[:, b, :], t.x_nodes[:, b, :], mean[:, b:b + 1], rstd[:, b:b + 1], ALU.subtract, ALU.mult)
                last.then_inc(dve_normal, 1)

        @block.sync
        def _(sp):
            for q in range(4):
                sp.wait_ge(dve_normal, q + 1)
                sp.wait_ge(act_normal, q + 1)
                sp.dma_start(t.x1_dram[q * QB * P:(q + 1) * QB * P, :].rearrange("(b p) d -> p b d", p=P), t.x_nodes[:, q * QB:(q + 1) * QB, :]).then_inc(x1_stored, 16)
            sp.wait_ge(x1_stored, 64)


def attention(nc, t):
    with ExitStack() as ctx:
        def sb(name, shape, dt=F32):
            return ctx.enter_context(nc.sbuf_tensor(name, shape, dt))

        def ps(name):
            return [ctx.enter_context(nc.psum_tensor(f"{name}{u}", [P, 4 * P], F32)) for u in range(2)]

        def sem(name):
            return ctx.enter_context(nc.semaphore(name))

        W, K = STEP // 2, 2
        N = NW2 // W
        NONE = BIG / 2
        meta = [sb(f"meta_l1{u}", [P, STEP, 4]) for u in range(BODY)]
        source = [sb(f"source{u}", [P, STEP], I32) for u in range(BODY)]
        xg = [sb(f"xg{u}", [P, STEP, MSG]) for u in range(BODY)]
        local = [sb(f"local_l1{u}", [P, STEP]) for u in range(2)]
        other = [sb(f"other{u}", [P, STEP, P], BF16) for u in range(2)]
        top = [sb(f"top{u}", [P, W]) for u in range(BODY)]
        below = [sb(f"minus_top{u}", [P, W]) for u in range(BODY)]
        new, diff, shrink = ([sb(f"{x}{u}", [P, W]) for u in range(BODY)] for x in ("new_max", "diff", "shrink"))
        fresh = sb("fresh", [P, P * Q2])
        grown, share = [sb(f"ew{u}", [P, STEP * P]) for u in range(2)], [sb(f"ewT{u}", [P, STEP, P]) for u in range(2)]
        ps_w, ps_ewT, ps_sum = ps("ps_w"), ps("ps_ewT"), ps("ps_l1")
        xT = [sb(f"x1T{u}", [P, 4 * P]) for u in range(2)]
        ps_xT, ps_self = (ctx.enter_context(nc.psum_tensor(x, [P, 4 * P], F32)) for x in ("ps_x1T", "ps_self"))
        xT_made, xT_ok, self_made, self_ok = (sem(x) for x in ("x1T_made", "x1T_ok", "self_made", "self_ok"))

        def has_batch(j, u):
            return isinstance(j, int) and j + u < QB

        loaded, gathered = [sem(f"meta_l1_loaded{u}") for u in range(BODY)], [sem(f"gathered{u}") for u in range(BODY)]
        (source_ok, local_ok, other_ok, w_made, top_ok, below_ok, new_ok, diff_ok, ew_ok, ewT_made, ewT_ok, sum_made, sum_added,
         start_ok) = (sem(x) for x in ("source_ok", "local_l1_ok", "other_ok", "w_made", "top_ok", "minus_top_ok", "new_ok", "diff_ok", "ew_ok",
                                       "ewT_made", "ewT_ok", "l1_sum_made", "l1_sum_added", "start_ok"))
        block = ctx.enter_context(nc.Block())

        @block.sync
        def _(sp):
            def load(j, u):
                i = j + u
                wait(sp, w_made, i - BODY + 1)
                rows = load_rows(nc, sp, t.regs["dst"], 0, W * i, W, ET - G2)
                for w in range(W):
                    sp.dma_start(meta[u][:, K * w:K * w + K, :].rearrange("p k d -> p (k d)"),
                                 t.meta_by_dst[bass.ds(rows[w], G2), :].rearrange("(p k) d -> p (k d)", p=P)).then_inc(loaded[u], 16)

            steps(sp, N, (0, load))

        @block.gpsimd
        def _(pool):
            for u in range(BODY):
                nc.gpsimd.memset(xg[u][:, :, D:MSG], 1.0).then_inc(start_ok, 1)
            pool.wait_ge(start_ok, BODY)

            def gather(j, u):
                i = j + u
                pool.wait_ge(source_ok, i + 1)
                pool.sem_inc(t.ticks, 1)
                if not isinstance(j, int) or i >= BODY:
                    pool.wait_ge(sum_made, i - BODY + 1)
                    pool.sem_inc(t.ticks, 1)
                for k in range(STEP):
                    pool.indirect_dma_start(xg[u][:, k, 0:D], None, t.x1_dram, bass.IndirectOffsetOnAxis(ap=source[u][:, k:k + 1], axis=0),
                                            bounds_check=NBP * P - 1, oob_is_err=False).then_inc(gathered[u], 16)

            steps(pool, N, (0, gather))
            for u in range(BODY):
                pool.wait_ge(gathered[u], 16 * STEP * uses(N, u))

        @block.vector
        def _(dve):
            v = nc.vector
            chain = Chain(dve, sem("l1_start"))
            chain.then(v.memset(t.sums[:, :], 0.0))
            chain.then(v.memset(new[BODY - 1][:, :], NONE))
            chain.then(v.memset(fresh[:, 0:1], 1.0))
            chain.then(v.tensor_tensor(fresh[:, 1:], t.first["dst"][:, 1:], t.first["dst"][:, 0:P * Q2 - 1], ALU.not_equal))
            chain.then(v.tensor_scalar(fresh[:, :], fresh[:, :], 2 * NONE, -NONE, ALU.mult, ALU.add))

            def classify(j, u):
                i, b = j + u, u % 2
                dve.wait_ge(loaded[u], rounds(j, 0, W))
                wait(dve, gathered[u], rounds(j, 1, STEP))
                v.tensor_copy(source[u][:, :], meta[u][:, :, 1]).then_inc(source_ok, 1)
                v.tensor_tensor(local[b][:, :].rearrange("p (w k) -> p w k", w=W), meta[u][:, :, 2].rearrange("p (w k) -> p w k", w=W),
                                t.first["dst"][:, bass.ds(W * i, W)][:, :, None].to_broadcast([P, W, K]), ALU.subtract).then_inc(local_ok, 1)
                dve.wait_ge(local_ok, i + 1)
                wait(dve, w_made, i - 1)
                for k in range(STEP):
                    last = v.tensor_scalar(other[b][:, k, :], t.ids16[:, :], local[b][:, k:k + 1], None, ALU.not_equal)
                last.then_inc(other_ok, 1)

            def maxima(j, u):
                i, b = j + u, u % 2
                dve.wait_ge(w_made, i + 1)
                v.tensor_reduce(top[u][:, :], ps_w[b][:, :].rearrange("p (w e) -> p w e", w=W), AX.X, ALU.max).then_inc(top_ok, 1)
                dve.wait_ge(top_ok, i + 1)
                v.tensor_scalar(below[u][:, :], top[u][:, :], -1.0, NONE, ALU.mult, ALU.min).then_inc(below_ok, 1)
                dve.wait_ge(below_ok, i + 1)
                before = new[(u - 1) % BODY][:, W - 1:W]
                v.tensor_tensor_scan(new[u][:, :], fresh[:, bass.ds(W * i, W)], below[u][:, :], before, ALU.max, ALU.min).then_inc(new_ok, 1)
                dve.wait_ge(new_ok, i + 1)
                v.tensor_scalar(diff[u][:, 0:1], new[u][:, 0:1], before, 0.0, ALU.subtract, ALU.min)
                v.tensor_scalar(diff[u][:, 1:2], new[u][:, 1:2], new[u][:, 0:1], 0.0, ALU.subtract, ALU.min).then_inc(diff_ok, 1)

            def add(j, u):
                i, b = j + u, u % 2
                at = load_rows(nc, dve, t.regs["dst"], 1, W * i, W, (NBLK - 1) * MSG)
                dve.wait_ge(sum_made, i + 1)
                for w in range(W):
                    wait(dve, sum_added, i * W + w)
                    sums = t.sums[:, bass.ds(at[w], MSG)]
                    v.scalar_tensor_tensor(sums, sums, shrink[u][:, w:w + 1], ps_sum[b][:, w * 256:w * 256 + MSG], ALU.mult, ALU.add).then_inc(sum_added, 1)

            def self_part(j, u):
                if has_batch(j, u):
                    i = j + u
                    dve.wait_ge(self_made, i + 1)
                    v.tensor_tensor(t.comb[:, 4 * i:4 * i + 4, :], ps_self[:, :].rearrange("p (b d) -> p b d", d=D),
                                    t.b_comb[:, None, :].to_broadcast([P, 4, D]), ALU.add).then_inc(self_ok, 1)

            steps(dve, N, (2, maxima), (0, classify), (6, add), (3, self_part))

        @block.tensor
        def _(pe):
            def weights(j, u):
                i, b = j + u, u % 2
                pe.wait_ge(other_ok, i + 1)
                wait(pe, ew_ok, i - 1)
                for k in range(STEP):
                    to = ps_w[b][:, k * P:(k + 1) * P]
                    nc.tensor.matmul(to, meta[u][:, k, 0:1].to_broadcast([P, P]), t.ident[:, :], start=True, stop=False, skip_group_check=True)
                    last = nc.tensor.matmul(to, other[b][:, k, :], t.minus_big[:, :], start=False, stop=True, skip_group_check=True)
                last.then_inc(w_made, 1)

            def transposes(j, u):
                i, b = j + u, u % 2
                pe.wait_ge(ew_ok, i + 1)
                wait(pe, ewT_ok, i - 1)
                for k in range(STEP):
                    last = nc.tensor.transpose(ps_ewT[b][:, k * P:(k + 1) * P], grown[b][:, k * P:(k + 1) * P], t.ident[:, :])
                last.then_inc(ewT_made, 1)

            def total(j, u):
                i, b = j + u, u % 2
                pe.wait_ge(ewT_ok, i + 1)
                pe.wait_ge(gathered[u], rounds(j, 0, STEP))
                wait(pe, sum_added, W * (i - 1))
                for k in range(STEP):
                    at = k // K * 256
                    last = nc.tensor.matmul(ps_sum[b][:, at:at + MSG], share[b][:, k, :], xg[u][:, k, :], start=(k % K == 0), stop=(k % K == K - 1))
                last.then_inc(sum_made, 1)

            def node_transposes(j, u):
                if has_batch(j, u):
                    i = j + u
                    wait(pe, xT_ok, i)
                    for k in range(4):
                        last = nc.tensor.transpose(ps_xT[:, k * P:(k + 1) * P], t.x_nodes[:, 4 * i + k, :], t.ident[:, :])
                    last.then_inc(xT_made, 1)

            def self_products(j, u):
                if has_batch(j, u):
                    i = j + u
                    pe.wait_ge(xT_ok, i + 1)
                    wait(pe, self_ok, i)
                    for k in range(4):
                        cols = slice(k * P, (k + 1) * P)
                        last = nc.tensor.matmul(ps_self[:, cols], xT[i % 2][:, cols], t.weights[:, 4, :], start=True, stop=True)
                    last.then_inc(self_made, 1)

            pe.wait_ge(start_ok, BODY)
            steps(pe, N, (4, transposes), (1, weights), (5, total), (0, node_transposes), (2, self_products))

        @block.scalar
        def _(act):
            s = nc.scalar
            act.preload_act_table_set(EXP_LN)

            def exponentials(j, u):
                i, b = j + u, u % 2
                act.wait_ge(diff_ok, i + 1)
                wait(act, ewT_made, i - 1)
                for w in range(W):
                    cols = slice(w * K * P, (w + 1) * K * P)
                    s.activation(grown[b][:, cols], ps_w[b][:, cols], ACT.Exp, bias=new[u][:, w:w + 1])
                s.activation(shrink[u][:, :], diff[u][:, :], ACT.Exp).then_inc(ew_ok, 1)

            def evacuate(j, u):
                i, b = j + u, u % 2
                act.wait_ge(ewT_made, i + 1)
                wait(act, sum_made, i - 1)
                s.copy(share[b][:, :, :].rearrange("p k n -> p (k n)"), ps_ewT[b][:, :]).then_inc(ewT_ok, 1)

            def copy_nodes(j, u):
                if has_batch(j, u):
                    i = j + u
                    act.wait_ge(xT_made, i + 1)
                    wait(act, self_made, i - 1)
                    s.copy(xT[i % 2][:, :], ps_xT[:, :]).then_inc(xT_ok, 1)

            steps(act, N, (3, exponentials), (4, evacuate), (1, copy_nodes))


def second_layer_out(nc, t, out):
    with ExitStack() as ctx:
        def sb(name, shape, dt=F32):
            return ctx.enter_context(nc.sbuf_tensor(name, shape, dt))

        def ps(name, n=2):
            return [ctx.enter_context(nc.psum_tensor(f"{name}{u}", [P, 4 * P], F32)) for u in range(n)]

        def sem(name):
            return ctx.enter_context(nc.semaphore(name))

        B = QB
        comb, x_beta, stats = t.comb, sb("x_beta", [P, NBP, D]), sb("stats2", [P, NBP, 6])
        mean, var, scratch, squares, roots, factor, unit, gain, shift = (sb(f"{x}_out", [P, NBP])[:, :] for x in (
            "mean", "var", "scratch", "squares", "roots", "factor", "unit", "gain", "shift"))
        nT = [sb(f"nT{u}", [P, 4 * P]) for u in range(2)]
        ps_nT, ps_nb = ps("ps_nT"), ps("ps_nb")
        (T_made, T_ok, comb_made, comb_ok, stats_ok, asked, made, x_beta_ok, centred, y_ok, gain_ok, dve_normal, act_normal,
         out_stored, dve_step) = (sem(x) for x in (
             "T_made", "T_ok", "comb_made", "comb_ok", "stats2_ok", "root2_asked", "root2_made", "x_beta_ok", "centred", "y_ok", "gain_ok",
             "dve_normal2", "act_normal2", "out_stored", "out_step"))
        block = ctx.enter_context(nc.Block())

        @block.gpsimd
        def _(pool):
            for q in range(4):
                rows = slice(q * QB, (q + 1) * QB)
                nc.gpsimd.tensor_tensor(x_beta[:, rows, :], t.x_nodes[:, rows, :], t.gb[:, 1, :][:, None, :].to_broadcast([P, QB, D]), ALU.add).then_inc(x_beta_ok, 1)

        @block.vector
        def _(dve):
            v = nc.vector
            chain = Chain(dve, dve_step)
            sums = t.sums[:, :].rearrange("p (b d) -> p b d", d=MSG)
            for b in range(NBP):
                last = v.bn_stats(stats[:, b, :], sums[:, b, 0:D])
            last.then_inc(stats_ok, 1)
            dve.wait_ge(stats_ok, 1)
            moments(nc, chain, stats, mean, var, scratch)
            norms_squared(nc, chain, scratch, mean, var)
            v.tensor_scalar(squares, scratch, 1.0, None, ALU.mult).then_inc(asked, 1)
            chain.then(v.tensor_scalar(factor, sums[:, :, D], 0.5, EPS, ALU.max, ALU.mult))
            dve.wait_ge(made, 1)
            chain.then(v.tensor_tensor(factor, factor, roots, ALU.add))
            chain.then(v.reciprocal(factor, factor))
            for q in range(B + 1):
                if q < B:
                    dve.wait_ge(comb_made, q + 1)
                    for k in range(4):
                        b = 4 * q + k
                        last = v.scalar_tensor_tensor(comb[:, b, :], ps_nb[q % 2][:, k * P:(k + 1) * P], factor[:, b:b + 1], comb[:, b, :], ALU.mult, ALU.add)
                    last.then_inc(comb_ok, 1)
                if q >= 1:
                    dve.wait_ge(comb_ok, q)
                    for b in range(4 * (q - 1), 4 * q):
                        last = v.bn_stats(stats[:, b, :], comb[:, b, :])
                    last.then_inc(stats_ok, 1)
            dve.wait_ge(stats_ok, B + 1)
            moments(nc, chain, stats, mean, var, scratch)
            norms_squared(nc, chain, scratch, mean, var)
            v.tensor_scalar(squares, scratch, 1.0, None, ALU.mult).then_inc(asked, 1)
            dve.wait_ge(made, 2)
            chain.then(v.tensor_scalar(unit, roots, 2.0 * EPS, None, ALU.add))
            chain.then(v.reciprocal(unit, unit))
            chain.then(v.tensor_tensor(scratch, unit, unit, ALU.mult))
            chain.then(v.tensor_tensor(scratch, scratch, var, ALU.mult))
            v.tensor_scalar(squares, scratch, LN_EPS, None, ALU.add).then_inc(asked, 1)
            dve.wait_ge(made, 3)
            chain.then(v.reciprocal(gain, roots))
            chain.then(v.tensor_tensor(gain, gain, unit, ALU.mult))
            for q in range(4 + 1):
                if q < 4:
                    for b in range(q * QB, (q + 1) * QB):
                        last = v.scalar_tensor_tensor(comb[:, b, :], comb[:, b, :], mean[:, b:b + 1], t.gb[:, 0, :], ALU.subtract, ALU.mult)
                    last.then_inc(centred, 1)
                    dve.wait_ge(centred, q + 1)
                    dve.wait_ge(x_beta_ok, q + 1)
                    for b in range(q * QB, (q + 1) * QB):
                        last = v.scalar_tensor_tensor(comb[:, b, :], comb[:, b, :], gain[:, b:b + 1], x_beta[:, b, :], ALU.mult, ALU.add)
                    last.then_inc(y_ok, 1)
                if q >= 1:
                    dve.wait_ge(y_ok, q)
                    for b in range((q - 1) * QB, q * QB):
                        last = v.bn_stats(stats[:, b, :], comb[:, b, :])
                    last.then_inc(stats_ok, 1)
            dve.wait_ge(stats_ok, B + 5)
            moments(nc, chain, stats, mean, var, scratch)
            v.tensor_scalar(squares, var, LN_EPS, None, ALU.add).then_inc(asked, 1)
            dve.wait_ge(made, 4)
            chain.then(v.reciprocal(gain, roots))
            v.scalar_tensor_tensor(shift, mean, -1.0, gain, ALU.mult, ALU.mult).then_inc(gain_ok, 1)
            for q in range(4):
                for b in range(q * QB, (q + 1) * QB - ACT_BLOCKS):
                    last = v.tensor_scalar(comb[:, b, :], comb[:, b, :], mean[:, b:b + 1], gain[:, b:b + 1], ALU.subtract, ALU.mult)
                last.then_inc(dve_normal, 1)

        @block.tensor
        def _(pe):
            for q in range(B + 1):
                if q < B:
                    wait(pe, T_ok, q - 1)
                    for k in range(4):
                        at, cols = (4 * q + k) * MSG, slice(k * P, (k + 1) * P)
                        last = nc.tensor.transpose(ps_nT[q % 2][:, cols], t.sums[:, at:at + D], t.ident[:, :])
                    last.then_inc(T_made, 1)
                if q >= 1:
                    r = q - 1
                    pe.wait_ge(T_ok, r + 1)
                    wait(pe, comb_ok, r - 1)
                    for k in range(4):
                        cols = slice(k * P, (k + 1) * P)
                        last = nc.tensor.matmul(ps_nb[r % 2][:, cols], nT[r % 2][:, cols], t.weights[:, 5, :], start=True, stop=True)
                    last.then_inc(comb_made, 1)

        @block.scalar
        def _(act):
            s = nc.scalar
            for q in range(B):
                act.wait_ge(T_made, q + 1)
                wait(act, comb_made, q - 1)
                s.copy(nT[q % 2][:, :], ps_nT[q % 2][:, :]).then_inc(T_ok, 1)
                if q == 1:
                    square_roots(nc, act, squares, roots, asked, made, 0, 1)
            square_roots(nc, act, squares, roots, asked, made, 1, 3)
            act.wait_ge(gain_ok, 1)
            for q in range(4):
                for b in range((q + 1) * QB - ACT_BLOCKS, (q + 1) * QB):
                    last = s.activation(comb[:, b, :], comb[:, b, :], ACT.Identity, bias=shift[:, b:b + 1], scale=gain[:, b:b + 1])
                last.then_inc(act_normal, 1)

        @block.sync
        def _(sp):
            for q in range(4):
                sp.wait_ge(dve_normal, q + 1)
                sp.wait_ge(act_normal, q + 1)
                sp.dma_start(out[q * QB * P:(q + 1) * QB * P, :].rearrange("(b p) d -> p b d", p=P), comb[:, q * QB:(q + 1) * QB, :]).then_inc(out_stored, 16)
            sp.wait_ge(out_stored, 64)


def build(nc, a, out):
    with ExitStack() as ctx:
        def sb(name, shape, dt=F32):
            return ctx.enter_context(nc.sbuf_tensor(name, shape, dt))

        def dram(name, shape, dt=F32):
            return nc.dram_tensor(name, shape, dt, kind="Internal").ap()

        t = Program()
        t.ticks = ctx.enter_context(nc.semaphore("ticks"))
        t.ones, t.ident, t.before, t.ids = (sb(x, [P, P]) for x in ("ones", "ident", "before", "ids"))
        t.ident16, t.ids16, t.minus_big = (sb(x, [P, P], BF16) for x in ("ident16", "ids16", "minus_big"))
        t.ones_row, t.ones3 = sb("ones_row", [P, COLS], BF16), sb("ones3", [3, P], BF16)
        t.bucket_ids = sb("bucket_ids", [P, NBU + 1])
        t.pool_junk, t.dve_junk = sb("pool_junk", [P, 1]), sb("dve_junk", [P, 2])
        t.w1, t.weights, t.rows = sb("w1", [P, STEP, D]), sb("weights", [P, 6, D]), sb("rows", [1, 2, D])
        t.gb, t.b_o1, t.bo2, t.b_comb = sb("gb", [P, 4, D]), sb("b_o1", [P, 1]), sb("bo2", [1, D]), sb("b_comb", [P, D])
        t.b2_rows = sb("b2_rows", [3, STEP, D], BF16)
        t.x_nodes = sb("x_nodes", [P, NBP, D])
        t.window_ids = {"src": sb("window_ids_src", [P, Q4]), "dst": sb("window_ids_dst", [P, Q2])}
        t.window_ints = {"src": sb("window_ints_src", [P, 2, Q4], I32), "dst": sb("window_ints_dst", [P, 3, Q2], I32)}
        t.window_nodes = {"src": sb("window_nodes_src", [P, Q4]), "dst": sb("window_nodes_dst", [P, Q2])}
        t.regs = {"src": sb("regs_src", [1, 2, P * Q4], I32), "dst": sb("regs_dst", [1, 3, P * Q2], I32)}
        t.first = {"src": sb("first_src", [P, P * Q4]), "dst": sb("first_dst", [P, P * Q2])}
        t.ints_dram = {"src": dram("ints_src", [2, P * Q4], I32), "dst": dram("ints_dst", [3, P * Q2], I32)}
        t.nodes_dram = {"src": dram("nodes_src", [P * Q4]), "dst": dram("nodes_dst", [P * Q2])}
        t.b2_dram = dram("b2_parts", [3, D], BF16)
        t.flag = sb("flag", [P, 1], I32)
        t.filters_by_dst, t.meta_by_dst = dram("filters_by_dst", [ET, RBF]), dram("meta_by_dst", [ET, 4])
        t.messages = dram("messages", [ET, MSG])
        t.x1_dram = dram("x1_nodes", [NBP * P, D])
        t.f_ones = sb("f_ones", [P, BODY, STEP, P // STEP])

        with ExitStack() as c1:
            t.h3 = c1.enter_context(nc.sbuf_tensor("h3", [P, NBP, 3, D], BF16))
            with ExitStack() as c2:
                t.meta = c2.enter_context(nc.sbuf_tensor("meta", [P, COLS, 4], F32))
                t.hi_dst = c2.enter_context(nc.sbuf_tensor("hi_dst", [P, COLS], BF16))
                t.base_dst = c2.enter_context(nc.sbuf_tensor("base_dst", [P, NBU + 1], F32))
                prologue(nc, t, a)
                order_by_dst(nc, t, a)
            messages(nc, t)
        t.sums = sb("sums", [P, NBP * MSG])
        t.comb = sb("comb", [P, NBP, D])
        sum_messages(nc, t)
        first_layer_out(nc, t)
        attention(nc, t)
        second_layer_out(nc, t, out)


def kernel(x, src, dst, edge_attr_20, edge_weight, L0_gnn_W_in2f, L0_gnn_W_f1, L0_gnn_b_f1, L0_gnn_W_f2, L0_gnn_b_f2,
           L0_gnn_W_o1, L0_gnn_b_o1, L0_gnn_W_o2, L0_gnn_b_o2, L1_gnn_W_self, L1_gnn_b_self, L1_gnn_W_nb, L1_gnn_b_nb,
           L1_gnn_gamma, L1_gnn_beta):
    import numpy as np
    import concourse.bacc as bacc
    from concourse.bass_utils import run_bass_kernel_spmd

    def padded(v, rows, fill=0):
        v = np.asarray(v)
        wide = np.full((rows,) + v.shape[1:], fill, v.dtype)
        wide[:v.shape[0]] = v
        return wide

    arrays = {
        "x": padded(x, NBP * P), "src": padded(src, ET, PAD_NODE), "dst": padded(dst, ET + 1, PAD_NODE),
        "edge_attr": padded(edge_attr_20, ET), "edge_weight": padded(edge_weight, ET),
        "W_in2f": L0_gnn_W_in2f, "W_f1": L0_gnn_W_f1, "b_f1": L0_gnn_b_f1, "W_f2": L0_gnn_W_f2, "b_f2": L0_gnn_b_f2,
        "W_o1": L0_gnn_W_o1, "b_o1": L0_gnn_b_o1, "W_o2": L0_gnn_W_o2, "b_o2": L0_gnn_b_o2,
        "W_self": L1_gnn_W_self, "b_self": L1_gnn_b_self, "W_nb": L1_gnn_W_nb, "b_nb": L1_gnn_b_nb,
        "gamma": L1_gnn_gamma, "beta": L1_gnn_beta,
    }
    arrays = {f"in_{k}": np.ascontiguousarray(v) for k, v in arrays.items()}
    nc = bacc.Bacc("TRN2", target_bir_lowering=False, num_devices=1)
    a = {k[3:]: nc.dram_tensor(k, v.shape, mybir.dt.from_np(v.dtype), kind="ExternalInput").ap() for k, v in arrays.items()}
    out = nc.dram_tensor("out_x", (NBP * P, D), F32, kind="ExternalOutput").ap()
    build(nc, a, out)
    results = run_bass_kernel_spmd(nc, [arrays], core_ids=[0])
    return results.results[0]["out_x"][:NODES]
```
